# Optimizing a Trainium2 kernel written in Bass

```python
import numpy as np
import jax
import jax.numpy as jnp

def _softmax(x, axis=-1):
    return jax.nn.softmax(x, axis=axis)

def _gelu(x):
    return jax.nn.gelu(x, approximate=True)

def _silu(x):
    return jax.nn.silu(x)

def _sigmoid(x):
    return jax.nn.sigmoid(x)

def _layernorm(x, axis=-1, eps=1e-05):
    m = jnp.mean(x, axis=axis, keepdims=True)
    v = jnp.var(x, axis=axis, keepdims=True)
    return (x - m) / jnp.sqrt(v + eps)

def _scatter_add(tgt, idx, src, axis=0):
    return tgt.at[idx].add(src)

def _segment_sum(src, seg, n):
    return jax.ops.segment_sum(src, seg, n)
kernel_name = 'mk_gnn_resnorm_d4_gnn_r16_d47cf1'

def setup_inputs(seed: int=0):
    np.random.seed(seed)
    _w = jnp.asarray

    def _rec_inputs():
        import jax
        import jax.numpy as jnp
        _gk = jax.random.key(seed)
        x = -0.000202 + 1 * jax.random.normal(jax.random.fold_in(_gk, 1), (6250, 64), jnp.float32)
        _s = jax.random.randint(jax.random.fold_in(_gk, 2), (50000,), 0, 6250, jnp.int32)
        _d = jax.random.randint(jax.random.fold_in(_gk, 3), (50000,), 0, 6250, jnp.int32)
        _loop = jnp.arange(6250, dtype=jnp.int32)
        src = jnp.concatenate([_s, _d, _loop])
        dst = jnp.concatenate([_d, _s, _loop])
        _o = jnp.argsort(dst, stable=True)
        src = src[_o]
        dst = dst[_o]
        edge_type_16 = jax.random.randint(jax.random.fold_in(_gk, 13), (106250,), 0, 16, jnp.int32)
        edge_type_8 = jax.random.randint(jax.random.fold_in(_gk, 14), (106250,), 0, 8, jnp.int32)
        return (x, src, dst, edge_type_16, edge_type_8)
    x, src, dst, edge_type_16, edge_type_8 = _rec_inputs()

    def _L0_gnn_setup():
        import jax, jax.numpy as jnp
        import numpy as np
        N_NODES = 6250
        N_EDGES = 62500
        D_IN = 64
        D_OUT = 64
        N_RELS = 16
        key = jax.random.key(seed)
        k1, k2, k3, k4, k5 = jax.random.split(key, 5)
        feat = jax.random.normal(k1, (N_NODES, D_IN), dtype=jnp.float32)
        weight = jax.random.normal(k2, (N_RELS, D_IN, D_OUT), dtype=jnp.float32) * 0.05
        src = jax.random.randint(k3, (N_EDGES,), 0, N_NODES)
        dst = jax.random.randint(k4, (N_EDGES,), 0, N_NODES)
        etypes = jax.random.randint(k5, (N_EDGES,), 0, N_RELS)
        return {'feat': feat, 'weight': weight, 'src': src, 'dst': dst, 'etypes': etypes}
    _L0_gnn_all = _L0_gnn_setup()
    _L0_gnn_in = {k: v for k, v in _L0_gnn_all.items() if k in ('weight',)}
    del _L0_gnn_all

    def _L1_gnn_setup():
        import jax, jax.numpy as jnp
        import numpy as np
        N_NODES = 3125
        N_EDGES = 50000
        FEAT_DIM = 64
        key = jax.random.key(seed)
        k1, k2, k3 = jax.random.split(key, 3)
        x = jax.random.normal(k1, (N_NODES, FEAT_DIM), dtype=jnp.float32)
        beta = jnp.ones((1,), dtype=jnp.float32)
        row_index = jnp.sort(jax.random.randint(k2, (N_EDGES,), 0, N_NODES, dtype=jnp.int32))
        col_index = jax.random.randint(k3, (N_EDGES,), 0, N_NODES, dtype=jnp.int32)
        return {'x': x, 'beta': beta, 'row_index': row_index, 'col_index': col_index}
    _L1_gnn_all = _L1_gnn_setup()
    _L1_gnn_in = {k: v for k, v in _L1_gnn_all.items() if k in ('beta',)}
    del _L1_gnn_all

    def _L2_gnn_setup():
        import jax, jax.numpy as jnp
        import numpy as np
        N = 3125
        E = 50000
        H = 6
        F_IN = 64
        F_OUT = 64
        NEG_SLOPE = 0.2
        key = jax.random.key(seed)
        k1, k2, k3, k4, k5 = jax.random.split(key, 5)
        x = jax.random.normal(k1, (N, F_IN), jnp.float32)
        edge_idx = jax.random.randint(k2, (2, E), 0, N, dtype=jnp.int64)
        scale = 1.0 / np.sqrt(F_IN)
        W_l = jax.random.normal(k3, (F_IN, H * F_OUT), jnp.float32) * scale
        W_r = jax.random.normal(k4, (F_IN, H * F_OUT), jnp.float32) * scale
        att = jax.random.normal(k5, (H, F_OUT), jnp.float32) * scale
        bias = jnp.zeros((F_OUT,), jnp.float32)
        return {'x': x, 'edge_idx': edge_idx, 'W_l': W_l, 'W_r': W_r, 'att': att, 'bias': bias}
    _L2_gnn_all = _L2_gnn_setup()
    _L2_gnn_in = {k: v for k, v in _L2_gnn_all.items() if k in ('W_l', 'W_r', 'att', 'bias')}
    del _L2_gnn_all

    def _L3_gnn_setup():
        import jax, jax.numpy as jnp
        import numpy as np
        N_NODES = 6250
        N_EDGES = 100000
        IN_FEAT = 64
        OUT_FEAT = 64
        NUM_RELS = 8
        NUM_BASES = 2
        key = jax.random.key(seed)
        k_feat, k_w, k_c, k_lw, k_src, k_dst, k_et = jax.random.split(key, 7)
        feat = jax.random.normal(k_feat, (N_NODES, IN_FEAT), dtype=jnp.float32)
        bound = 1.0 / np.sqrt(IN_FEAT)
        W = jax.random.uniform(k_w, (NUM_BASES, IN_FEAT, OUT_FEAT), dtype=jnp.float32, minval=-bound, maxval=bound)
        coeff = jax.random.normal(k_c, (NUM_RELS, NUM_BASES), dtype=jnp.float32)
        h_bias = jnp.zeros((OUT_FEAT,), dtype=jnp.float32)
        loop_weight = jax.random.normal(k_lw, (IN_FEAT, OUT_FEAT), dtype=jnp.float32) * (1.0 / np.sqrt(IN_FEAT))
        src = jax.random.randint(k_src, (N_EDGES,), 0, N_NODES, dtype=jnp.int32)
        dst = jax.random.randint(k_dst, (N_EDGES,), 0, N_NODES, dtype=jnp.int32)
        etypes = jax.random.randint(k_et, (N_EDGES,), 0, NUM_RELS, dtype=jnp.int32)
        return {'feat': feat, 'W': W, 'coeff': coeff, 'h_bias': h_bias, 'loop_weight': loop_weight, 'src': src, 'dst': dst, 'etypes': etypes}
    _L3_gnn_all = _L3_gnn_setup()
    _L3_gnn_in = {k: v for k, v in _L3_gnn_all.items() if k in ('W', 'coeff', 'h_bias', 'loop_weight')}
    del _L3_gnn_all
    return {'x': x, 'src': src, 'dst': dst, 'edge_type_16': edge_type_16, 'edge_type_8': edge_type_8, 'L0_gnn_weight': _L0_gnn_in['weight'], 'L1_gnn_beta': _L1_gnn_in['beta'], 'L2_gnn_W_l': _L2_gnn_in['W_l'], 'L2_gnn_W_r': _L2_gnn_in['W_r'], 'L2_gnn_att': _L2_gnn_in['att'], 'L2_gnn_bias': _L2_gnn_in['bias'], 'L3_gnn_W': _L3_gnn_in['W'], 'L3_gnn_coeff': _L3_gnn_in['coeff'], 'L3_gnn_h_bias': _L3_gnn_in['h_bias'], 'L3_gnn_loop_weight': _L3_gnn_in['loop_weight']}

def reference(x, src, dst, edge_type_16, edge_type_8, L0_gnn_weight, L1_gnn_beta, L2_gnn_W_l, L2_gnn_W_r, L2_gnn_att, L2_gnn_bias, L3_gnn_W, L3_gnn_coeff, L3_gnn_h_bias, L3_gnn_loop_weight):
    import jax
    import jax.numpy as jnp

    def _L0_gnn_ref(feat, weight, src, dst, etypes):
        import jax, jax.numpy as jnp
        import numpy as np
        N_NODES = 6250
        N_EDGES = 62500
        D_IN = 64
        D_OUT = 64
        N_RELS = 16
        h = feat[src]
        n_rels = weight.shape[0]
        e, d_out = (h.shape[0], weight.shape[2])

        def step(m, rw):
            r, w_r = rw
            mask = jnp.where(etypes == r, 1.0, 0.0).astype(h.dtype)
            m = m + mask[:, None] * (h @ w_r)
            return (m, None)
        m0 = jnp.zeros((e, d_out), dtype=h.dtype)
        m, _ = jax.lax.scan(step, m0, (jnp.arange(n_rels), weight))
        out = jax.ops.segment_sum(m, dst, num_segments=feat.shape[0])
        return out

    def _L1_gnn_ref(x, beta, row_index, col_index):
        import jax, jax.numpy as jnp
        import numpy as np
        N_NODES = 3125
        N_EDGES = 50000
        FEAT_DIM = 64
        'AGNN layer: SDDMM edge attention (beta * cosine similarity) over the\n            sparse graph, per-row softmax, then sparse neighbor aggregation.\n            Equivalent math to mygraph.SDDMM + mygraph.agnn_udf (select_id == 5).\n            x: [N, D]; row_index/col_index: [E] edge endpoints (row = destination).\n            '
        N = x.shape[0]
        eps = 1e-08
        xn = x * jax.lax.rsqrt(jnp.sum(x * x, axis=-1, keepdims=True) + eps)
        att = beta[0] * jnp.sum(xn[row_index] * xn[col_index], axis=-1)
        m = jax.ops.segment_max(att, row_index, num_segments=N)
        m = jnp.where(jnp.isfinite(m), m, 0.0)
        e = jnp.exp(att - m[row_index])
        denom = jax.ops.segment_sum(e, row_index, num_segments=N)
        alpha = e / jnp.maximum(denom[row_index], 1e-16)
        out = jax.ops.segment_sum(alpha[:, None] * x[col_index], row_index, num_segments=N)
        return out

    def _L2_gnn_ref(x, edge_idx, W_l, W_r, att, bias):
        import jax, jax.numpy as jnp
        import numpy as np
        N = 3125
        E = 50000
        H = 6
        F_IN = 64
        F_OUT = 64
        NEG_SLOPE = 0.2
        n = x.shape[0]
        loops = jnp.arange(n, dtype=edge_idx.dtype)
        src = jnp.concatenate([edge_idx[0], loops])
        dst = jnp.concatenate([edge_idx[1], loops])
        gl = (x @ W_l).reshape(n, H, F_OUT)
        gr = (x @ W_r).reshape(n, H, F_OUT)
        s = jax.nn.leaky_relu(gl[src] + gr[dst], NEG_SLOPE)
        e = jnp.einsum('ehf,hf->eh', s, att)
        m = jax.ops.segment_max(e, dst, num_segments=n)
        p = jnp.exp(e - m[dst])
        denom = jax.ops.segment_sum(p, dst, num_segments=n)
        alpha = p / (denom[dst] + 1e-16)
        msg = alpha[:, :, None] * gl[src]
        out = jax.ops.segment_sum(msg, dst, num_segments=n)
        out = out.mean(axis=1) + bias
        return jax.nn.selu(out)

    def _L3_gnn_ref(feat, W, coeff, h_bias, loop_weight, src, dst, etypes):
        import jax, jax.numpy as jnp
        import numpy as np
        N_NODES = 6250
        N_EDGES = 100000
        IN_FEAT = 64
        OUT_FEAT = 64
        NUM_RELS = 8
        NUM_BASES = 2
        n_nodes, in_feat = feat.shape
        num_bases = coeff.shape[1]
        out_feat = W.shape[-1]
        msg = coeff[etypes][:, :, None] * feat[src][:, None, :]
        agg = jax.ops.segment_sum(msg, dst, num_segments=n_nodes)
        h = agg.reshape(n_nodes, num_bases * in_feat) @ W.reshape(num_bases * in_feat, out_feat)
        h = h + h_bias
        h = h + feat @ loop_weight
        return h
    edge_index = jnp.stack([src, dst])
    x = _layernorm(x + _L0_gnn_ref(x, L0_gnn_weight, src, dst, edge_type_16), axis=-1)
    x = _layernorm(x + _L1_gnn_ref(x, L1_gnn_beta, src, dst), axis=-1)
    x = _layernorm(x + _L2_gnn_ref(x, edge_index, L2_gnn_W_l, L2_gnn_W_r, L2_gnn_att, L2_gnn_bias), axis=-1)
    x = _layernorm(x + _L3_gnn_ref(x, L3_gnn_W, L3_gnn_coeff, L3_gnn_h_bias, L3_gnn_loop_weight, src, dst, edge_type_8), axis=-1)
    return x

_drawn_inputs = setup_inputs


def setup_inputs(seed=0):
    import zlib

    import numpy as np

    out = dict(_drawn_inputs(seed))
    spreads = {'L2_gnn_bias': (0.0, 0.1), 'L3_gnn_h_bias': (0.0, 0.295)}
    factors = {}
    for name, (base, spread) in spreads.items():
        noise = np.random.default_rng([zlib.crc32(name.encode()), seed]).standard_normal(out[name].shape)
        drawn = base * np.exp(spread * noise) if base else spread * noise
        out[name] = jnp.asarray(drawn.astype(out[name].dtype))
    for name, factor in factors.items():
        out[name] = (out[name] * factor).astype(out[name].dtype)
    return out
```

```python
from contextlib import ExitStack

import concourse.bass as bass
from concourse import mybir

P = 128
D = 64
N = 6250
NL = 49
NN = P * NL
E = 106250
NC = 832
EP = P * NC
CH = 16
NCH = NC // CH
R0 = 16
R3 = 8
H = 6
HW = H * 65
RW = HW + H
BIG = 1e30
SKIP = 200000.0
GN = 7
NG = NL // GN


class Queues:

    ENGINES = ("sync", "gpsimd", "scalar", "vector", "tensor")

    def __init__(self, sems):
        self.items = {e: [] for e in self.ENGINES}
        self.seen = {e: {} for e in self.ENGINES}
        self.value = {}
        self.sems = sems
        self.saved = {}

    def wait(self, eng, *tokens):
        for t in tokens:
            if t is None:
                continue
            name, v = t
            if v > self.seen[eng].get(name, 0):
                self.seen[eng][name] = v
                self.items[eng].append(("wait", self.sems[name], v))

    def emit(self, eng, fn, waits, sem, inc):
        self.wait(eng, *waits)
        self.value[sem] = self.value.get(sem, 0) + inc
        self.items[eng].append(("do", fn, self.sems[sem], inc))
        return (sem, self.value[sem])

    def begin_if(self, eng, flag):
        self.items[eng].append(("if", flag))
        self.saved[eng] = dict(self.seen[eng])

    def end_if(self, eng):
        self.items[eng].append(("end",))
        self.seen[eng] = self.saved.pop(eng)

    def play(self, eng, e):
        stack = []
        for it in self.items[eng]:
            if it[0] == "wait":
                e.wait_ge(it[1], it[2])
            elif it[0] == "do":
                it[1](e).then_inc(it[2], it[3])
            elif it[0] == "if":
                reg = e.value_load(it[1])
                c = e.If(reg != 0)
                c.__enter__()
                stack.append(c)
            else:
                stack.pop().__exit__(None, None, None)


def build(nc, x, src, dst, et16, et8, w0, beta, wl, wr, att, bias2, w3, coeff, hbias, loopw, out):
    F32 = mybir.dt.float32
    I32 = mybir.dt.int32
    BF16 = mybir.dt.bfloat16
    ALU = mybir.AluOpType
    ACT = mybir.ActivationFunctionType
    AX = mybir.AxisListType.X

    def dram(name, shape, dt=F32):
        return nc.dram_tensor(name, shape, dt).ap()

    y0 = dram("y0", (NN * R0, D))
    y3 = dram("y3", (NN * R3, D))
    s0 = dram("s0", (EP + 1, D))
    s1 = dram("s1", (EP + 1, 66))
    s2 = dram("s2", (EP + 1, RW))
    s3 = dram("s3", (EP + 1, D))
    xd = dram("xd", (EP, D))
    xt1 = dram("xt1", (NN, 65))
    xt2 = dram("xt2", (NN, D))
    cntd = dram("cntd", (NN,))
    srt = dram("srt", (EP, 4), I32)

    with ExitStack() as ctx:
        names = ["dve", "act", "pe", "pool", "ld", "ldn", "ldw", "z", "cnt", "row", "dbg",
                 "fdve", "fpe", "fpool", "fsc", "fld", "xdi", "ysb0", "ysb1", "ysb2", "ysb3", "xt", "sc", "zr", "out"]
        names += [f"g{i}" for i in range(5)] + [f"x{i}" for i in range(4)] + [f"s{i}" for i in range(4)]
        names += [f"n{i}" for i in range(2)]
        sems = {n: ctx.enter_context(nc.semaphore("k_" + n)) for n in names}
        Q = Queues(sems)

        def sb(name, shape, dt=F32):
            return ctx.enter_context(nc.sbuf_tensor(name, shape, dt))

        def V(fn, *w):
            return Q.emit("vector", lambda e: fn(), w, "dve", 1)

        def VL(fn, *w):
            return V(fn, ("dve", Q.value.get("dve", 0)), *w)

        def A(fn, *w):
            return Q.emit("scalar", lambda e: fn(), w, "act", 1)

        def T(fn, *w):
            return Q.emit("tensor", lambda e: fn(), w, "pe", 1)

        def G(fn, *w):
            return Q.emit("gpsimd", lambda e: fn(), w, "pool", 1)

        def ld(o, i, *w, sem, eng="sync"):
            return Q.emit(eng, lambda e: e.dma_start(o, i, allow_slow_non_contiguous=True), w, sem, 16)

        def gather(o, table, idx, *w, sem):
            return Q.emit("gpsimd", lambda e: e.indirect_dma_start(
                out=o, out_offset=None, in_=table,
                in_offset=bass.IndirectOffsetOnAxis(ap=idx, axis=0)), w, sem, 16)

        def scatter(table, i, idx, bound, *w, sem):
            return Q.emit("gpsimd", lambda e: e.indirect_dma_start(
                out=table, out_offset=bass.IndirectOffsetOnAxis(ap=idx, axis=0), in_=i,
                in_offset=None, bounds_check=bound, oob_is_err=False), w, sem, 16)

        v, s, g, t = nc.vector, nc.scalar, nc.gpsimd, nc.tensor

        Dd = sb("Dd", [P, NC], I32)
        Df = sb("Df", [P, NC])
        Si = sb("Si", [P, NC], I32)
        I0 = sb("I0", [P, NC], I32)
        I3 = sb("I3", [P, NC], I32)
        gf = sb("gf", [P, NC])
        Bn = sb("Bn", [P, NC + 1])
        X = sb("X", [P, NL, D])
        R = sb("R", [P, NL, D])
        ident = sb("ident", [P, P])
        ones = sb("ones", [P, P])
        lower = sb("lower", [P, P])
        sm = sb("sm", [P, 32])
        dn = sb("dn", [P, 1], I32)
        flag = sb("flag", [P, 2], I32)
        Cq = sb("Cq", [P, P])
        CTn = sb("CTn", [P, P])
        En = sb("En", [P, P])
        cntn = sb("cntn", [P, NL])
        incl = sb("incl", [P, NL])
        nfl = sb("nfl", [P, NL])
        endi = sb("endi", [P, NL], I32)
        stai = sb("stai", [P, NL], I32)
        fixg = sb("fixg", [P, 1], I32)
        fixs = sb("fixs", [P, 1], I32)
        W0 = sb("W0", [D, R0 * D])
        W3 = sb("W3", [D, R3 * D + D])
        WLR = sb("WLR", [P, H * D])
        WS = sb("WS", [D, H * D])
        W2 = sb("W2", [P, 3, D])
        A8 = sb("A8", [P, 3, H])
        Vm = sb("Vm", [P, H])
        Vs = sb("Vs", [D, H])
        att3 = sb("att3", [P, 3])
        co = sb("co", [D, R3 * 2])
        wb = sb("wb", [D, 2, D])
        b2 = sb("b2", [P, D])
        b3 = sb("b3", [P, D])
        bet = sb("bet", [P, 1])
        es = sb("es", [P, NL, H])
        ARENA = 34000
        AR = sb("AR", [P, ARENA])

        def arena(off, *shape):
            n = 1
            for k in shape:
                n *= k
            assert off + n <= ARENA, (off, shape)
            a = AR[:, off:off + n]
            if len(shape) == 2:
                a = a.rearrange("p (a b) -> p a b", a=shape[0])
            if len(shape) == 3:
                a = a.rearrange("p (a b c) -> p a b c", a=shape[0], b=shape[1])
            return a

        PS = [ctx.enter_context(nc.psum_tensor(f"ps{i}", [P, 512], F32)) for i in range(8)]

        def bc(a, shape):
            return a.broadcast_to(shape)

        AF = AR[:, 0:NC * 2].bitcast(I32)
        e16t, e8t = AF[:, 0:NC], AF[:, NC:2 * NC]
        ld(Dd[:], dst[0:EP].rearrange("(p j) -> p j", j=NC), sem="ld")
        ld(dn[:], dst[NC:NC + EP].rearrange("(p j) -> p j", j=NC)[:, 0:1], sem="ld")
        ld(Si[:], src.rearrange("(p j) -> p j", j=NC), sem="ld")
        ld(e16t, et16.rearrange("(p j) -> p j", j=NC), sem="ld")
        l_edges = ld(e8t, et8.rearrange("(p j) -> p j", j=NC), sem="ld")
        l_x = ld(X[:], x.rearrange("(p l) d -> p l d", l=NL), sem="ldn")
        ld(W0[:].rearrange("p (r o) -> p r o", r=R0), w0.rearrange("r i o -> i r o"), sem="ldw")
        l_w0 = None
        ld(WLR[0:D, :], wl, sem="ldw")
        ld(WLR[D:P, :], wr, sem="ldw")
        ld(WS[:], wr, sem="ldw")
        wlv = wl.rearrange("f (c h o) -> f c h o", c=3, h=2)
        ld(W2[0:D, :, :], wlv[:, :, 0, :], sem="ldw")
        ld(W2[D:P, :, :], wlv[:, :, 1, :], sem="ldw")
        attf = att.rearrange("h o -> (h o)")
        ld(att3[:], attf.rearrange("(c q) -> q c", c=3), sem="ldw")
        ld(co[:], coeff.rearrange("r b -> (r b)").partition_broadcast(D), sem="ldw")
        ld(wb[:], w3.rearrange("b i o -> i b o"), sem="ldw")
        ld(W3[:, R3 * D:], loopw, sem="ldw")
        ld(b2[:], bias2.partition_broadcast(P), sem="ldw")
        ld(b3[:], hbias.partition_broadcast(P), sem="ldw")
        ld(bet[:], beta.partition_broadcast(P), sem="ldw")
        attb = arena(2 * NC, H, D)
        l_w = ld(attb.rearrange("p h o -> p (h o)"), attf.partition_broadcast(P), sem="ldw")

        k_ones = V(lambda: v.memset(ones[:], 1.0))
        c1 = G(lambda: g.affine_select(out=ident[:], in_=ones[:], compare_op=ALU.is_equal, fill=0.0, base=0,
                                       pattern=[[-1, P]], channel_multiplier=1), k_ones)
        c2 = G(lambda: g.affine_select(out=lower[:], in_=ones[:], compare_op=ALU.is_gt, fill=0.0, base=0,
                                       pattern=[[1, P]], channel_multiplier=-1))
        hi98 = arena(2100, 98).bitcast(I32)
        lo64 = arena(2200, 64).bitcast(I32)
        pidx = sm[:, 30:31].bitcast(I32)
        G(lambda: g.iota(hi98, [[1, 98]], base=0, channel_multiplier=0))
        G(lambda: g.iota(pidx, [[0, 1]], base=0, channel_multiplier=1))
        c3 = G(lambda: g.iota(lo64, [[1, 64]], base=0, channel_multiplier=0))

        zt = arena(27000, CH * D)
        zrow = sb("zrow", [1, RW])
        k_z = V(lambda: v.memset(zt, 0.0))
        V(lambda: v.memset(zrow[:], 0.0))
        VL(lambda: v.memset(zrow[0:1, HW:], -BIG))
        zr1 = sb("zr1", [1, 66])
        V(lambda: v.memset(zr1[:], 0.0))
        k_zr = VL(lambda: v.memset(zr1[0:1, 65:66], -BIG))
        ld(s0[EP:EP + 1, :], zr1[0:1, 0:D], k_zr, sem="zr")
        ld(s3[EP:EP + 1, :], zr1[0:1, 0:D], k_zr, sem="zr")
        ld(s1[EP:EP + 1, :], zr1[:], k_zr, sem="zr")
        l_zr = ld(s2[EP:EP + 1, :], zrow[:], k_zr, sem="zr")

        dnf, bad, badc = sm[:, 0:1], sm[:, 1:2], sm[:, 2:3]
        scr = arena(5000, NC)
        V(lambda: v.tensor_copy(Df[:], Dd[:]), l_edges)
        VL(lambda: v.tensor_copy(dnf, dn[:]))
        VL(lambda: v.tensor_tensor(scr[:, 0:NC - 1], Df[:, 0:NC - 1], Df[:, 1:NC], ALU.is_gt))
        VL(lambda: v.tensor_tensor(scr[:, NC - 1:NC], Df[:, NC - 1:NC], dnf, ALU.is_gt))
        a = VL(lambda: v.tensor_reduce(bad, scr, AX, ALU.max))
        b = T(lambda: t.matmul(PS[0][:, 0:1], ones[:], bad, start=True, stop=True), a)
        k_flag = V(lambda: v.tensor_copy(flag[:, 0:1], PS[0][:, 0:1]), b)

        def resort():
            def FV(fn, *w):
                return Q.emit("vector", lambda e: fn(), (("fdve", Q.value.get("fdve", 0)),) + w, "fdve", 1)

            def FT(fn, *w):
                return Q.emit("tensor", lambda e: fn(), w, "fpe", 1)

            NB = (NN + 511) // 512
            IO = arena(5000, NN).bitcast(I32)
            CN = arena(5000 + NN, NN)
            JJ = arena(5000 + 2 * NN, NN)
            RR = arena(5000 + 3 * NN, NC, 4).bitcast(I32)
            rank = arena(5000 + 3 * NN + 4 * NC, NC)
            posi = gf[:].bitcast(I32)
            tmp = Bn[:, 0:NC]
            io = Q.emit("gpsimd", lambda e: g.iota(IO, [[1, NN]], base=0, channel_multiplier=0), (k_flag,), "fpool", 1)
            FV(lambda: v.memset(CN, 0.0), io)
            FV(lambda: v.memset(tmp, 0.0))
            FV(lambda: v.memset(rank, 0.0))
            for j in range(NC):
                FV(lambda j=j: v.scalar_tensor_tensor(out=JJ, in0=IO, scalar=Df[:, j:j + 1], in1=CN, op0=ALU.is_equal,
                                                      op1=ALU.mult, accum_out=rank[:, j:j + 1]))
                FV(lambda j=j: v.scalar_tensor_tensor(out=CN, in0=IO, scalar=Df[:, j:j + 1], in1=CN, op0=ALU.is_equal,
                                                      op1=ALU.add))
            done = (("fdve", Q.value["fdve"]))
            for bk in range(NB):
                lo, hi = bk * 512, min(NN, bk * 512 + 512)
                FT(lambda lo=lo, hi=hi: t.matmul(PS[0][:, 0:hi - lo], ones[:], CN[:, lo:hi], start=True, stop=True), done)
                p = FT(lambda lo=lo, hi=hi: t.matmul(PS[1][:, 0:hi - lo], lower[:], CN[:, lo:hi], start=True, stop=True), c2)
                FV(lambda lo=lo, hi=hi: v.tensor_copy(JJ[:, lo:hi], PS[0][:, 0:hi - lo]), p)
                done = FV(lambda lo=lo, hi=hi: v.tensor_copy(CN[:, lo:hi], PS[1][:, 0:hi - lo]))
            FV(lambda: v.tensor_tensor_scan(JJ, JJ, JJ, 0.0, ALU.add, ALU.bypass))
            FV(lambda: v.tensor_tensor(CN[:, 1:NN], CN[:, 1:NN], JJ[:, 0:NN - 1], ALU.add))
            for j in range(NC):
                FV(lambda j=j: v.scalar_tensor_tensor(out=JJ, in0=IO, scalar=Df[:, j:j + 1], in1=CN, op0=ALU.is_equal,
                                                      op1=ALU.mult, accum_out=tmp[:, j:j + 1]))
            FV(lambda: v.tensor_tensor(rank, rank, tmp, ALU.add))
            FV(lambda: v.tensor_copy(posi, rank))
            for k, c in enumerate((Si[:], Dd[:], e16t, e8t)):
                fin = FV(lambda k=k, c=c: v.tensor_copy(RR[:, :, k], c))
            for j in range(NC):
                sc = scatter(srt, RR[:, j, :], posi[:, j:j + 1], EP - 1, fin, sem="fsc")
            sv = srt.rearrange("(p j) k -> p j k", j=NC)
            ld(RR, sv, sc, sem="fld")
            l = ld(dn[0:P - 1, :], sv[1:P, 0, 1:2], sem="fld")
            FV(lambda: v.tensor_copy(Si[:], RR[:, :, 0]), l)
            FV(lambda: v.tensor_copy(Dd[:], RR[:, :, 1]))
            FV(lambda: v.tensor_copy(e16t, RR[:, :, 2]))
            FV(lambda: v.tensor_copy(e8t, RR[:, :, 3]))
            FV(lambda: v.tensor_copy(Df[:], Dd[:]))
            FV(lambda: v.tensor_copy(dnf, dn[:]))

        for e_ in ("vector", "tensor", "gpsimd", "sync"):
            Q.wait(e_, k_flag)
            Q.begin_if(e_, flag[0:1, 0:1])
        resort()
        for e_ in ("vector", "tensor", "gpsimd", "sync"):
            Q.end_if(e_)

        dhi = arena(3000, NC).bitcast(I32)
        dlo = arena(4000, NC).bitcast(I32)
        V(lambda: v.scalar_tensor_tensor(out=I0[:], in0=Si[:], scalar=16.0, in1=e16t, op0=ALU.mult, op1=ALU.add))
        k_i0 = V(lambda: v.scalar_tensor_tensor(out=I3[:], in0=Si[:], scalar=8.0, in1=e8t, op0=ALU.mult, op1=ALU.add))
        V(lambda: v.memset(gf[:, 0:1], 0.0))
        V(lambda: v.memset(Bn[:, NC:NC + 1], -BIG))
        V(lambda: v.tensor_tensor(gf[:, 1:NC], Df[:, 1:NC], Df[:, 0:NC - 1], ALU.is_equal))
        k_bn = VL(lambda: v.tensor_scalar(Bn[:, 0:NC], gf[:], -1.0, BIG, op0=ALU.add, op1=ALU.mult))
        V(lambda: v.tensor_scalar(dhi, Dd[:], 6, None, op0=ALU.logical_shift_right))
        k_dl = V(lambda: v.tensor_scalar(dlo, Dd[:], 63, None, op0=ALU.bitwise_and), c3)

        pf, cont, key, df_, eqn, inv, pos, eqc = (sm[:, k:k + 1] for k in range(3, 11))
        scr2 = arena(5000, NC)
        V(lambda: v.tensor_copy(pf, pidx))
        V(lambda: v.tensor_copy(df_, Df[:, 0:1]))
        V(lambda: v.tensor_tensor(eqn, Df[:, NC - 1:NC], dnf, ALU.is_equal))
        VL(lambda: v.tensor_scalar(inv, pf, 126.5, None, op0=ALU.is_lt))
        VL(lambda: v.tensor_tensor(cont, eqn, inv, ALU.mult))
        VL(lambda: v.tensor_scalar(key, Df[:, NC - 1:NC], 1.0, None, op0=ALU.add))
        VL(lambda: v.tensor_scalar(key, key, cont, -1.0, op0=ALU.mult, op1=ALU.add))
        dg = arena(6000, 2, P)
        VL(lambda: v.tensor_scalar(dg[:, 0, :], ident[:], key, None, op0=ALU.mult), c1)
        a = VL(lambda: v.tensor_scalar(dg[:, 1, :], ident[:], df_, None, op0=ALU.mult))
        b = T(lambda: t.matmul(PS[1][:, 0:2 * P], ones[:], dg.rearrange("p a b -> p (a b)"), start=True, stop=True), a)
        V(lambda: v.tensor_scalar(Cq[:], PS[1][:, P:2 * P], key, None, op0=ALU.is_equal), b)
        V(lambda: v.tensor_scalar(CTn[:], PS[1][:, 0:P], df_, None, op0=ALU.is_equal))
        V(lambda: v.tensor_scalar(En[:], PS[1][:, 0:P], key, None, op0=ALU.is_equal))
        VL(lambda: v.tensor_reduce(inv, CTn[:], AX, ALU.max))
        VL(lambda: v.tensor_scalar(CTn[:], CTn[:], -1.0, BIG, op0=ALU.add, op1=ALU.mult))
        VL(lambda: v.tensor_scalar(En[:], En[:], -1.0, BIG, op0=ALU.add, op1=ALU.mult))
        VL(lambda: v.tensor_scalar(scr2, Df[:], df_, None, op0=ALU.is_equal))
        VL(lambda: v.reduce_sum(eqc, scr2, AX))
        VL(lambda: v.tensor_scalar(pos, pf, float(NC), -1.0, op0=ALU.mult, op1=ALU.add))
        VL(lambda: v.tensor_tensor(pos, pos, eqc, ALU.add))
        VL(lambda: v.tensor_copy(fixg[:], pos))
        VL(lambda: v.tensor_scalar(eqc, eqc, float(NC) - 0.5, None, op0=ALU.is_gt))
        VL(lambda: v.tensor_tensor(eqc, eqc, cont, ALU.mult))
        VL(lambda: v.tensor_tensor(inv, inv, eqc, ALU.is_gt))
        VL(lambda: v.tensor_scalar(inv, inv, -SKIP, SKIP, op0=ALU.mult, op1=ALU.add))
        VL(lambda: v.tensor_tensor(pos, pos, inv, ALU.add))
        k_fix = VL(lambda: v.tensor_copy(fixs[:], pos))

        tA = arena(7000, H, D)
        V(lambda: v.tensor_tensor(tA, WLR[:].rearrange("p (h o) -> p h o", h=H), attb, ALU.mult), l_w)
        VL(lambda: v.reduce_sum(Vm[:], tA, AX))
        VL(lambda: v.tensor_scalar(Vm[:], Vm[:], 0.2, None, op0=ALU.mult))
        V(lambda: v.tensor_tensor(WS[:], WS[:], WLR[0:D, :], ALU.add))
        VL(lambda: v.tensor_tensor(tA[0:D], WS[:].rearrange("p (h o) -> p h o", h=H), attb[0:D], ALU.mult))
        VL(lambda: v.reduce_sum(Vs[:], tA[0:D], AX))
        VL(lambda: v.tensor_scalar(Vs[:], Vs[:], 0.2, None, op0=ALU.mult))
        VL(lambda: v.memset(A8[:], 0.0))
        for c in range(3):
            VL(lambda c=c: v.tensor_scalar(A8[0:D, c, 2 * c:2 * c + 1], att3[0:D, c:c + 1], 0.8, None, op0=ALU.mult))
            VL(lambda c=c: v.tensor_scalar(A8[D:P, c, 2 * c + 1:2 * c + 2], att3[D:P, c:c + 1], 0.8, None, op0=ALU.mult))
        for r in range(R3):
            V(lambda r=r: v.tensor_scalar(W3[:, r * D:(r + 1) * D], wb[:, 0, :], co[:, 2 * r:2 * r + 1], None, op0=ALU.mult))
            k_w = VL(lambda r=r: v.scalar_tensor_tensor(out=W3[:, r * D:(r + 1) * D], in0=wb[:, 1, :],
                                                        scalar=co[:, 2 * r + 1:2 * r + 2],
                                                        in1=W3[:, r * D:(r + 1) * D], op0=ALU.mult, op1=ALU.add))

        xtt = arena(8000, 2, P)
        ysb = arena(9000, 4, R0 * D)
        ydone = {}
        pe_x, ev_x = {}, {}

        def table_col(l, k, W, nrel, ytab, ready, extra=None):
            w = nrel * D
            st = pe_x.get(("x", k - 2))
            a = T(lambda: t.transpose(PS[2 + k % 2][0:D, 0:P], X[:, l, :], ident[:]), *ready, ev_x.get(("x", k - 2)))
            pe_x[("x", k)] = a
            ev = V(lambda: v.tensor_copy(xtt[0:D, k % 2, :], PS[2 + k % 2][0:D, 0:P]), a, pe_x.get(("y", k - 2)))
            ev_x[("x", k)] = ev
            toks = []
            nb = (w + 511) // 512
            for i in range(nb):
                bnk = 4 + (2 * k + i) % 4
                cols = min(512, w - 512 * i)
                p = T(lambda i=i, bnk=bnk, cols=cols: t.matmul(PS[bnk][:, 0:cols], xtt[0:D, k % 2, :],
                                                              W[:, 512 * i:512 * i + cols], start=True, stop=True),
                      ev, ev_x.get(("b", bnk)))
                dstt = ysb[:, k % 4, 512 * i:512 * i + cols]
                if extra is not None and i == nb - 1 and nb > 1:
                    extra(l, PS[bnk], p)
                    ev_x[("b", bnk)] = ("dve", Q.value["dve"])
                    continue
                if i == 0:
                    q = A(lambda dstt=dstt, bnk=bnk, cols=cols: s.copy(dstt, PS[bnk][:, 0:cols]), p, ydone.get(k - 4))
                else:
                    q = V(lambda dstt=dstt, bnk=bnk, cols=cols: v.tensor_copy(dstt, PS[bnk][:, 0:cols]), p, ydone.get(k - 4))
                ev_x[("b", bnk)] = q
                toks.append(q)
            pe_x[("y", k)] = p
            wt = nrel * D
            yv = ytab.rearrange("(p l r) d -> p l (r d)", l=NL, r=nrel)
            ydone[k] = ld(yv[:, l, :], ysb[:, k % 4, 0:wt], *toks, sem=f"ysb{k % 4}")

        for l in range(NL):
            table_col(l, l, W0, R0, y0, (l_x, l_w, c1))
        for c in range(NCH):
            l_z = ld(xd.rearrange("(p j) d -> p j d", j=NC)[:, c * CH:(c + 1) * CH, :].rearrange("p j d -> p (j d)"),
                     zt, k_z, sem="z")
        t_y0 = [ydone[k] for k in range(NL - 4, NL)]

        def chunk_view(st, c, w):
            return st[0:EP, :].rearrange("(p j) d -> p j d", j=NC)[:, c * CH:(c + 1) * CH, :].rearrange("p j d -> p (j d)")

        def linear_chunks(tab, idx, st, ready, side=None):
            NBUF = 4
            GB = arena(13200, NBUF, CH * D)
            stored, first = {}, {}
            last = None
            for c in range(NCH):
                b_ = c % NBUF
                buf = GB[:, b_, :].rearrange("p (j d) -> p j d", j=CH)
                prev = GB[:, (c - 1) % NBUF, :].rearrange("p (j d) -> p j d", j=CH)
                for j in range(CH):
                    tk = gather(buf[:, j, :], tab, idx[:, c * CH + j:c * CH + j + 1], *ready, stored.get(c - NBUF),
                                first.get(c - NBUF + 1), sem=f"g{b_}")
                if side is not None:
                    side(c)
                for j in range(CH):
                    if c == 0 and j == 0:
                        continue
                    pr = buf[:, j - 1, :] if j else prev[:, CH - 1, :]
                    last = VL(lambda c=c, j=j, pr=pr, buf=buf: v.scalar_tensor_tensor(
                        out=buf[:, j, :], in0=pr, scalar=gf[:, c * CH + j:c * CH + j + 1], in1=buf[:, j, :],
                        op0=ALU.mult, op1=ALU.add), tk, k_bn)
                    if j == 0:
                        first[c] = last
                stored[c] = ld(chunk_view(st, c, D), GB[:, b_, :], last, sem=f"s{b_}")
            return GB[:, (NCH - 1) % NBUF, (CH - 1) * D:CH * D], last, [stored[c] for c in range(NCH - NBUF, NCH)]

        ohh = arena(17400, CH * 98 // 2).bitcast(BF16).rearrange("p (j a) -> p j a", j=CH)
        ohl = arena(18300, CH * 64 // 2).bitcast(BF16).rearrange("p (j a) -> p j a", j=CH)
        hist_pe = {}

        def hist(c):
            V(lambda: v.tensor_tensor(ohh, bc(dhi[:, c * CH:(c + 1) * CH].unsqueeze(2), [P, CH, 98]),
                                      bc(hi98.unsqueeze(1), [P, CH, 98]), ALU.is_equal), hist_pe.get(c - 1), k_dl)
            a = V(lambda: v.tensor_tensor(ohl, bc(dlo[:, c * CH:(c + 1) * CH].unsqueeze(2), [P, CH, 64]),
                                          bc(lo64.unsqueeze(1), [P, CH, 64]), ALU.is_equal))
            for j in range(CH):
                hist_pe[c] = T(lambda j=j: t.matmul(PS[0][0:98, 0:64], ohh[:, j, :], ohl[:, j, :],
                                                    start=(c == 0 and j == 0), stop=(c == NCH - 1 and j == CH - 1)), a)

        T0, k_t, st_t = linear_chunks(y0, I0, s0, [*t_y0, k_i0], hist)

        hsb = arena(19000, 64)
        a = V(lambda: v.tensor_copy(hsb[0:98, :], PS[0][0:98, 0:64]), hist_pe[NCH - 1])
        b = ld(cntd.rearrange("(a b) -> a b", b=64), hsb[0:98, :], a, sem="cnt")
        b = ld(cntn[:], cntd.rearrange("(p l) -> p l", l=NL), b, sem="cnt")
        V(lambda: v.tensor_tensor_scan(incl[:], cntn[:], cntn[:], 0.0, ALU.add, ALU.bypass), b)
        a = VL(lambda: v.tensor_copy(sm[:, 11:12], incl[:, NL - 1:NL]))
        b = T(lambda: t.matmul(PS[1][:, 0:1], lower[:], sm[:, 11:12], start=True, stop=True), a, c2)
        VL(lambda: v.tensor_copy(sm[:, 12:13], PS[1][:, 0:1]), b)
        VL(lambda: v.tensor_scalar(incl[:], incl[:], sm[:, 12:13], None, op0=ALU.add))
        VL(lambda: v.tensor_scalar(nfl[:], cntn[:], 0.5, None, op0=ALU.is_gt))
        VL(lambda: v.tensor_tensor(cntn[:], incl[:], cntn[:], ALU.subtract))
        VL(lambda: v.tensor_scalar(incl[:], incl[:], -1.0 - EP, None, op0=ALU.add))
        VL(lambda: v.tensor_tensor(incl[:], incl[:], nfl[:], ALU.mult))
        VL(lambda: v.tensor_scalar(endi[:], incl[:], float(EP), None, op0=ALU.add))
        VL(lambda: v.tensor_scalar(nfl[:], nfl[:], -SKIP, SKIP, op0=ALU.mult, op1=ALU.add))
        k_node = VL(lambda: v.tensor_tensor(stai[:], cntn[:], nfl[:], ALU.add))

        def mend_linear(st, Tl, k_last, stored):
            fr = arena(19100, D)
            gt = gather(fr, st[:], fixg[:], *stored, k_fix, l_zr, sem="row")
            a = T(lambda: t.matmul(PS[2][:, 0:D], Cq[:], Tl, start=True, stop=True), k_last)
            b = VL(lambda: v.tensor_tensor(fr, fr, PS[2][:, 0:D], ALU.add), a, gt)
            return scatter(st[:], fr, fixs[:], EP - 1, b, sem="row")

        def norm(y, o, sq, mu, rs, *w):
            n = y.shape[1]
            sh = [P, n, D]
            V(lambda: v.reduce_sum(mu, y, AX), *w)
            VL(lambda: v.tensor_scalar(mu, mu, 1.0 / D, None, op0=ALU.mult))
            VL(lambda: v.tensor_tensor(y, y, bc(mu.unsqueeze(2), sh), ALU.subtract))
            VL(lambda: v.tensor_tensor(sq, y, y, ALU.mult))
            VL(lambda: v.reduce_sum(rs, sq, AX))
            a = VL(lambda: v.tensor_scalar(rs, rs, 1.0 / D, 1e-5, op0=ALU.mult, op1=ALU.add))
            a = A(lambda: s.sqrt(rs, rs), a)
            VL(lambda: v.reciprocal(rs, rs), a)
            return VL(lambda: v.tensor_tensor(o, y, bc(rs.unsqueeze(2), sh), ALU.mult))

        sq = arena(19300, GN, D)
        mu = arena(19800, GN)
        rs = arena(19820, GN)

        m0 = mend_linear(s0, T0, k_t, st_t)
        xts = arena(20000, NL, 65)
        zz = R
        NG0 = arena(23400, 2, GN * D)
        used = {}
        sc_done = None
        for q in range(NG):
            nb = NG0[:, q % 2, :].rearrange("p (l d) -> p l d", l=GN)
            sl = slice(q * GN, (q + 1) * GN)
            for i in range(GN):
                tk = gather(nb[:, i, :], s0[:], endi[:, q * GN + i:q * GN + i + 1], m0, k_node, used.get(q - 2), sem=f"n{q % 2}")
            VL(lambda nb=nb, sl=sl: v.tensor_tensor(nb, nb, X[:, sl, :], ALU.add), tk)
            k = norm(nb, X[:, sl, :], sq, mu, rs, ("dve", Q.value["dve"]))
            used[q] = k
            VL(lambda sl=sl: v.tensor_tensor(sq, X[:, sl, :], X[:, sl, :], ALU.mult))
            VL(lambda: v.reduce_sum(rs, sq, AX))
            a = VL(lambda: v.tensor_scalar(rs, rs, 1e-8, None, op0=ALU.add))
            a = A(lambda: s.sqrt(rs, rs), a)
            VL(lambda: v.reciprocal(rs, rs), a)
            VL(lambda sl=sl: v.tensor_copy(xts[:, sl, 0:D], X[:, sl, :]))
            a = VL(lambda sl=sl: v.tensor_copy(xts[:, sl, D], rs))
            VL(lambda: v.tensor_scalar(mu, rs, bet[:], None, op0=ALU.mult))
            b = VL(lambda sl=sl: v.tensor_tensor(zz[:, sl, :], X[:, sl, :], bc(mu.unsqueeze(2), [P, GN, D]), ALU.mult))
            xw = ld(xt1.rearrange("(p l) d -> p l d", l=NL)[:, sl, :].rearrange("p l d -> p (l d)"),
                    xts[:, sl, :].rearrange("p l d -> p (l d)"), a, sem="xt")
            for l in range(q * GN, (q + 1) * GN):
                sc_done = scatter(xd, zz[:, l, :], stai[:, l:l + 1], EP - 1, b, l_z, sem="sc")
        k_end = ("dve", Q.value["dve"])

        def fence(*toks):
            for e_ in Queues.ENGINES:
                Q.wait(e_, *toks)

        def attention(heads, tab, tw, st, ready_g, ready_x, logits_factory, xinit):
            pass

        fence(k_end)

        def idle():
            return [(n_, Q.value[n_]) for n_ in ("dve", "act", "pe") if n_ in Q.value]

        def merged(*lists):
            total = max(len(x_) for x_ in lists)
            at = [0] * len(lists)
            for i in range(total):
                for k_, x_ in enumerate(lists):
                    while at[k_] * total < (i + 1) * len(x_):
                        x_[at[k_]]()
                        at[k_] += 1

        G1 = arena(0, 4, CH * 65)
        XB1 = arena(4200, 3, CH * D)
        XF1 = arena(7300, 2, CH * D)
        TM1 = arena(9400, CH, D)
        S1 = arena(10500, 3, CH * 66)
        e1, m1 = arena(13700, CH), arena(13720, CH)
        mf1 = arena(13740, CH)
        pf1 = arena(13760, 2, CH + 1)
        xi1 = arena(13800, 65)
        xdv = xd.rearrange("(p j) d -> p j d", j=NC)

        gi = gather(xi1, xt1, Dd[:, 0:1], xw, k_end, sem="xdi")
        k_g, k_xb, freeG, freeXB, freeXF, stored, pxd = {}, {}, {}, {}, {}, {}, {}
        k_fill = {}

        def g1(c):
            for j in range(CH):
                k_g[c] = gather(G1[:, c % 4, j * 65:(j + 1) * 65], xt1, Si[:, c * CH + j:c * CH + j + 1],
                                xw, freeG.get(c - 4), sem=f"g{c % 4}")

        def xb(c, XB, free, ready):
            k_xb[c] = ld(XB[:, c % XBN, :], xdv[:, c * CH:(c + 1) * CH, :].rearrange("p j d -> p (j d)"),
                         ready, free.get(c - XBN), sem=f"x{c % XBN}")

        XBN = 3

        def fills1(c):
            ops = []
            XBv = XB1[:, c % 3, :].rearrange("p (j d) -> p j d", j=CH)
            XFv = XF1[:, c % 2, :].rearrange("p (j d) -> p j d", j=CH)
            XFp = XF1[:, (c - 1) % 2, :].rearrange("p (j d) -> p j d", j=CH)
            mine = [None]

            def one(j):
                if c == 0 and j == 0:
                    def f():
                        V(lambda: v.tensor_scalar(mu[:, 0:1], xi1[:, 64:65], bet[:], None, op0=ALU.mult), gi)
                        mine[0] = VL(lambda: v.tensor_scalar(XFv[:, 0, :], xi1[:, 0:D], mu[:, 0:1], None, op0=ALU.mult))
                    return f
                pr = XFv[:, j - 1, :] if j else XFp[:, CH - 1, :]

                def f():
                    mine[0] = V(lambda: v.scalar_tensor_tensor(
                        out=XFv[:, j, :], in0=pr, scalar=gf[:, c * CH + j:c * CH + j + 1], in1=XBv[:, j, :],
                        op0=ALU.mult, op1=ALU.add), k_xb[c], mine[0] or k_fill.get(c - 1), freeXF.get(c - 2))
                    k_fill[c] = mine[0]
                    freeXB[c] = mine[0]
                return f
            return [one(j) for j in range(CH)]

        def soft1(c):
            Gv = G1[:, c % 4, :].rearrange("p (j d) -> p j d", j=CH)
            XFv = XF1[:, c % 2, :].rearrange("p (j d) -> p j d", j=CH)
            Sv = S1[:, c % 3, :].rearrange("p (j d) -> p j d", j=CH)
            Sp = S1[:, (c - 1) % 3, :].rearrange("p (j d) -> p j d", j=CH)
            pe_ = pf1[:, c % 2, :]
            mine = [None]

            def L(fn, *w):
                def f():
                    mine[0] = V(fn, mine[0] or k_fill[c], *w)
                return f

            def at_dot():
                freeXF[c] = V(lambda: v.tensor_tensor(TM1, Gv[:, :, 0:D], XFv, ALU.mult), k_fill[c], k_g[c])
                mine[0] = freeXF[c]
            ops = [at_dot,
                   L(lambda: v.reduce_sum(e1, TM1, AX)),
                   L(lambda: v.tensor_tensor(e1, e1, Gv[:, :, D], ALU.mult)),
                   L(lambda: v.tensor_tensor_scan(mf1, Bn[:, c * CH:(c + 1) * CH], e1,
                                                  Sp[:, CH - 1, 65:66] if c else -BIG, ALU.add, ALU.max)),
                   L(lambda: v.tensor_tensor_scan(m1[:, ::-1], Bn[:, c * CH + 1:(c + 1) * CH + 1][:, ::-1], mf1[:, ::-1],
                                                  -BIG, ALU.add, ALU.max)),
                   L(lambda: v.tensor_tensor(pe_[:, 0:CH], e1, m1, ALU.subtract))]
            if c:
                ops.append(L(lambda: v.scalar_tensor_tensor(out=pe_[:, CH:CH + 1], in0=Sp[:, CH - 1, 65:66],
                                                            scalar=Bn[:, c * CH:c * CH + 1], in1=m1[:, 0:1],
                                                            op0=ALU.add, op1=ALU.subtract)))
            n_ = CH + 1 if c else CH

            def ex():
                pxd[c] = A(lambda: s.activation(pe_[:, 0:n_], pe_[:, 0:n_], ACT.Exp), mine[0])
            ops.append(ex)
            ops.append(L(lambda: v.tensor_copy(Sv[:, :, 65], m1), stored.get(c - 3)))
            return ops

        def px1(c):
            Gv = G1[:, c % 4, :].rearrange("p (j d) -> p j d", j=CH)
            Sv = S1[:, c % 3, :].rearrange("p (j d) -> p j d", j=CH)
            pe_ = pf1[:, c % 2, 0:CH]
            V(lambda: v.tensor_tensor(Sv[:, :, 0:D], Gv[:, :, 0:D], bc(pe_.unsqueeze(2), [P, CH, D]), ALU.mult),
              pxd[c], stored.get(c - 3))
            freeG[c] = V(lambda: v.tensor_copy(Sv[:, :, D], pe_))

        k_step = {}

        def steps1(c):
            Sv = S1[:, c % 3, :].rearrange("p (j d) -> p j d", j=CH)
            Sp = S1[:, (c - 1) % 3, :].rearrange("p (j d) -> p j d", j=CH)
            mine = [None]

            def one(j):
                if c == 0 and j == 0:
                    return lambda: None
                pr = Sv[:, j - 1, 0:65] if j else Sp[:, CH - 1, 0:65]
                sc_ = gf[:, c * CH + j:c * CH + j + 1] if j else pf1[:, c % 2, CH:CH + 1]

                def f():
                    mine[0] = V(lambda: v.scalar_tensor_tensor(out=Sv[:, j, 0:65], in0=pr, scalar=sc_, in1=Sv[:, j, 0:65],
                                                               op0=ALU.mult, op1=ALU.add),
                                mine[0] or freeG[c], k_step.get(c - 1))
                    k_step[c] = mine[0]
                return f
            return [one(j) for j in range(CH)]

        for c in range(3):
            xb(c, XB1, freeXB, sc_done)
        g1(0)
        g1(1)
        merged(fills1(0))
        merged(soft1(0))
        px1(0)
        merged(fills1(1))
        for c in range(NCH):
            if c + 2 < NCH:
                g1(c + 2)
            if c + 3 < NCH:
                xb(c + 3, XB1, freeXB, sc_done)
            B_ = []
            if c + 1 < NCH:
                B_ += soft1(c + 1)
            if c + 2 < NCH:
                B_ += fills1(c + 2)
            merged(steps1(c), B_)
            stored[c] = ld(chunk_view(s1, c, 66), S1[:, c % 3, :], k_step[c], sem=f"s{c % 3}")
            if c + 1 < NCH:
                px1(c + 1)
        st_t = [stored[c] for c in range(NCH - 3, NCH)]
        T1 = S1[:, (NCH - 1) % 3, :].rearrange("p (j d) -> p j d", j=CH)[:, CH - 1, :]

        def mend_soft(st, Tl, heads, k_last, stored_, base):
            aw = heads * 65
            o = base

            def take(*shape):
                nonlocal o
                n = 1
                for k_ in shape:
                    n *= k_
                a_ = arena(o, *shape)
                o += n
                return a_
            fr = take(aw + heads)
            dgm, mk = take(heads, P), take(heads, P)
            Ts, mseg, mc = take(aw), take(heads), take(heads)
            Mx, w1, w2 = take(heads), take(heads), take(heads)
            gt = gather(fr, st[:], fixg[:], *stored_, k_fix, l_zr, sem="row")
            ml = Tl[:, aw:aw + heads]
            a = None
            for h in range(heads):
                a = V(lambda h=h: v.tensor_scalar(dgm[:, h, :], ident[:], ml[:, h:h + 1], None, op0=ALU.mult), k_last)
            nb = (heads + 2) // 3
            for i in range(nb):
                k_ = min(3, heads - 3 * i)
                b = T(lambda i=i, k_=k_: t.matmul(PS[i][:, 0:k_ * P], ones[:],
                                                  dgm[:, 3 * i:3 * i + k_, :].rearrange("p a b -> p (a b)"),
                                                  start=True, stop=True), a)
            for msk, res in ((En, mseg), (CTn, mc)):
                for i in range(nb):
                    k_ = min(3, heads - 3 * i)
                    V(lambda i=i, k_=k_, msk=msk: v.tensor_tensor(
                        mk[:, 3 * i:3 * i + k_, :], PS[i][:, 0:k_ * P].rearrange("p (a b) -> p a b", b=P),
                        bc(msk[:].unsqueeze(1), [P, k_, P]), ALU.add), b, ("dve", Q.value["dve"]))
                VL(lambda res=res: v.tensor_reduce(res, mk, AX, ALU.max))
            a = VL(lambda: v.tensor_tensor(mseg, ml, mseg, ALU.subtract))
            a = A(lambda: s.activation(mseg, mseg, ACT.Exp), a)
            Tv = Tl[:, 0:aw].rearrange("p (h d) -> p h d", h=heads)
            a = V(lambda: v.tensor_tensor(Ts.rearrange("p (h d) -> p h d", h=heads), Tv,
                                          bc(mseg.unsqueeze(2), [P, heads, 65]), ALU.mult), a)
            b = T(lambda: t.matmul(PS[2][:, 0:aw], Cq[:], Ts, start=True, stop=True), a)
            mr = fr[:, aw:aw + heads]
            V(lambda: v.tensor_tensor(Mx, mr, mc, ALU.max), gt, a)
            VL(lambda: v.tensor_tensor(w1, mr, Mx, ALU.subtract))
            a = V(lambda: v.tensor_tensor(w2, mc, Mx, ALU.subtract))
            A(lambda: s.activation(w1, w1, ACT.Exp), a)
            a = A(lambda: s.activation(w2, w2, ACT.Exp))
            frv = fr[:, 0:aw].rearrange("p (h d) -> p h d", h=heads)
            tv = Ts.rearrange("p (h d) -> p h d", h=heads)
            V(lambda: v.tensor_tensor(frv, frv, bc(w1.unsqueeze(2), [P, heads, 65]), ALU.mult), a)
            V(lambda: v.tensor_tensor(tv, PS[2][:, 0:aw].rearrange("p (h d) -> p h d", h=heads),
                                      bc(w2.unsqueeze(2), [P, heads, 65]), ALU.mult), b)
            VL(lambda: v.tensor_tensor(frv, frv, tv, ALU.add))
            a = VL(lambda: v.tensor_copy(mr, Mx))
            return scatter(st[:], fr, fixs[:], EP - 1, a, sem="row")

        m1_ = mend_soft(s1, T1, 1, k_step[NCH - 1], st_t, 14000)

        NG1 = arena(23400, 2, GN * 66)
        den = arena(24400, GN)
        xq = arena(24420, 2, 512)
        rl = arena(25500, 3, 512)
        used, ps_free, xq_free, rl_free = {}, {}, {}, {}
        zz2 = X
        xcols = 0
        for q in range(NG):
            nb = NG1[:, q % 2, :].rearrange("p (l d) -> p l d", l=GN)
            sl = slice(q * GN, (q + 1) * GN)
            for i in range(GN):
                tk = gather(nb[:, i, :], s1[:], endi[:, q * GN + i:q * GN + i + 1], m1_, used.get(q - 2), sem=f"n{q % 2}")
            V(lambda nb=nb: v.tensor_scalar(den, nb[:, :, D], 1e-16, None, op0=ALU.max), tk, ("dve", Q.value["dve"]))
            VL(lambda: v.reciprocal(den, den))
            VL(lambda nb=nb: v.tensor_tensor(nb[:, :, 0:D], nb[:, :, 0:D], bc(den.unsqueeze(2), [P, GN, D]), ALU.mult))
            VL(lambda nb=nb, sl=sl: v.tensor_tensor(nb[:, :, 0:D], nb[:, :, 0:D], X[:, sl, :], ALU.add))
            used[q] = k = norm(nb[:, :, 0:D], X[:, sl, :], sq, mu, rs, ("dve", Q.value["dve"]))
            xw = ld(xt2.rearrange("(p l) d -> p l d", l=NL)[:, sl, :].rearrange("p l d -> p (l d)"),
                    X[:, sl, :].rearrange("p l d -> p (l d)"), k, sem="xt")
            for l in range(q * GN, (q + 1) * GN):
                sc_done = scatter(xd, X[:, l, :], stai[:, l:l + 1], EP - 1, k, *[k_xb[c] for c in range(NCH - 3, NCH)], sem="sc")
            for l0 in range(q * GN, (q + 1) * GN, 4):
                nl_ = min(4, (q + 1) * GN - l0)
                u = xcols
                xcols += 1
                for i in range(nl_):
                    a = T(lambda i=i, l0=l0, u=u: t.transpose(PS[u % 2][0:D, i * P:(i + 1) * P], X[:, l0 + i, :], ident[:]),
                          k, ps_free.get(("t", u - 2)))
                w_ = nl_ * P
                a = V(lambda u=u, w_=w_: v.tensor_copy(xq[0:D, u % 2, 0:w_], PS[u % 2][0:D, 0:w_]), a, xq_free.get(u - 2))
                ps_free[("t", u)] = a
                for ch in range(3):
                    b = T(lambda ch=ch, u=u, w_=w_: t.matmul(PS[2 + ch][:, 0:w_], WS[:, ch * P:(ch + 1) * P],
                                                            xq[0:D, u % 2, 0:w_], start=True, stop=True),
                          a, ps_free.get(("z", ch)))
                    ps_free[("z", ch)] = A(lambda ch=ch, w_=w_: s.activation(rl[:, ch, 0:w_], PS[2 + ch][:, 0:w_], ACT.Relu),
                                           b, rl_free.get(u - 1))
                for i in range(nl_):
                    for ch in range(3):
                        T(lambda i=i, ch=ch: t.matmul(PS[5][:, i * H:(i + 1) * H], rl[:, ch, i * P:(i + 1) * P], A8[:, ch, :],
                                                      start=(ch == 0), stop=False), ps_free[("z", 2)], ps_free.get("e"))
                    b = T(lambda i=i, u=u: t.matmul(PS[5][:, i * H:(i + 1) * H], xq[0:D, u % 2, i * P:(i + 1) * P], Vs[:],
                                                    start=False, stop=True))
                xq_free[u] = rl_free[u] = b
                ps_free["e"] = V(lambda l0=l0, nl_=nl_: v.tensor_copy(
                    es[:, l0:l0 + nl_, :], PS[5][:, 0:nl_ * H].rearrange("p (l h) -> p l h", h=H)), b)
        k_end = ("dve", Q.value["dve"])
        fence(k_end, ("act", Q.value["act"]), ("pe", Q.value["pe"]))

        NX = 5
        XBN = 4
        XS = arena(0, NX, CH * P)
        XB2 = arena(10240, XBN, CH * D)
        S2 = arena(14336, 2, CH * RW)
        XT2 = arena(27008, 3, 512)
        RL2 = arena(28544, 2, 3 * 512)
        eb = arena(31616, H, CH)
        mf2 = arena(31712, H, CH)
        mb2 = arena(31808, H, CH)
        Bf = arena(31904, H, CH)
        Bb = arena(32000, H, CH)
        pf2 = arena(32096, 2, H * (CH + 1))
        tmp2 = arena(32300, H, 65)
        stored, k_step, k_xb, freeXB, k_fill, k_g, pxd = {}, {}, {}, {}, {}, {}, {}
        freeXS, k_T, k_E, k_px = {}, {}, {}, {}
        V(lambda: v.memset(Bf, -BIG))
        V(lambda: v.memset(Bb, -BIG))

        def xsv(c):
            return XS[:, c % NX, :].rearrange("p (j d) -> p j d", j=CH)

        gi = gather(xsv(0)[:, 0, D:P], xt2, Dd[:, 0:1], xw, sem="xdi")

        def g2(c):
            for j in range(CH):
                k_g[c] = gather(xsv(c)[:, j, 0:D], xt2, Si[:, c * CH + j:c * CH + j + 1], xw,
                                freeXS.get(c - NX), sem=f"g{c % NX}")

        def fills2(c):
            XBv = XB2[:, c % XBN, :].rearrange("p (j d) -> p j d", j=CH)
            cur, prv = xsv(c), xsv(c - 1)
            mine = [None]

            def one(j):
                if c == 0 and j == 0:
                    return lambda: None
                pr = cur[:, j - 1, D:P] if j else prv[:, CH - 1, D:P]

                def f():
                    mine[0] = V(lambda: v.scalar_tensor_tensor(
                        out=cur[:, j, D:P], in0=pr, scalar=gf[:, c * CH + j:c * CH + j + 1], in1=XBv[:, j, :],
                        op0=ALU.mult, op1=ALU.add), k_xb[c], mine[0] or k_fill.get(c - 1), gi, freeXS.get(c - NX))
                    k_fill[c] = freeXB[c] = mine[0]
                return f
            return [one(j) for j in range(CH)]

        evT, zT, peM, peE, relu = {}, {}, {}, {}, {}
        NGR = CH // 4

        def pe_t(u):
            c, q = divmod(u, NGR)
            for i in range(4):
                a = T(lambda i=i: t.transpose(PS[u % 2][:, i * P:(i + 1) * P], xsv(c)[:, 4 * q + i, :], ident[:]),
                      k_g[c], k_fill[c], evT.get(u - 2))
            evT[u] = A(lambda: s.copy(XT2[:, u % 3, :], PS[u % 2][:]), a, peE.get(u - 3))
            if q == NGR - 1:
                k_T[c] = a

        def pe_m(u):
            for ch in range(3):
                bnk = 2 + (3 * u + ch) % 4
                a = T(lambda ch=ch, bnk=bnk: t.matmul(PS[bnk][:], WLR[:, ch * P:(ch + 1) * P], XT2[:, u % 3, :],
                                                      start=True, stop=True), evT[u], relu.get(3 * u + ch - 4))
                relu[3 * u + ch] = A(lambda ch=ch, bnk=bnk: s.activation(
                    RL2[:, u % 2, ch * 512:(ch + 1) * 512], PS[bnk][:], ACT.Relu), a, peE.get(u - 2))

        e_read = {}

        def pe_e(u):
            c, q = divmod(u, NGR)
            for i in range(4):
                col = (4 * q + i) * H
                for ch in range(3):
                    T(lambda i=i, ch=ch, col=col: t.matmul(
                        PS[6 + c % 2][:, col:col + H], RL2[:, u % 2, ch * 512 + i * P:ch * 512 + (i + 1) * P], A8[:, ch, :],
                        start=(ch == 0), stop=False), relu[3 * u + 2], e_read.get(c - 2))
                peE[u] = T(lambda i=i, col=col: t.matmul(PS[6 + c % 2][:, col:col + H], XT2[:, u % 3, i * P:(i + 1) * P], Vm[:],
                                                         start=False, stop=True))
            if q == NGR - 1:
                k_E[c] = peE[u]

        NU = NCH * NGR
        pe_at = [0]

        def pe_chunk(c):
            while pe_at[0] < (c + 1) * NGR:
                u = pe_at[0]
                pe_t(u)
                if u >= 1:
                    pe_m(u - 1)
                if u >= 2:
                    pe_e(u - 2)
                pe_at[0] += 1
            if c == NCH - 1:
                pe_m(NU - 1)
                pe_e(NU - 2)
                pe_e(NU - 1)

        def soft2(c):
            ep = PS[6 + c % 2][:, 0:CH * H].rearrange("p (j h) -> p h j", h=H)
            Sv = S2[:, c % 2, :].rearrange("p (j d) -> p j d", j=CH)
            Sp = S2[:, (c - 1) % 2, :].rearrange("p (j d) -> p j d", j=CH)
            pe_ = pf2[:, c % 2, 0:H * CH].rearrange("p (h j) -> p h j", h=H)
            pq = pf2[:, c % 2, H * CH:H * CH + H]
            mine = [None]
            fl = lambda a_: a_.rearrange("p h j -> p (h j)")

            def L(fn, *w):
                def f():
                    mine[0] = V(fn, mine[0], *w)
                return f

            def first():
                mine[0] = e_read[c] = V(lambda: v.tensor_copy(eb, ep), k_E[c])
            ops = [first,
                   lambda: V(lambda: v.tensor_copy(Bf[:, :, 1:CH], bc(Bn[:, c * CH + 1:(c + 1) * CH].unsqueeze(1), [P, H, CH - 1])),
                             ("dve", Q.value["dve"])),
                   L(lambda: v.tensor_copy(Bb[:, :, 0:CH - 1], bc(Bn[:, c * CH + 1:(c + 1) * CH].unsqueeze(1), [P, H, CH - 1])))]
            if c:
                ops.append(L(lambda: v.scalar_tensor_tensor(out=eb[:, :, 0], in0=Sp[:, CH - 1, HW:], scalar=Bn[:, c * CH:c * CH + 1],
                                                            in1=eb[:, :, 0], op0=ALU.add, op1=ALU.max)))
            ops += [L(lambda: v.tensor_tensor_scan(fl(mf2), fl(Bf), fl(eb), -BIG, ALU.add, ALU.max)),
                    L(lambda: v.tensor_tensor_scan(fl(mb2)[:, ::-1], fl(Bb)[:, ::-1], fl(mf2)[:, ::-1], -BIG, ALU.add, ALU.max)),
                    L(lambda: v.tensor_tensor(pe_, ep, mb2, ALU.subtract))]

            def note():
                e_read[c] = mine[0]
            ops.append(note)
            if c:
                ops.append(L(lambda: v.scalar_tensor_tensor(out=pq, in0=Sp[:, CH - 1, HW:], scalar=Bn[:, c * CH:c * CH + 1],
                                                            in1=mb2[:, :, 0], op0=ALU.add, op1=ALU.subtract)))
            n_ = H * (CH + 1) if c else H * CH

            def ex():
                pxd[c] = A(lambda: s.activation(pf2[:, c % 2, 0:n_], pf2[:, c % 2, 0:n_], ACT.Exp), mine[0])
            ops.append(ex)
            ops.append(L(lambda: v.tensor_copy(Sv[:, :, HW:].rearrange("p j h -> p h j"), mb2), stored.get(c - 2), k_step.get(c - 1)))
            return ops

        def px2(c):
            Sv = S2[:, c % 2, :].rearrange("p (j d) -> p j d", j=CH)
            pe_ = pf2[:, c % 2, 0:H * CH].rearrange("p (h j) -> p h j", h=H)
            for h in range(H):
                V(lambda h=h: v.tensor_tensor(Sv[:, :, h * 65:h * 65 + D], xsv(c)[:, :, 0:D],
                                              bc(pe_[:, h, :].unsqueeze(2), [P, CH, D]), ALU.mult), pxd[c], stored.get(c - 2),
                  k_step.get(c - 1))
            k_px[c] = V(lambda: v.tensor_copy(
                Sv[:, :, 0:HW].rearrange("p j (h d) -> p j h d", h=H)[:, :, :, D].rearrange("p j h -> p h j"), pe_))
            freeXS[c] = k_px[c]

        def steps2(c):
            Sv = S2[:, c % 2, :].rearrange("p (j d) -> p j d", j=CH)
            Sp = S2[:, (c - 1) % 2, :].rearrange("p (j d) -> p j d", j=CH)
            pq = pf2[:, c % 2, H * CH:H * CH + H]
            mine = [None]

            def one(j):
                if c == 0 and j == 0:
                    return lambda: None
                if j == 0:
                    def f():
                        a = V(lambda: v.tensor_tensor(tmp2, Sp[:, CH - 1, 0:HW].rearrange("p (h d) -> p h d", h=H),
                                                      bc(pq.unsqueeze(2), [P, H, 65]), ALU.mult), k_px[c], k_step.get(c - 1))
                        mine[0] = V(lambda: v.tensor_tensor(Sv[:, 0, 0:HW], Sv[:, 0, 0:HW], tmp2.rearrange("p h d -> p (h d)"),
                                                            ALU.add), a)
                    return f

                def f():
                    mine[0] = V(lambda: v.scalar_tensor_tensor(
                        out=Sv[:, j, 0:HW], in0=Sv[:, j - 1, 0:HW], scalar=gf[:, c * CH + j:c * CH + j + 1],
                        in1=Sv[:, j, 0:HW], op0=ALU.mult, op1=ALU.add), mine[0] or k_px[c])
                    k_step[c] = mine[0]
                return f
            return [one(j) for j in range(CH)]

        for c in range(XBN):
            xb(c, XB2, freeXB, sc_done)
        for c in range(3):
            g2(c)
            merged(fills2(c))
        pe_chunk(0)
        pe_chunk(1)
        merged(soft2(0))
        px2(0)
        for c in range(NCH):
            if c + 2 < NCH:
                pe_chunk(c + 2)
            if c + 3 < NCH:
                g2(c + 3)
            if c + 4 < NCH:
                xb(c + 4, XB2, freeXB, sc_done)
            B_ = []
            if c + 3 < NCH:
                B_ += fills2(c + 3)
            if c + 1 < NCH:
                B_ += soft2(c + 1)
            merged(steps2(c), B_)
            stored[c] = ld(chunk_view(s2, c, RW), S2[:, c % 2, :], k_step[c], sem=f"s{c % 2}")
            if c + 1 < NCH:
                px2(c + 1)
        st_t = [stored[c] for c in range(NCH - 2, NCH)]
        T2 = S2[:, (NCH - 1) % 2, :].rearrange("p (j d) -> p j d", j=CH)[:, CH - 1, :]
        m2_ = mend_soft(s2, T2, H, k_step[NCH - 1], st_t, 0)
        fence(("pe", Q.value["pe"]), ("act", Q.value["act"]))
        k_m2 = ("dve", Q.value["dve"])

        N2 = arena(19300 + 900, 2, GN * RW)
        U = arena(3500, GN, H * D)
        TU = arena(6200, GN, D)
        UT = arena(13200, 3, P)
        wv = arena(13600, 6, GN * H)
        O2 = arena(13900, GN, D)
        O3 = arena(14400, GN, D)
        used, ut_free = {}, {}
        kcol = NL
        N1, AL_ = None, None

        def loop_extra(l, ps, p):
            V(lambda: v.tensor_tensor(R[:, l, :], X[:, l, :], ps[:, 0:D], ALU.add), p)
            VL(lambda: v.tensor_tensor(R[:, l, :], R[:, l, :], b3[:], ALU.add))

        for q in range(NG):
            nb = N2[:, q % 2, :].rearrange("p (l d) -> p l d", l=GN)
            sl = slice(q * GN, (q + 1) * GN)
            for i in range(GN):
                tk = gather(nb[:, i, :], s2[:], endi[:, q * GN + i:q * GN + i + 1], m2_, k_m2, used.get(q - 2), sem=f"n{q % 2}")
            W_ = [wv[:, i, :].rearrange("p (l h) -> p l h", h=H) for i in range(6)]
            mm, w1, w3_, dd = W_[0], W_[1], W_[2], W_[3]
            nv = nb[:, :, 0:HW].rearrange("p l (h d) -> p l h d", h=H)
            V(lambda nb=nb, sl=sl: v.tensor_tensor(mm, nb[:, :, HW:], es[:, sl, :], ALU.max), tk, ("dve", Q.value["dve"]))
            VL(lambda nb=nb: v.tensor_tensor(w1, nb[:, :, HW:], mm, ALU.subtract))
            a = V(lambda sl=sl: v.tensor_tensor(w3_, es[:, sl, :], mm, ALU.subtract))
            A(lambda: s.activation(w1, w1, ACT.Exp), a)
            a = A(lambda: s.activation(w3_, w3_, ACT.Exp))
            V(lambda nv=nv: v.tensor_tensor(dd, nv[:, :, :, D], w1, ALU.mult), a)
            VL(lambda: v.tensor_tensor(dd, dd, w3_, ALU.add))
            VL(lambda: v.tensor_scalar(dd, dd, 1e-16, float(H), op0=ALU.add, op1=ALU.mult))
            VL(lambda: v.reciprocal(dd, dd))
            VL(lambda: v.tensor_tensor(w1, w1, dd, ALU.mult))
            VL(lambda: v.tensor_tensor(w3_, w3_, dd, ALU.mult))
            for h in range(H):
                a = V(lambda h=h, nv=nv: v.tensor_tensor(U[:, :, h * D:(h + 1) * D], nv[:, :, h, 0:D],
                                                         bc(w1[:, :, h:h + 1], [P, GN, D]), ALU.mult),
                      ("dve", Q.value["dve"]), ut_free.get("U"))
                used[q] = a
                VL(lambda h=h, sl=sl: v.tensor_tensor(TU, X[:, sl, :], bc(w3_[:, :, h:h + 1], [P, GN, D]), ALU.mult))
                k_u = VL(lambda h=h: v.tensor_tensor(U[:, :, h * D:(h + 1) * D], U[:, :, h * D:(h + 1) * D], TU, ALU.add))
            for i in range(GN):
                for ch in range(3):
                    a = T(lambda i=i, ch=ch: t.transpose(PS[0][:, ch * P:(ch + 1) * P], U[:, i, ch * P:(ch + 1) * P], ident[:]),
                          k_u, ut_free.get("ps0"))
                ut_free["U"] = a
                ut_free["ps0"] = e_ = A(lambda: s.copy(UT.rearrange("p c n -> p (c n)"), PS[0][:, 0:3 * P]), a, ut_free.get("ut"))
                for ch in range(3):
                    b = T(lambda i=i, ch=ch: t.matmul(PS[1][:, i * D:(i + 1) * D], UT[:, ch, :], W2[:, ch, :],
                                                      start=(ch == 0), stop=(ch == 2)), e_, ut_free.get("ps1"))
                ut_free["ut"] = b
            ps1 = PS[1][:, 0:GN * D].rearrange("p (l d) -> p l d", d=D)
            ut_free["ps1"] = V(lambda: v.tensor_tensor(O2, ps1, bc(b2[:].unsqueeze(1), [P, GN, D]), ALU.add), b,
                               ("dve", Q.value["dve"]))
            a = VL(lambda: v.tensor_scalar(O3, O2, 0.0, None, op0=ALU.min))
            a = A(lambda: s.activation(O3, O3, ACT.Exp), a)
            LAM, ALP = 1.0507009873554805, 1.6732632423543772
            V(lambda: v.tensor_scalar(O2, O2, 0.0, LAM, op0=ALU.max, op1=ALU.mult), ("dve", Q.value["dve"]))
            VL(lambda: v.tensor_scalar(O3, O3, -1.0, LAM * ALP, op0=ALU.add, op1=ALU.mult), a)
            VL(lambda: v.tensor_tensor(O2, O2, O3, ALU.add))
            VL(lambda sl=sl: v.tensor_tensor(O2, O2, X[:, sl, :], ALU.add))
            k = norm(O2, X[:, sl, :], sq, mu, rs, ("dve", Q.value["dve"]))
            for l in range(q * GN, (q + 1) * GN):
                table_col(l, kcol, W3, R3, y3, (k,), None)
                lk = kcol
                p = T(lambda lk=lk: t.matmul(PS[2 + lk % 2][:, 0:D], xtt[0:D, lk % 2, :], W3[:, R3 * D:],
                                             start=True, stop=True), ev_x[("x", lk)])
                pe_x[("y", lk)] = p
                V(lambda l=l, lk=lk: v.tensor_tensor(R[:, l, :], X[:, l, :], PS[2 + lk % 2][:, 0:D], ALU.add), p)
                ev_x[("x", lk)] = VL(lambda l=l: v.tensor_tensor(R[:, l, :], R[:, l, :], b3[:], ALU.add))
                kcol += 1
        t_y3 = [ydone[k_] for k_ in range(kcol - 4, kcol)]
        k_end = ("dve", Q.value["dve"])

        T3, k_t, st_t = linear_chunks(y3, I3, s3, [*t_y3, k_end])
        m3 = mend_linear(s3, T3, k_t, st_t)
        used = {}
        ov = out.rearrange("(p l) d -> p l d", l=NL)
        NG3 = arena(23400, 2, GN * D)
        for q in range(NG):
            nb = NG3[:, q % 2, :].rearrange("p (l d) -> p l d", l=GN)
            sl = slice(q * GN, (q + 1) * GN)
            for i in range(GN):
                tk = gather(nb[:, i, :], s3[:], endi[:, q * GN + i:q * GN + i + 1], m3, used.get(q - 2), sem=f"n{q % 2}")
            VL(lambda nb=nb, sl=sl: v.tensor_tensor(nb, nb, R[:, sl, :], ALU.add), tk)
            used[q] = k = norm(nb, X[:, sl, :], sq, mu, rs, ("dve", Q.value["dve"]))
            fin = ld(ov[:, sl, :].rearrange("p l d -> p (l d)"), X[:, sl, :].rearrange("p l d -> p (l d)"), k, sem="out")
        Q.wait("sync", fin, ("z", Q.value["z"]), ("zr", Q.value["zr"]))
        for n_ in names:
            if n_ in Q.value and n_ not in ("dve", "act", "pe", "pool", "fdve", "fpe", "fpool", "fsc", "fld"):
                Q.wait("sync", (n_, Q.value[n_]))

        block = ctx.enter_context(nc.Block())

        @block.sync
        def _(e):
            Q.play("sync", e)

        @block.gpsimd
        def _(e):
            Q.play("gpsimd", e)

        @block.scalar
        def _(e):
            Q.play("scalar", e)

        @block.vector
        def _(e):
            Q.play("vector", e)

        @block.tensor
        def _(e):
            Q.play("tensor", e)


_INS = ["x", "src", "dst", "edge_type_16", "edge_type_8", "L0_gnn_weight", "L1_gnn_beta", "L2_gnn_W_l", "L2_gnn_W_r",
        "L2_gnn_att", "L2_gnn_bias", "L3_gnn_W", "L3_gnn_coeff", "L3_gnn_h_bias", "L3_gnn_loop_weight"]


def kernel(**inputs):
    import numpy as np
    import concourse.bacc as bacc
    from concourse.bass_utils import run_bass_kernel_spmd

    nc = bacc.Bacc("TRN2", target_bir_lowering=False, num_devices=1)
    arrays, args = {}, []
    for name in _INS:
        a = np.ascontiguousarray(inputs[name])
        if name == "x":
            a = np.concatenate([a, np.zeros((NN - N, D), a.dtype)])
        elif name == "dst":
            a = np.concatenate([a, np.full((EP + NC - E,), N, a.dtype)])
        elif name in ("src", "edge_type_16", "edge_type_8"):
            a = np.concatenate([a, np.zeros((EP - E,), a.dtype)])
        arrays["in_" + name] = a
        args.append(nc.dram_tensor("in_" + name, a.shape, mybir.dt.from_np(a.dtype), kind="ExternalInput").ap())
    args.append(nc.dram_tensor("out_0", (NN, D), mybir.dt.float32, kind="ExternalOutput").ap())
    build(nc, *args)
    r = run_bass_kernel_spmd(nc, [arrays], core_ids=[0])
    return np.asarray(r.results[0]["out_0"])[:N]
```

```python
from contextlib import ExitStack

import concourse.bass as bass
from concourse import mybir

P = 128
D = 64
N = 6250
NL = 49
NN = P * NL
E = 106250
NC = 832
EP = P * NC
CH = 16
NCH = NC // CH
R0 = 16
R3 = 8
H = 6
HW = H * 65
RW = HW + H
BIG = 1e30
SKIP = 200000.0
GN = 7
NG = NL // GN


class Queues:

    ENGINES = ("sync", "gpsimd", "scalar", "vector", "tensor")

    def __init__(self, sems):
        self.items = {e: [] for e in self.ENGINES}
        self.seen = {e: {} for e in self.ENGINES}
        self.value = {}
        self.sems = sems
        self.saved = {}

    def wait(self, eng, *tokens):
        for t in tokens:
            if t is None:
                continue
            name, v = t
            if v > self.seen[eng].get(name, 0):
                self.seen[eng][name] = v
                self.items[eng].append(("wait", self.sems[name], v))

    def emit(self, eng, fn, waits, sem, inc):
        self.wait(eng, *waits)
        self.value[sem] = self.value.get(sem, 0) + inc
        self.items[eng].append(("do", fn, self.sems[sem], inc))
        return (sem, self.value[sem])

    def begin_if(self, eng, flag):
        self.items[eng].append(("if", flag))
        self.saved[eng] = dict(self.seen[eng])

    def end_if(self, eng):
        self.items[eng].append(("end",))
        self.seen[eng] = self.saved.pop(eng)

    def play(self, eng, e):
        stack = []
        for it in self.items[eng]:
            if it[0] == "wait":
                e.wait_ge(it[1], it[2])
            elif it[0] == "do":
                it[1](e).then_inc(it[2], it[3])
            elif it[0] == "if":
                reg = e.value_load(it[1])
                c = e.If(reg != 0)
                c.__enter__()
                stack.append(c)
            else:
                stack.pop().__exit__(None, None, None)


def build(nc, x, src, dst, et16, et8, w0, beta, wl, wr, att, bias2, w3, coeff, hbias, loopw, out):
    F32 = mybir.dt.float32
    I32 = mybir.dt.int32
    BF16 = mybir.dt.bfloat16
    ALU = mybir.AluOpType
    ACT = mybir.ActivationFunctionType
    AX = mybir.AxisListType.X

    def dram(name, shape, dt=F32):
        return nc.dram_tensor(name, shape, dt).ap()

    y0 = dram("y0", (NN * R0, D))
    y3 = dram("y3", (NN * R3, D))
    s0 = dram("s0", (EP + 1, D))
    s1 = dram("s1", (EP + 1, 66))
    s2 = dram("s2", (EP + 1, RW))
    s3 = dram("s3", (EP + 1, D))
    xd = dram("xd", (EP, D))
    xt1 = dram("xt1", (NN, 65))
    xt2 = dram("xt2", (NN, D))
    cntd = dram("cntd", (NN,))
    srt = dram("srt", (EP, 4), I32)

    with ExitStack() as ctx:
        names = ["dve", "act", "pe", "pool", "ld", "ldn", "ldw", "z", "cnt", "row", "xdi", "xt", "sc", "zr", "out"]
        names += [f"ysb{i}" for i in range(4)] + [f"g{i}" for i in range(5)] + [f"x{i}" for i in range(3)]
        names += [f"s{i}" for i in range(4)] + [f"n{i}" for i in range(2)]
        names += [f"f{k}{n}" for k in range(3) for n in ("dve", "pe", "pool", "sc", "ld", "cnt", "xs")]
        sems = {n: ctx.enter_context(nc.semaphore("k_" + n)) for n in names}
        Q = Queues(sems)

        def sb(name, shape, dt=F32):
            return ctx.enter_context(nc.sbuf_tensor(name, shape, dt))

        class Em:

            def __init__(self, pre):
                self.pre = pre

            def V(self, fn, *w):
                return Q.emit("vector", lambda e: fn(), w, self.pre + "dve", 1)

            def VL(self, fn, *w):
                return self.V(fn, self.last("dve"), *w)

            def T(self, fn, *w):
                return Q.emit("tensor", lambda e: fn(), w, self.pre + "pe", 1)

            def G(self, fn, *w):
                return Q.emit("gpsimd", lambda e: fn(), w, self.pre + "pool", 1)

            def last(self, n):
                return (self.pre + n, Q.value.get(self.pre + n, 0))

        main = Em("")
        V, VL, T, G = main.V, main.VL, main.T, main.G

        def A(fn, *w):
            return Q.emit("scalar", lambda e: fn(), w, "act", 1)

        def ld(o, i, *w, sem, eng="sync"):
            return Q.emit(eng, lambda e: e.dma_start(o, i, allow_slow_non_contiguous=True), w, sem, 16)

        def gather(o, table, idx, *w, sem):
            return Q.emit("gpsimd", lambda e: e.indirect_dma_start(
                out=o, out_offset=None, in_=table,
                in_offset=bass.IndirectOffsetOnAxis(ap=idx, axis=0)), w, sem, 16)

        def scatter(table, i, idx, bound, *w, sem):
            return Q.emit("gpsimd", lambda e: e.indirect_dma_start(
                out=table, out_offset=bass.IndirectOffsetOnAxis(ap=idx, axis=0), in_=i,
                in_offset=None, bounds_check=bound, oob_is_err=False), w, sem, 16)

        v, s, g, t = nc.vector, nc.scalar, nc.gpsimd, nc.tensor

        Dd = sb("Dd", [P, NC], I32)
        Si = sb("Si", [P, NC], I32)
        I3 = sb("I3", [P, NC], I32)
        gf = sb("gf", [P, NC])
        Bn = sb("Bn", [P, NC + 1])
        X = sb("X", [P, NL, D])
        R = sb("R", [P, NL, D])
        I0 = R[:].rearrange("p l d -> p (l d)")[:, 0:NC].bitcast(I32)
        W0 = R[:].rearrange("p l d -> p (l d)")[0:D, NC:NC + R0 * D]
        ident = sb("ident", [P, P])
        ones = sb("ones", [P, P])
        lower = sb("lower", [P, P])
        sm = sb("sm", [P, 32])
        dn = sb("dn", [P, 1], I32)
        flag = sb("flag", [P, 2], I32)
        Cq = sb("Cq", [P, P])
        CTn = sb("CTn", [P, P])
        En = sb("En", [P, P])
        cntn = sb("cntn", [P, NL])
        incl = sb("incl", [P, NL])
        nfl = sb("nfl", [P, NL])
        endi = sb("endi", [P, NL], I32)
        stai = sb("stai", [P, NL], I32)
        fixg = sb("fixg", [P, 1], I32)
        fixs = sb("fixs", [P, 1], I32)
        W3 = sb("W3", [D, R3 * D + D])
        WLR = sb("WLR", [P, H * D])
        WS = sb("WS", [D, H * D])
        W2 = sb("W2", [P, 3, D])
        A8 = sb("A8", [P, 3, 32])
        Vm = sb("Vm", [P, 32])
        Vs = sb("Vs", [D, H])
        att3 = sb("att3", [P, 3])
        co = sb("co", [D, R3 * 2])
        wb = sb("wb", [D, 2, D])
        b2 = sb("b2", [P, D])
        b3 = sb("b3", [P, D])
        bet = sb("bet", [P, 1])
        es = sb("es", [P, NL, H])
        hi98 = sb("hi98", [P, 98], I32)[:]
        lo64 = sb("lo64", [P, 64], I32)[:]
        zrow = sb("zrow", [1, RW])
        zr1 = sb("zr1", [1, 66])
        ARENA = 38400
        AR = sb("AR", [P, ARENA])

        def arena(off, *shape):
            n = 1
            for k in shape:
                n *= k
            assert off + n <= ARENA, (off, shape)
            a = AR[:, off:off + n]
            if len(shape) == 2:
                a = a.rearrange("p (a b) -> p a b", a=shape[0])
            if len(shape) == 3:
                a = a.rearrange("p (a b c) -> p a b c", a=shape[0], b=shape[1])
            return a

        PS = [ctx.enter_context(nc.psum_tensor(f"ps{i}", [P, 512], F32)) for i in range(8)]

        def bc(a, shape):
            return a.broadcast_to(shape)

        AF = AR[:, 0:NC * 2].bitcast(I32)
        Df = arena(2100, NC)
        e16t, e8t = AF[:, 0:NC], AF[:, NC:2 * NC]
        ld(Dd[:], dst[0:EP].rearrange("(p j) -> p j", j=NC), sem="ld")
        ld(dn[:], dst[NC:NC + EP].rearrange("(p j) -> p j", j=NC)[:, 0:1], sem="ld")
        ld(Si[:], src.rearrange("(p j) -> p j", j=NC), sem="ld")
        ld(e16t, et16.rearrange("(p j) -> p j", j=NC), sem="ld")
        l_edges = ld(e8t, et8.rearrange("(p j) -> p j", j=NC), sem="ld")
        l_x = ld(X[:], x.rearrange("(p l) d -> p l d", l=NL), sem="ldn")
        ld(W0.rearrange("p (r o) -> p r o", r=R0), w0.rearrange("r i o -> i r o"), sem="ldw")
        l_w0 = None
        ld(WLR[0:D, :], wl, sem="ldw")
        ld(WLR[D:P, :], wr, sem="ldw")
        ld(WS[:], wr, sem="ldw")
        wlv = wl.rearrange("f (c h o) -> f c h o", c=3, h=2)
        ld(W2[0:D, :, :], wlv[:, :, 0, :], sem="ldw")
        ld(W2[D:P, :, :], wlv[:, :, 1, :], sem="ldw")
        attf = att.rearrange("h o -> (h o)")
        ld(att3[:], attf.rearrange("(c q) -> q c", c=3), sem="ldw")
        ld(co[:], coeff.rearrange("r b -> (r b)").partition_broadcast(D), sem="ldw")
        ld(wb[:], w3.rearrange("b i o -> i b o"), sem="ldw")
        ld(W3[:, R3 * D:], loopw, sem="ldw")
        ld(b2[:], bias2.partition_broadcast(P), sem="ldw")
        ld(b3[:], hbias.partition_broadcast(P), sem="ldw")
        ld(bet[:], beta.partition_broadcast(P), sem="ldw")
        attb = arena(2 * NC, H, D)
        l_w = ld(attb.rearrange("p h o -> p (h o)"), attf.partition_broadcast(P), sem="ldw")

        k_ones = V(lambda: v.memset(ones[:], 1.0))
        c1 = G(lambda: g.affine_select(out=ident[:], in_=ones[:], compare_op=ALU.is_equal, fill=0.0, base=0,
                                       pattern=[[-1, P]], channel_multiplier=1), k_ones)
        c2 = G(lambda: g.affine_select(out=lower[:], in_=ones[:], compare_op=ALU.is_gt, fill=0.0, base=0,
                                       pattern=[[1, P]], channel_multiplier=-1))
        pidx = sm[:, 30:31].bitcast(I32)
        G(lambda: g.iota(hi98, [[1, 98]], base=0, channel_multiplier=0))
        G(lambda: g.iota(pidx, [[0, 1]], base=0, channel_multiplier=1))
        c3 = G(lambda: g.iota(lo64, [[1, 64]], base=0, channel_multiplier=0))

        zt = arena(31500, CH * D)
        k_z = V(lambda: v.memset(zt, 0.0))
        V(lambda: v.memset(zrow[:], 0.0))
        VL(lambda: v.memset(zrow[0:1, HW:], -BIG))
        V(lambda: v.memset(zr1[:], 0.0))
        k_zr = VL(lambda: v.memset(zr1[0:1, 65:66], -BIG))
        ld(s0[EP:EP + 1, :], zr1[0:1, 0:D], k_zr, sem="zr")
        ld(s3[EP:EP + 1, :], zr1[0:1, 0:D], k_zr, sem="zr")
        ld(s1[EP:EP + 1, :], zr1[:], k_zr, sem="zr")
        l_zr = ld(s2[EP:EP + 1, :], zrow[:], k_zr, sem="zr")

        dnf, bad, badc = sm[:, 0:1], sm[:, 1:2], sm[:, 2:3]
        scr = arena(5000, NC)
        V(lambda: v.tensor_copy(Df, Dd[:]), l_edges)
        VL(lambda: v.tensor_copy(dnf, dn[:]))
        VL(lambda: v.tensor_tensor(scr[:, 0:NC - 1], Df[:, 0:NC - 1], Df[:, 1:NC], ALU.is_gt))
        VL(lambda: v.tensor_tensor(scr[:, NC - 1:NC], Df[:, NC - 1:NC], dnf, ALU.is_gt))
        a = VL(lambda: v.tensor_reduce(bad, scr, AX, ALU.max))
        b = T(lambda: t.matmul(PS[0][:, 0:1], ones[:], bad, start=True, stop=True), a)
        k_flag = V(lambda: v.tensor_copy(flag[:, 0:1], PS[0][:, 0:1]), b)

        def resort(em, swap):
            FV, pre = em.VL, em.pre
            NB = (NN + 511) // 512
            IO = arena(5000, NN).bitcast(I32)
            CN = arena(5000 + NN, NN)
            JJ = arena(5000 + 2 * NN, NN)
            RR = arena(5000 + 3 * NN, NC, 4).bitcast(I32)
            rank = arena(5000 + 3 * NN + 4 * NC, NC)
            posi = gf[:].bitcast(I32)
            tmp = Bn[:, 0:NC]
            io = em.G(lambda: g.iota(IO, [[1, NN]], base=0, channel_multiplier=0))
            cols = (Dd[:], Si[:], e16t, e8t) if swap else (Si[:], Dd[:], e16t, e8t)
            for k, c in enumerate(cols):
                FV(lambda k=k, c=c: v.tensor_copy(RR[:, :, k], c))
            FV(lambda: v.tensor_copy(Df, RR[:, :, 1]))
            FV(lambda: v.memset(CN, 0.0), io)
            FV(lambda: v.memset(tmp, 0.0))
            FV(lambda: v.memset(rank, 0.0))
            for j in range(NC):
                FV(lambda j=j: v.scalar_tensor_tensor(out=JJ, in0=IO, scalar=Df[:, j:j + 1], in1=CN, op0=ALU.is_equal,
                                                      op1=ALU.mult, accum_out=rank[:, j:j + 1]))
                FV(lambda j=j: v.scalar_tensor_tensor(out=CN, in0=IO, scalar=Df[:, j:j + 1], in1=CN, op0=ALU.is_equal,
                                                      op1=ALU.add))
            done = em.last("dve")
            for bk in range(NB):
                lo, hi = bk * 512, min(NN, bk * 512 + 512)
                em.T(lambda lo=lo, hi=hi: t.matmul(PS[0][:, 0:hi - lo], ones[:], CN[:, lo:hi], start=True, stop=True), done)
                p = em.T(lambda lo=lo, hi=hi: t.matmul(PS[1][:, 0:hi - lo], lower[:], CN[:, lo:hi], start=True, stop=True), c2)
                FV(lambda lo=lo, hi=hi: v.tensor_copy(JJ[:, lo:hi], PS[0][:, 0:hi - lo]), p)
                done = FV(lambda lo=lo, hi=hi: v.tensor_copy(CN[:, lo:hi], PS[1][:, 0:hi - lo]))
            FV(lambda: v.tensor_tensor_scan(JJ, JJ, JJ, 0.0, ALU.add, ALU.bypass))
            FV(lambda: v.tensor_tensor(CN[:, 1:NN], CN[:, 1:NN], JJ[:, 0:NN - 1], ALU.add))
            for j in range(NC):
                FV(lambda j=j: v.scalar_tensor_tensor(out=JJ, in0=IO, scalar=Df[:, j:j + 1], in1=CN, op0=ALU.is_equal,
                                                      op1=ALU.mult, accum_out=tmp[:, j:j + 1]))
            FV(lambda: v.tensor_tensor(rank, rank, tmp, ALU.add))
            fin = FV(lambda: v.tensor_copy(posi, rank))
            for j in range(NC):
                sc = scatter(srt, RR[:, j, :], posi[:, j:j + 1], EP - 1, fin, sem=pre + "sc")
            sv = srt.rearrange("(p j) k -> p j k", j=NC)
            ld(RR, sv, sc, sem=pre + "ld")
            l = ld(dn[0:P - 1, :], sv[1:P, 0, 1:2], sc, sem=pre + "ld")
            FV(lambda: v.tensor_copy(Si[:], RR[:, :, 0]), l)
            FV(lambda: v.tensor_copy(Dd[:], RR[:, :, 1]))
            FV(lambda: v.tensor_copy(e16t, RR[:, :, 2]))
            FV(lambda: v.tensor_copy(e8t, RR[:, :, 3]))
            FV(lambda: v.tensor_copy(Df, Dd[:]))
            FV(lambda: v.tensor_copy(dnf, dn[:]))

        dhi = arena(3000, NC).bitcast(I32)
        dlo = arena(4000, NC).bitcast(I32)

        def flags(em):
            em.V(lambda: v.scalar_tensor_tensor(out=I3[:], in0=Si[:], scalar=8.0, in1=e8t, op0=ALU.mult, op1=ALU.add),
                 em.last("dve"))
            em.V(lambda: v.memset(gf[:, 0:1], 0.0))
            em.V(lambda: v.memset(Bn[:, NC:NC + 1], -BIG))
            em.V(lambda: v.tensor_tensor(gf[:, 1:NC], Df[:, 1:NC], Df[:, 0:NC - 1], ALU.is_equal))
            em.VL(lambda: v.tensor_scalar(Bn[:, 0:NC], gf[:], -1.0, BIG, op0=ALU.add, op1=ALU.mult))
            em.V(lambda: v.tensor_scalar(dhi, Dd[:], 6, None, op0=ALU.logical_shift_right))
            return em.V(lambda: v.tensor_scalar(dlo, Dd[:], 63, None, op0=ALU.bitwise_and))

        pf, cont, key, df_, eqn, inv, pos, eqc = (sm[:, k:k + 1] for k in range(3, 11))

        def masks(em):
            scr2 = arena(5000, NC)
            dg = arena(6000, 2, P)
            V, VL = em.V, em.VL
            V(lambda: v.tensor_copy(pf, pidx), c3)
            V(lambda: v.tensor_copy(df_, Df[:, 0:1]))
            V(lambda: v.tensor_tensor(eqn, Df[:, NC - 1:NC], dnf, ALU.is_equal), em.last("dve"))
            VL(lambda: v.tensor_scalar(inv, pf, 126.5, None, op0=ALU.is_lt))
            VL(lambda: v.tensor_tensor(cont, eqn, inv, ALU.mult))
            VL(lambda: v.tensor_scalar(key, Df[:, NC - 1:NC], 1.0, None, op0=ALU.add))
            VL(lambda: v.tensor_scalar(key, key, cont, -1.0, op0=ALU.mult, op1=ALU.add))
            VL(lambda: v.tensor_scalar(dg[:, 0, :], ident[:], key, None, op0=ALU.mult), c1)
            a = VL(lambda: v.tensor_scalar(dg[:, 1, :], ident[:], df_, None, op0=ALU.mult))
            b = em.T(lambda: t.matmul(PS[1][:, 0:2 * P], ones[:], dg.rearrange("p a b -> p (a b)"), start=True, stop=True), a)
            V(lambda: v.tensor_scalar(Cq[:], PS[1][:, P:2 * P], key, None, op0=ALU.is_equal), b)
            V(lambda: v.tensor_scalar(CTn[:], PS[1][:, 0:P], df_, None, op0=ALU.is_equal))
            V(lambda: v.tensor_scalar(En[:], PS[1][:, 0:P], key, None, op0=ALU.is_equal))
            VL(lambda: v.tensor_reduce(inv, CTn[:], AX, ALU.max))
            VL(lambda: v.tensor_scalar(CTn[:], CTn[:], -1.0, BIG, op0=ALU.add, op1=ALU.mult))
            VL(lambda: v.tensor_scalar(En[:], En[:], -1.0, BIG, op0=ALU.add, op1=ALU.mult))
            VL(lambda: v.tensor_scalar(scr2, Df, df_, None, op0=ALU.is_equal))
            VL(lambda: v.reduce_sum(eqc, scr2, AX))
            VL(lambda: v.tensor_scalar(pos, pf, float(NC), -1.0, op0=ALU.mult, op1=ALU.add))
            VL(lambda: v.tensor_tensor(pos, pos, eqc, ALU.add))
            VL(lambda: v.tensor_copy(fixg[:], pos))
            VL(lambda: v.tensor_scalar(eqc, eqc, float(NC) - 0.5, None, op0=ALU.is_gt))
            VL(lambda: v.tensor_tensor(eqc, eqc, cont, ALU.mult))
            VL(lambda: v.tensor_tensor(inv, inv, eqc, ALU.is_gt))
            VL(lambda: v.tensor_scalar(inv, inv, -SKIP, SKIP, op0=ALU.mult, op1=ALU.add))
            VL(lambda: v.tensor_tensor(pos, pos, inv, ALU.add))
            return VL(lambda: v.tensor_copy(fixs[:], pos))

        ohh = arena(17400, CH * 98 // 2).bitcast(BF16).rearrange("p (j a) -> p j a", j=CH)
        ohl = arena(18300, CH * 64 // 2).bitcast(BF16).rearrange("p (j a) -> p j a", j=CH)

        def hist(em, c, before):
            em.V(lambda: v.tensor_tensor(ohh, bc(dhi[:, c * CH:(c + 1) * CH].unsqueeze(2), [P, CH, 98]),
                                         bc(hi98.unsqueeze(1), [P, CH, 98]), ALU.is_equal), before, c3,
                 k_dl if em is main else em.last("dve"))
            a = em.V(lambda: v.tensor_tensor(ohl, bc(dlo[:, c * CH:(c + 1) * CH].unsqueeze(2), [P, CH, 64]),
                                             bc(lo64.unsqueeze(1), [P, CH, 64]), ALU.is_equal))
            for j in range(CH):
                b = em.T(lambda j=j: t.matmul(PS[0][0:98, 0:64], ohh[:, j, :], ohl[:, j, :],
                                              start=(c == 0 and j == 0), stop=(c == NCH - 1 and j == CH - 1)), a)
            return b

        def node_rows(em, before):
            VL, pre = em.VL, em.pre
            hsb = arena(19000, 64)
            a = em.V(lambda: v.tensor_copy(hsb[0:98, :], PS[0][0:98, 0:64]), before)
            b = ld(cntd.rearrange("(a b) -> a b", b=64), hsb[0:98, :], a, sem=pre + "cnt")
            b = ld(cntn[:], cntd.rearrange("(p l) -> p l", l=NL), b, sem=pre + "cnt")
            em.V(lambda: v.tensor_tensor_scan(incl[:], cntn[:], cntn[:], 0.0, ALU.add, ALU.bypass), b)
            a = VL(lambda: v.tensor_copy(sm[:, 11:12], incl[:, NL - 1:NL]))
            b = em.T(lambda: t.matmul(PS[1][:, 0:1], lower[:], sm[:, 11:12], start=True, stop=True), a, c2)
            VL(lambda: v.tensor_copy(sm[:, 12:13], PS[1][:, 0:1]), b)
            VL(lambda: v.tensor_scalar(incl[:], incl[:], sm[:, 12:13], None, op0=ALU.add))
            VL(lambda: v.tensor_scalar(nfl[:], cntn[:], 0.5, None, op0=ALU.is_gt))
            VL(lambda: v.tensor_tensor(cntn[:], incl[:], cntn[:], ALU.subtract))
            VL(lambda: v.tensor_scalar(incl[:], incl[:], -1.0 - EP, None, op0=ALU.add))
            VL(lambda: v.tensor_tensor(incl[:], incl[:], nfl[:], ALU.mult))
            VL(lambda: v.tensor_scalar(endi[:], incl[:], float(EP), None, op0=ALU.add))
            VL(lambda: v.tensor_scalar(nfl[:], nfl[:], -SKIP, SKIP, op0=ALU.mult, op1=ALU.add))
            return VL(lambda: v.tensor_tensor(stai[:], cntn[:], nfl[:], ALU.add))

        BRANCHING = ("vector", "tensor", "gpsimd", "sync")
        xdv = xd.rearrange("(p j) d -> p j d", j=NC)

        def exchange(em, which, rows, *before):
            for e_ in BRANCHING:
                Q.wait(e_, *before)
                Q.begin_if(e_, which)
            em.V(lambda: v.memset(e16t, 0.0))
            em.V(lambda: v.tensor_scalar(e8t, I3[:], 7, None, op0=ALU.bitwise_and))
            resort(em, True)
            flags(em)
            masks(em)
            b = None
            for c in range(NCH):
                b = hist(em, c, b)
            a = node_rows(em, b)
            k = em.V(lambda: v.memset(zt, 0.0), a)
            for c in range(NCH):
                z = ld(xdv[:, c * CH:(c + 1) * CH, :].rearrange("p j d -> p (j d)"), zt, k, sem=em.pre + "ld")
            for l in range(NL):
                z = scatter(xd, rows[:, l, :], stai[:, l:l + 1], EP - 1, k, z, sem=em.pre + "xs")
            for e_ in BRANCHING:
                Q.wait(e_, z)
            for e_ in BRANCHING:
                Q.end_if(e_)

        for e_ in BRANCHING:
            Q.wait(e_, k_flag)
            Q.begin_if(e_, flag[0:1, 0:1])
        resort(Em("f0"), False)
        for e_ in BRANCHING:
            Q.end_if(e_)
        k_i0 = V(lambda: v.scalar_tensor_tensor(out=I0, in0=Si[:], scalar=16.0, in1=e16t, op0=ALU.mult, op1=ALU.add))
        k_dl = k_bn = flags(main)

        xtt = arena(8000, 2, 512)
        ysb = arena(9024, 4, R0 * D)
        ydone, tfree = {}, {}
        tcount = {"b": 0, "y": 0, "k": 0}

        def turn(l0, n, banks, ready):
            u = tcount["b"]
            tcount["b"] += 1
            bnk = banks[u % len(banks)]
            for i in range(n):
                a = T(lambda i=i: t.transpose(PS[bnk][0:D, i * P:(i + 1) * P], X[:, l0 + i, :], ident[:]),
                      *ready, tfree.get(("t", bnk)))
            a = V(lambda: v.tensor_copy(xtt[0:D, u % 2, 0:n * P], PS[bnk][0:D, 0:n * P]), a, tfree.get(("x", u - 2)))
            tfree[("t", bnk)] = a
            return u, a

        def products(u, ev, l0, n, W, nrel, ytab, banks, engines):
            yv = ytab.rearrange("(p l r) d -> p l (r d)", l=NL, r=nrel)
            for i in range(n):
                k = tcount["k"]
                tcount["k"] += 1
                toks = []
                for o in range(0, nrel * D, 512):
                    y = tcount["y"]
                    tcount["y"] += 1
                    bnk = banks[y % len(banks)]
                    p = T(lambda i=i, o=o, bnk=bnk: t.matmul(PS[bnk][:], xtt[0:D, u % 2, i * P:(i + 1) * P], W[:, o:o + 512],
                                                             start=True, stop=True), ev, tfree.get(("y", bnk)))
                    to = ysb[:, k % 4, o:o + 512]
                    if engines[y % len(engines)] == "a":
                        q = A(lambda bnk=bnk, to=to: s.copy(to, PS[bnk][:]), p, ydone.get(k - 4))
                    else:
                        q = V(lambda bnk=bnk, to=to: v.tensor_copy(to, PS[bnk][:]), p, ydone.get(k - 4))
                    tfree[("y", bnk)] = q
                    toks.append(q)
                ydone[k] = ld(yv[:, l0 + i, :], ysb[:, k % 4, 0:nrel * D], *toks, sem=f"ysb{k % 4}")
            tfree[("x", u)] = p

        batches = [(l0, min(4, NL - l0)) for l0 in range(0, NL, 4)]
        nxt = turn(*batches[0], (2, 3), (l_x, l_w, c1))
        for n_, (l0, n) in enumerate(batches):
            cur = nxt
            if n_ + 1 < len(batches):
                nxt = turn(*batches[n_ + 1], (2, 3), ())
            products(*cur, l0, n, W0, R0, y0, (4, 5, 6, 7), "av")
        for c in range(NCH):
            l_z = ld(xdv[:, c * CH:(c + 1) * CH, :].rearrange("p j d -> p (j d)"), zt, k_z, sem="z")
        t_y0 = [ydone[k] for k in range(NL - 4, NL)]
        k_fix = masks(main)

        tA = arena(7000, H, D)
        V(lambda: v.tensor_tensor(tA, WLR[:].rearrange("p (h o) -> p h o", h=H), attb, ALU.mult), l_w)
        VL(lambda: v.memset(Vm[:], 0.0))
        VL(lambda: v.reduce_sum(Vm[:, 0:H], tA, AX))
        VL(lambda: v.tensor_scalar(Vm[:], Vm[:], 0.2, None, op0=ALU.mult))
        V(lambda: v.tensor_tensor(WS[:], WS[:], WLR[0:D, :], ALU.add))
        VL(lambda: v.tensor_tensor(tA[0:D], WS[:].rearrange("p (h o) -> p h o", h=H), attb[0:D], ALU.mult))
        VL(lambda: v.reduce_sum(Vs[:], tA[0:D], AX))
        VL(lambda: v.tensor_scalar(Vs[:], Vs[:], 0.2, None, op0=ALU.mult))
        VL(lambda: v.memset(A8[:], 0.0))
        for c in range(3):
            VL(lambda c=c: v.tensor_scalar(A8[0:D, c, 2 * c:2 * c + 1], att3[0:D, c:c + 1], 0.8, None, op0=ALU.mult))
            VL(lambda c=c: v.tensor_scalar(A8[D:P, c, 2 * c + 1:2 * c + 2], att3[D:P, c:c + 1], 0.8, None, op0=ALU.mult))
        for r in range(R3):
            V(lambda r=r: v.tensor_scalar(W3[:, r * D:(r + 1) * D], wb[:, 0, :], co[:, 2 * r:2 * r + 1], None, op0=ALU.mult))
            k_w = VL(lambda r=r: v.scalar_tensor_tensor(out=W3[:, r * D:(r + 1) * D], in0=wb[:, 1, :],
                                                        scalar=co[:, 2 * r + 1:2 * r + 2],
                                                        in1=W3[:, r * D:(r + 1) * D], op0=ALU.mult, op1=ALU.add))

        def chunk_view(st, c, w):
            return st[0:EP, :].rearrange("(p j) d -> p j d", j=NC)[:, c * CH:(c + 1) * CH, :].rearrange("p j d -> p (j d)")

        def linear_chunks(tab, idx, st, ready, side=None):
            NBUF = 4
            GB = arena(13200, NBUF, CH * D)
            stored, first = {}, {}
            last = None
            for c in range(NCH):
                b_ = c % NBUF
                buf = GB[:, b_, :].rearrange("p (j d) -> p j d", j=CH)
                prev = GB[:, (c - 1) % NBUF, :].rearrange("p (j d) -> p j d", j=CH)
                for j in range(CH):
                    tk = gather(buf[:, j, :], tab, idx[:, c * CH + j:c * CH + j + 1], *ready, stored.get(c - NBUF),
                                first.get(c - NBUF + 1), sem=f"g{b_}")
                if side is not None:
                    side(c)
                for j in range(CH):
                    if c == 0 and j == 0:
                        continue
                    pr = buf[:, j - 1, :] if j else prev[:, CH - 1, :]
                    last = VL(lambda c=c, j=j, pr=pr, buf=buf: v.scalar_tensor_tensor(
                        out=buf[:, j, :], in0=pr, scalar=gf[:, c * CH + j:c * CH + j + 1], in1=buf[:, j, :],
                        op0=ALU.mult, op1=ALU.add), tk, k_bn)
                    if j == 0:
                        first[c] = last
                stored[c] = ld(chunk_view(st, c, D), GB[:, b_, :], last, sem=f"s{b_}")
            return GB[:, (NCH - 1) % NBUF, (CH - 1) * D:CH * D], last, [stored[c] for c in range(NCH - NBUF, NCH)]

        HF = ((1999, 8), (1361, 9), (1733, 7), (1117, 10), (1871, 6), (1553, 9))
        HS = arena(20000, len(HF), NC).bitcast(I32)
        HD = arena(20000 + len(HF) * NC, len(HF), NC).bitcast(I32)
        hj = arena(30000, NC)
        acc = arena(30900, 32)
        pairs = [(a_, b_) for a_ in range(len(HF)) for b_ in range(a_)]
        twin = []
        for tile_, of in ((HS, Si), (HD, Dd)):
            for i, (m_, k_) in enumerate(HF):
                twin.append(lambda tile_=tile_, of=of, i=i, m_=m_: V(
                    lambda: v.tensor_scalar(tile_[:, i, :], of[:], float(m_), None, op0=ALU.mult)))
                twin.append(lambda tile_=tile_, i=i, k_=k_: VL(
                    lambda: v.tensor_scalar(tile_[:, i, :], tile_[:, i, :], k_, 7, op0=ALU.logical_shift_right,
                                            op1=ALU.bitwise_and)))
        for i, (a_, b_) in enumerate(pairs):
            for o_, (p_, q_) in ((i, (a_, b_)), (16 + i, (b_, a_))):
                twin.append(lambda o_=o_, p_=p_, q_=q_: VL(
                    lambda: v.scalar_tensor_tensor(out=hj, in0=HS[:, p_, :], scalar=1.0, in1=HD[:, q_, :], op0=ALU.mult,
                                                   op1=ALU.mult, accum_out=acc[:, o_:o_ + 1])))

        hist_pe = {}

        def side(c):
            hist_pe[c] = hist(main, c, hist_pe.get(c - 1))
            for _ in range(2):
                if twin:
                    twin.pop(0)()

        T0, k_t, st_t = linear_chunks(y0, I0, s0, [*t_y0, k_i0], side)
        npr = len(pairs)
        a = VL(lambda: v.tensor_tensor(acc[:, 0:npr], acc[:, 0:npr], acc[:, 16:16 + npr], ALU.subtract))
        b = T(lambda: t.matmul(PS[1][:, 0:npr], ones[:], acc[:, 0:npr], start=True, stop=True), a)
        V(lambda: v.tensor_copy(acc[:, 0:npr], PS[1][:, 0:npr]), b)
        VL(lambda: v.tensor_tensor(acc[:, 0:npr], acc[:, 0:npr], acc[:, 0:npr], ALU.mult))
        VL(lambda: v.tensor_reduce(sm[:, 13:14], acc[:, 0:npr], AX, ALU.max))
        VL(lambda: v.tensor_scalar(sm[:, 13:14], sm[:, 13:14], 0.5, None, op0=ALU.is_gt))
        k_twin = VL(lambda: v.tensor_copy(flag[:, 1:2], sm[:, 13:14]))
        k_node = node_rows(main, hist_pe[NCH - 1])

        def mend_linear(st, Tl, k_last, stored):
            fr = arena(19100, D)
            gt = gather(fr, st[:], fixg[:], *stored, k_fix, l_zr, sem="row")
            a = T(lambda: t.matmul(PS[2][:, 0:D], Cq[:], Tl, start=True, stop=True), k_last)
            b = VL(lambda: v.tensor_tensor(fr, fr, PS[2][:, 0:D], ALU.add), a, gt)
            return scatter(st[:], fr, fixs[:], EP - 1, b, sem="row")

        def norm(y, o, sq, mu, rs, *w):
            n = y.shape[1]
            sh = [P, n, D]
            V(lambda: v.reduce_sum(mu, y, AX), *w)
            VL(lambda: v.tensor_scalar(mu, mu, 1.0 / D, None, op0=ALU.mult))
            VL(lambda: v.tensor_tensor(y, y, bc(mu.unsqueeze(2), sh), ALU.subtract))
            VL(lambda: v.tensor_tensor(sq, y, y, ALU.mult))
            VL(lambda: v.reduce_sum(rs, sq, AX))
            a = VL(lambda: v.tensor_scalar(rs, rs, 1.0 / D, 1e-5, op0=ALU.mult, op1=ALU.add))
            a = A(lambda: s.sqrt(rs, rs), a)
            VL(lambda: v.reciprocal(rs, rs), a)
            return VL(lambda: v.tensor_tensor(o, y, bc(rs.unsqueeze(2), sh), ALU.mult))

        sq = arena(19300, GN, D)
        mu = arena(19800, GN)
        rs = arena(19820, GN)

        m0 = mend_linear(s0, T0, k_t, st_t)
        xts = arena(20000, NL, 65)
        zz = R
        NG0 = arena(23400, 2, GN * D)
        used = {}
        sc_done = None
        for q in range(NG):
            nb = NG0[:, q % 2, :].rearrange("p (l d) -> p l d", l=GN)
            sl = slice(q * GN, (q + 1) * GN)
            for i in range(GN):
                tk = gather(nb[:, i, :], s0[:], endi[:, q * GN + i:q * GN + i + 1], m0, k_node, used.get(q - 2), sem=f"n{q % 2}")
            VL(lambda nb=nb, sl=sl: v.tensor_tensor(nb, nb, X[:, sl, :], ALU.add), tk)
            k = norm(nb, X[:, sl, :], sq, mu, rs, ("dve", Q.value["dve"]))
            used[q] = k
            VL(lambda sl=sl: v.tensor_tensor(sq, X[:, sl, :], X[:, sl, :], ALU.mult))
            VL(lambda: v.reduce_sum(rs, sq, AX))
            a = VL(lambda: v.tensor_scalar(rs, rs, 1e-8, None, op0=ALU.add))
            a = A(lambda: s.sqrt(rs, rs), a)
            VL(lambda: v.reciprocal(rs, rs), a)
            VL(lambda sl=sl: v.tensor_copy(xts[:, sl, 0:D], X[:, sl, :]))
            a = VL(lambda sl=sl: v.tensor_copy(xts[:, sl, D], rs))
            VL(lambda: v.tensor_scalar(mu, rs, bet[:], None, op0=ALU.mult))
            b = VL(lambda sl=sl: v.tensor_tensor(zz[:, sl, :], X[:, sl, :], bc(mu.unsqueeze(2), [P, GN, D]), ALU.mult))
            xw = ld(xt1.rearrange("(p l) d -> p l d", l=NL)[:, sl, :].rearrange("p l d -> p (l d)"),
                    xts[:, sl, :].rearrange("p l d -> p (l d)"), a, sem="xt")
            for l in range(q * GN, (q + 1) * GN):
                sc_done = scatter(xd, zz[:, l, :], stai[:, l:l + 1], EP - 1, b, l_z, sem="sc")
        k_end = ("dve", Q.value["dve"])

        def now():
            return [(n_, Q.value[n_]) for n_ in ("dve", "act", "pe")]

        exchange(Em("f1"), flag[0:1, 1:2], zz, *now(), xw, sc_done)

        def fence(*toks):
            for e_ in Queues.ENGINES:
                Q.wait(e_, *toks)

        fence(k_end)

        def merged(*lists):
            total = max(len(x_) for x_ in lists)
            at = [0] * len(lists)
            for i in range(total):
                for k_, x_ in enumerate(lists):
                    while at[k_] * total < (i + 1) * len(x_):
                        x_[at[k_]]()
                        at[k_] += 1

        G1 = arena(0, 4, CH * 65)
        XB1 = arena(4200, 3, CH * D)
        XF1 = arena(7300, 2, CH * D)
        TM1 = arena(9400, CH, D)
        S1 = arena(10500, 3, CH * 66)
        e1, m1 = arena(13700, CH), arena(13720, CH)
        mf1 = arena(13740, CH)
        pf1 = arena(13760, 2, CH + 1)
        xi1 = arena(13800, 65)
        gi = gather(xi1, xt1, Dd[:, 0:1], xw, k_end, sem="xdi")
        k_g, k_xb, freeG, freeXB, freeXF, stored, pxd = {}, {}, {}, {}, {}, {}, {}
        k_fill = {}

        def g1(c):
            for j in range(CH):
                k_g[c] = gather(G1[:, c % 4, j * 65:(j + 1) * 65], xt1, Si[:, c * CH + j:c * CH + j + 1],
                                xw, freeG.get(c - 4), sem=f"g{c % 4}")

        def xb(c, XB, free, ready):
            k_xb[c] = ld(XB[:, c % XBN, :], xdv[:, c * CH:(c + 1) * CH, :].rearrange("p j d -> p (j d)"),
                         ready, free.get(c - XBN), sem=f"x{c % XBN}")

        XBN = 3

        def fills1(c):
            ops = []
            XBv = XB1[:, c % 3, :].rearrange("p (j d) -> p j d", j=CH)
            XFv = XF1[:, c % 2, :].rearrange("p (j d) -> p j d", j=CH)
            XFp = XF1[:, (c - 1) % 2, :].rearrange("p (j d) -> p j d", j=CH)
            mine = [None]

            def one(j):
                if c == 0 and j == 0:
                    def f():
                        V(lambda: v.tensor_scalar(mu[:, 0:1], xi1[:, 64:65], bet[:], None, op0=ALU.mult), gi)
                        mine[0] = VL(lambda: v.tensor_scalar(XFv[:, 0, :], xi1[:, 0:D], mu[:, 0:1], None, op0=ALU.mult))
                    return f
                pr = XFv[:, j - 1, :] if j else XFp[:, CH - 1, :]

                def f():
                    mine[0] = V(lambda: v.scalar_tensor_tensor(
                        out=XFv[:, j, :], in0=pr, scalar=gf[:, c * CH + j:c * CH + j + 1], in1=XBv[:, j, :],
                        op0=ALU.mult, op1=ALU.add), k_xb[c], mine[0] or k_fill.get(c - 1), freeXF.get(c - 2))
                    k_fill[c] = mine[0]
                    freeXB[c] = mine[0]
                return f
            return [one(j) for j in range(CH)]

        def soft1(c):
            Gv = G1[:, c % 4, :].rearrange("p (j d) -> p j d", j=CH)
            XFv = XF1[:, c % 2, :].rearrange("p (j d) -> p j d", j=CH)
            Sv = S1[:, c % 3, :].rearrange("p (j d) -> p j d", j=CH)
            Sp = S1[:, (c - 1) % 3, :].rearrange("p (j d) -> p j d", j=CH)
            pe_ = pf1[:, c % 2, :]
            mine = [None]

            def L(fn, *w):
                def f():
                    mine[0] = V(fn, mine[0] or k_fill[c], *w)
                return f

            def at_dot():
                freeXF[c] = V(lambda: v.tensor_tensor(TM1, Gv[:, :, 0:D], XFv, ALU.mult), k_fill[c], k_g[c])
                mine[0] = freeXF[c]
            ops = [at_dot,
                   L(lambda: v.reduce_sum(e1, TM1, AX)),
                   L(lambda: v.tensor_tensor(e1, e1, Gv[:, :, D], ALU.mult)),
                   L(lambda: v.tensor_tensor_scan(mf1, Bn[:, c * CH:(c + 1) * CH], e1,
                                                  Sp[:, CH - 1, 65:66] if c else -BIG, ALU.add, ALU.max)),
                   L(lambda: v.tensor_tensor_scan(m1[:, ::-1], Bn[:, c * CH + 1:(c + 1) * CH + 1][:, ::-1], mf1[:, ::-1],
                                                  -BIG, ALU.add, ALU.max)),
                   L(lambda: v.tensor_tensor(pe_[:, 0:CH], e1, m1, ALU.subtract))]
            if c:
                ops.append(L(lambda: v.scalar_tensor_tensor(out=pe_[:, CH:CH + 1], in0=Sp[:, CH - 1, 65:66],
                                                            scalar=Bn[:, c * CH:c * CH + 1], in1=m1[:, 0:1],
                                                            op0=ALU.add, op1=ALU.subtract)))
            n_ = CH + 1 if c else CH

            def ex():
                pxd[c] = A(lambda: s.activation(pe_[:, 0:n_], pe_[:, 0:n_], ACT.Exp), mine[0])
            ops.append(ex)
            ops.append(L(lambda: v.tensor_copy(Sv[:, :, 65], m1), stored.get(c - 3)))
            return ops

        def px1(c):
            Gv = G1[:, c % 4, :].rearrange("p (j d) -> p j d", j=CH)
            Sv = S1[:, c % 3, :].rearrange("p (j d) -> p j d", j=CH)
            pe_ = pf1[:, c % 2, 0:CH]
            V(lambda: v.tensor_tensor(Sv[:, :, 0:D], Gv[:, :, 0:D], bc(pe_.unsqueeze(2), [P, CH, D]), ALU.mult),
              pxd[c], stored.get(c - 3))
            freeG[c] = V(lambda: v.tensor_copy(Sv[:, :, D], pe_))

        k_step = {}

        def steps1(c):
            Sv = S1[:, c % 3, :].rearrange("p (j d) -> p j d", j=CH)
            Sp = S1[:, (c - 1) % 3, :].rearrange("p (j d) -> p j d", j=CH)
            mine = [None]

            def one(j):
                if c == 0 and j == 0:
                    return lambda: None
                pr = Sv[:, j - 1, 0:65] if j else Sp[:, CH - 1, 0:65]
                sc_ = gf[:, c * CH + j:c * CH + j + 1] if j else pf1[:, c % 2, CH:CH + 1]

                def f():
                    mine[0] = V(lambda: v.scalar_tensor_tensor(out=Sv[:, j, 0:65], in0=pr, scalar=sc_, in1=Sv[:, j, 0:65],
                                                               op0=ALU.mult, op1=ALU.add),
                                mine[0] or freeG[c], k_step.get(c - 1))
                    k_step[c] = mine[0]
                return f
            return [one(j) for j in range(CH)]

        for c in range(3):
            xb(c, XB1, freeXB, sc_done)
        g1(0)
        g1(1)
        merged(fills1(0))
        merged(soft1(0))
        px1(0)
        merged(fills1(1))
        for c in range(NCH):
            if c + 2 < NCH:
                g1(c + 2)
            if c + 3 < NCH:
                xb(c + 3, XB1, freeXB, sc_done)
            B_ = []
            if c + 1 < NCH:
                B_ += soft1(c + 1)
            if c + 2 < NCH:
                B_ += fills1(c + 2)
            merged(steps1(c), B_)
            stored[c] = ld(chunk_view(s1, c, 66), S1[:, c % 3, :], k_step[c], sem=f"s{c % 3}")
            if c + 1 < NCH:
                px1(c + 1)
        st_t = [stored[c] for c in range(NCH - 3, NCH)]
        T1 = S1[:, (NCH - 1) % 3, :].rearrange("p (j d) -> p j d", j=CH)[:, CH - 1, :]

        def mend_soft(st, Tl, heads, k_last, stored_, base):
            aw = heads * 65
            o = base

            def take(*shape):
                nonlocal o
                n = 1
                for k_ in shape:
                    n *= k_
                a_ = arena(o, *shape)
                o += n
                return a_
            fr = take(aw + heads)
            dgm, mk = take(heads, P), take(heads, P)
            Ts, mseg, mc = take(aw), take(heads), take(heads)
            Mx, w1, w2 = take(heads), take(heads), take(heads)
            gt = gather(fr, st[:], fixg[:], *stored_, k_fix, l_zr, sem="row")
            ml = Tl[:, aw:aw + heads]
            a = None
            for h in range(heads):
                a = V(lambda h=h: v.tensor_scalar(dgm[:, h, :], ident[:], ml[:, h:h + 1], None, op0=ALU.mult), k_last)
            nb = (heads + 2) // 3
            for i in range(nb):
                k_ = min(3, heads - 3 * i)
                b = T(lambda i=i, k_=k_: t.matmul(PS[i][:, 0:k_ * P], ones[:],
                                                  dgm[:, 3 * i:3 * i + k_, :].rearrange("p a b -> p (a b)"),
                                                  start=True, stop=True), a)
            for msk, res in ((En, mseg), (CTn, mc)):
                for i in range(nb):
                    k_ = min(3, heads - 3 * i)
                    V(lambda i=i, k_=k_, msk=msk: v.tensor_tensor(
                        mk[:, 3 * i:3 * i + k_, :], PS[i][:, 0:k_ * P].rearrange("p (a b) -> p a b", b=P),
                        bc(msk[:].unsqueeze(1), [P, k_, P]), ALU.add), b, ("dve", Q.value["dve"]))
                VL(lambda res=res: v.tensor_reduce(res, mk, AX, ALU.max))
            a = VL(lambda: v.tensor_tensor(mseg, ml, mseg, ALU.subtract))
            a = A(lambda: s.activation(mseg, mseg, ACT.Exp), a)
            Tv = Tl[:, 0:aw].rearrange("p (h d) -> p h d", h=heads)
            a = V(lambda: v.tensor_tensor(Ts.rearrange("p (h d) -> p h d", h=heads), Tv,
                                          bc(mseg.unsqueeze(2), [P, heads, 65]), ALU.mult), a)
            b = T(lambda: t.matmul(PS[2][:, 0:aw], Cq[:], Ts, start=True, stop=True), a)
            mr = fr[:, aw:aw + heads]
            V(lambda: v.tensor_tensor(Mx, mr, mc, ALU.max), gt, a)
            VL(lambda: v.tensor_tensor(w1, mr, Mx, ALU.subtract))
            a = V(lambda: v.tensor_tensor(w2, mc, Mx, ALU.subtract))
            A(lambda: s.activation(w1, w1, ACT.Exp), a)
            a = A(lambda: s.activation(w2, w2, ACT.Exp))
            frv = fr[:, 0:aw].rearrange("p (h d) -> p h d", h=heads)
            tv = Ts.rearrange("p (h d) -> p h d", h=heads)
            V(lambda: v.tensor_tensor(frv, frv, bc(w1.unsqueeze(2), [P, heads, 65]), ALU.mult), a)
            V(lambda: v.tensor_tensor(tv, PS[2][:, 0:aw].rearrange("p (h d) -> p h d", h=heads),
                                      bc(w2.unsqueeze(2), [P, heads, 65]), ALU.mult), b)
            VL(lambda: v.tensor_tensor(frv, frv, tv, ALU.add))
            a = VL(lambda: v.tensor_copy(mr, Mx))
            return scatter(st[:], fr, fixs[:], EP - 1, a, sem="row")

        m1_ = mend_soft(s1, T1, 1, k_step[NCH - 1], st_t, 14000)

        NG1 = arena(23400, 2, GN * 66)
        den = arena(24400, GN)
        xq = arena(24420, 2, 512)
        rl = arena(25500, 3, 512)
        used, ps_free, xq_free, rl_free = {}, {}, {}, {}
        zz2 = X
        xcols = 0
        for q in range(NG):
            nb = NG1[:, q % 2, :].rearrange("p (l d) -> p l d", l=GN)
            sl = slice(q * GN, (q + 1) * GN)
            for i in range(GN):
                tk = gather(nb[:, i, :], s1[:], endi[:, q * GN + i:q * GN + i + 1], m1_, used.get(q - 2), sem=f"n{q % 2}")
            V(lambda nb=nb: v.tensor_scalar(den, nb[:, :, D], 1e-16, None, op0=ALU.max), tk, ("dve", Q.value["dve"]))
            VL(lambda: v.reciprocal(den, den))
            VL(lambda nb=nb: v.tensor_tensor(nb[:, :, 0:D], nb[:, :, 0:D], bc(den.unsqueeze(2), [P, GN, D]), ALU.mult))
            VL(lambda nb=nb, sl=sl: v.tensor_tensor(nb[:, :, 0:D], nb[:, :, 0:D], X[:, sl, :], ALU.add))
            used[q] = k = norm(nb[:, :, 0:D], X[:, sl, :], sq, mu, rs, ("dve", Q.value["dve"]))
            xw = ld(xt2.rearrange("(p l) d -> p l d", l=NL)[:, sl, :].rearrange("p l d -> p (l d)"),
                    X[:, sl, :].rearrange("p l d -> p (l d)"), k, sem="xt")
            for l in range(q * GN, (q + 1) * GN):
                sc_done = scatter(xd, X[:, l, :], stai[:, l:l + 1], EP - 1, k, *[k_xb[c] for c in range(NCH - 3, NCH)], sem="sc")
            for l0 in range(q * GN, (q + 1) * GN, 4):
                nl_ = min(4, (q + 1) * GN - l0)
                u = xcols
                xcols += 1
                for i in range(nl_):
                    a = T(lambda i=i, l0=l0, u=u: t.transpose(PS[u % 2][0:D, i * P:(i + 1) * P], X[:, l0 + i, :], ident[:]),
                          k, ps_free.get(("t", u - 2)))
                w_ = nl_ * P
                a = V(lambda u=u, w_=w_: v.tensor_copy(xq[0:D, u % 2, 0:w_], PS[u % 2][0:D, 0:w_]), a, xq_free.get(u - 2))
                ps_free[("t", u)] = a
                for ch in range(3):
                    b = T(lambda ch=ch, u=u, w_=w_: t.matmul(PS[2 + ch][:, 0:w_], WS[:, ch * P:(ch + 1) * P],
                                                            xq[0:D, u % 2, 0:w_], start=True, stop=True),
                          a, ps_free.get(("z", ch)))
                    ps_free[("z", ch)] = A(lambda ch=ch, w_=w_: s.activation(rl[:, ch, 0:w_], PS[2 + ch][:, 0:w_], ACT.Relu),
                                           b, rl_free.get(u - 1))
                for i in range(nl_):
                    for ch in range(3):
                        T(lambda i=i, ch=ch: t.matmul(PS[5][:, i * H:(i + 1) * H], rl[:, ch, i * P:(i + 1) * P], A8[:, ch, 0:H],
                                                      start=(ch == 0), stop=False), ps_free[("z", 2)], ps_free.get("e"))
                    b = T(lambda i=i, u=u: t.matmul(PS[5][:, i * H:(i + 1) * H], xq[0:D, u % 2, i * P:(i + 1) * P], Vs[:],
                                                    start=False, stop=True))
                xq_free[u] = rl_free[u] = b
                ps_free["e"] = V(lambda l0=l0, nl_=nl_: v.tensor_copy(
                    es[:, l0:l0 + nl_, :], PS[5][:, 0:nl_ * H].rearrange("p (l h) -> p l h", h=H)), b)
        k_end = ("dve", Q.value["dve"])
        fence(k_end, ("act", Q.value["act"]), ("pe", Q.value["pe"]))
        exchange(Em("f2"), flag[0:1, 1:2], X, *now(), xw, sc_done)

        NX = 5
        XBN = 3
        XS = arena(0, NX, CH * P)
        XB2 = arena(10240, XBN, CH * D)
        S2 = arena(13312, 2, CH * RW)
        XT2 = arena(25984, 6, 512)
        RL2 = arena(29056, 5, 3 * 512)
        eb = arena(36736, H, CH)
        mf2 = arena(36832, H, CH)
        mb2 = arena(36928, H, CH)
        Bf = arena(37024, H, CH)
        Bb = arena(37120, H, CH)
        pf2 = arena(37216, 2, H * (CH + 1))
        tmp2 = arena(37420, H, 65)
        ETs = arena(37810, 512)
        stored, k_step, k_xb, freeXB, k_fill, k_g, pxd = {}, {}, {}, {}, {}, {}, {}
        freeXS, k_E, k_px, k_pa, k_step0 = {}, {}, {}, {}, {}
        V(lambda: v.memset(Bf, -BIG))
        V(lambda: v.memset(Bb, -BIG))

        HV = 4
        freeXA = {}

        def xsv(c):
            return XS[:, c % NX, :].rearrange("p (j d) -> p j d", j=CH)

        gi = gather(xsv(0)[:, 0, D:P], xt2, Dd[:, 0:1], xw, sem="xdi")

        def g2(c):
            for j in range(CH):
                k_g[c] = gather(xsv(c)[:, j, 0:D], xt2, Si[:, c * CH + j:c * CH + j + 1], xw,
                                freeXS.get(c - NX), freeXA.get(c - NX), sem=f"g{c % NX}")

        def fills2(c):
            XBv = XB2[:, c % XBN, :].rearrange("p (j d) -> p j d", j=CH)
            cur, prv = xsv(c), xsv(c - 1)
            mine = [None]

            def one(j):
                if c == 0 and j == 0:
                    return lambda: None
                pr = cur[:, j - 1, D:P] if j else prv[:, CH - 1, D:P]

                def f():
                    mine[0] = V(lambda: v.scalar_tensor_tensor(
                        out=cur[:, j, D:P], in0=pr, scalar=gf[:, c * CH + j:c * CH + j + 1], in1=XBv[:, j, :],
                        op0=ALU.mult, op1=ALU.add), k_xb[c], mine[0] or k_fill.get(c - 1), gi, freeXS.get(c - NX), freeXA.get(c - NX))
                    k_fill[c] = freeXB[c] = mine[0]
                return f
            return [one(j) for j in range(CH)]

        evT, relu, etok, et_ev, e_read = {}, {}, {}, {}, {}
        NGR = CH // 4

        def pe_t(u):
            c, q = divmod(u, NGR)
            for i in range(4):
                a = T(lambda i=i: t.transpose(PS[u % 2][:, i * P:(i + 1) * P], xsv(c)[:, 4 * q + i, :], ident[:]),
                      k_g[c], k_fill[c], evT.get(u - 2))
            evT[u] = A(lambda: s.copy(XT2[:, u % 6, :], PS[u % 2][:]), a, etok.get((u - 6) // NGR))

        def pe_m(u, ch):
            bnk = 2 + (3 * u + ch) % 4
            a = T(lambda: t.matmul(PS[bnk][:], WLR[:, ch * P:(ch + 1) * P], XT2[:, u % 6, :], start=True, stop=True),
                  evT[u], relu.get(3 * u + ch - 4))
            relu[3 * u + ch] = A(lambda: s.activation(RL2[:, u % 5, ch * 512:(ch + 1) * 512], PS[bnk][:], ACT.Relu),
                                 a, etok.get((u - 5) // NGR))

        def pe_e(c):
            for ch in range(4):
                for q in range(NGR):
                    u = c * NGR + q
                    if ch < 3:
                        w_, m_ = A8[:, ch, :], RL2[:, u % 5, ch * 512:(ch + 1) * 512]
                    else:
                        w_, m_ = Vm[:], XT2[:, u % 6, :]
                    a = T(lambda ch=ch, q=q, w_=w_, m_=m_: t.matmul(PS[6][32 * q:32 * q + 32, :], w_, m_, start=(ch == 0),
                                                                    stop=(ch == 3)), relu[3 * u + 2], et_ev.get(c - 1))
            etok[c] = a
            et_ev[c] = A(lambda: s.copy(ETs, PS[6][:]), a, k_E.get(c - 1))

        def pe_f(c):
            for i in range(4):
                a = T(lambda i=i: t.transpose(PS[7][:, i * P:(i + 1) * P], ETs[:, i * P:(i + 1) * P], ident[:]),
                      et_ev[c], e_read.get(c - 1))
            k_E[c] = a

        def pe_ops(c):
            ops = []
            for q in range(NGR):
                u = c * NGR + q
                ops.append(lambda u=u: pe_t(u))
                if u == 0:
                    continue
                ops += [lambda u=u, ch=ch: pe_m(u - 1, ch) for ch in range(3)]
                if c and q == 1:
                    ops.append(lambda: pe_e(c - 1))
                if c and q == 2:
                    ops.append(lambda: pe_f(c - 1))
            return ops

        def pe_last():
            for ch in range(3):
                pe_m(NCH * NGR - 1, ch)
            pe_e(NCH - 1)
            pe_f(NCH - 1)

        def soft2(c):
            ep = PS[7][:].rearrange("p (i q x) -> p x q i", i=4, q=4)[:, 0:H]
            Sv = S2[:, c % 2, :].rearrange("p (j d) -> p j d", j=CH)
            Sp = S2[:, (c - 1) % 2, :].rearrange("p (j d) -> p j d", j=CH)
            pe_ = pf2[:, c % 2, 0:H * CH].rearrange("p (h j) -> p h j", h=H)
            pq = pf2[:, c % 2, H * CH:H * CH + H]
            mine = [None]
            fl = lambda a_: a_.rearrange("p h j -> p (h j)")

            def L(fn, *w):
                def f():
                    mine[0] = V(fn, mine[0], *w)
                return f

            def first():
                mine[0] = V(lambda: v.tensor_copy(eb.rearrange("p h (q i) -> p h q i", q=4), ep), k_E[c])
            ops = [first,
                   lambda: V(lambda: v.tensor_copy(Bf[:, :, 1:CH], bc(Bn[:, c * CH + 1:(c + 1) * CH].unsqueeze(1), [P, H, CH - 1])),
                             ("dve", Q.value["dve"])),
                   L(lambda: v.tensor_copy(Bb[:, :, 0:CH - 1], bc(Bn[:, c * CH + 1:(c + 1) * CH].unsqueeze(1), [P, H, CH - 1])))]
            if c:
                ops.append(L(lambda: v.scalar_tensor_tensor(out=eb[:, :, 0], in0=Sp[:, CH - 1, HW:], scalar=Bn[:, c * CH:c * CH + 1],
                                                            in1=eb[:, :, 0], op0=ALU.add, op1=ALU.max)))
            ops += [L(lambda: v.tensor_tensor_scan(fl(mf2), fl(Bf), fl(eb), -BIG, ALU.add, ALU.max)),
                    L(lambda: v.tensor_tensor_scan(fl(mb2)[:, ::-1], fl(Bb)[:, ::-1], fl(mf2)[:, ::-1], -BIG, ALU.add, ALU.max)),
                    L(lambda: v.tensor_tensor(pe_.rearrange("p h (q i) -> p h q i", q=4), ep,
                                              mb2.rearrange("p h (q i) -> p h q i", q=4), ALU.subtract))]

            def note():
                e_read[c] = mine[0]
            ops.append(note)
            if c:
                ops.append(L(lambda: v.scalar_tensor_tensor(out=pq, in0=Sp[:, CH - 1, HW:], scalar=Bn[:, c * CH:c * CH + 1],
                                                            in1=mb2[:, :, 0], op0=ALU.add, op1=ALU.subtract)))
            n_ = H * (CH + 1) if c else H * CH

            def ex():
                pxd[c] = A(lambda: s.activation(pf2[:, c % 2, 0:n_], pf2[:, c % 2, 0:n_], ACT.Exp), mine[0])
            ops.append(ex)
            ops.append(L(lambda: v.tensor_copy(Sv[:, :, HW:].rearrange("p j h -> p h j"), mb2), stored.get(c - 2), k_step.get(c - 1)))
            return ops

        def px2(c):
            Sv = S2[:, c % 2, :].rearrange("p (j d) -> p j d", j=CH)
            pe_ = pf2[:, c % 2, 0:H * CH].rearrange("p (h j) -> p h j", h=H)
            for h in range(HV):
                V(lambda h=h: v.tensor_tensor(Sv[:, :, h * 65:h * 65 + D], xsv(c)[:, :, 0:D],
                                              bc(pe_[:, h, :].unsqueeze(2), [P, CH, D]), ALU.mult), pxd[c], stored.get(c - 2),
                  k_step.get(c - 1))
            k_px[c] = V(lambda: v.tensor_copy(
                Sv[:, :, 0:HW].rearrange("p j (h d) -> p j h d", h=H)[:, :, :, D].rearrange("p j h -> p h j"), pe_))
            freeXS[c] = k_px[c]

        def px2_act(c):
            Sv = S2[:, c % 2, :].rearrange("p (j d) -> p j d", j=CH)
            pe_ = pf2[:, c % 2, 0:H * CH].rearrange("p (h j) -> p h j", h=H)

            def one(j, h):
                def f():
                    k_pa[(c, j)] = freeXA[c] = A(
                        lambda: s.activation(Sv[:, j, h * 65:h * 65 + D], xsv(c)[:, j, 0:D], ACT.Copy,
                                             scale=pe_[:, h, j:j + 1]), pxd[c], stored.get(c - 2), k_step0.get(c - 1))
                return f
            return [one(j, h) for j in range(CH) for h in range(HV, H)]

        def steps2(c):
            Sv = S2[:, c % 2, :].rearrange("p (j d) -> p j d", j=CH)
            Sp = S2[:, (c - 1) % 2, :].rearrange("p (j d) -> p j d", j=CH)
            pq = pf2[:, c % 2, H * CH:H * CH + H]
            mine = [None]

            def one(j):
                if c == 0 and j == 0:
                    return lambda: None
                if j == 0:
                    def f():
                        a = V(lambda: v.tensor_tensor(tmp2, Sp[:, CH - 1, 0:HW].rearrange("p (h d) -> p h d", h=H),
                                                      bc(pq.unsqueeze(2), [P, H, 65]), ALU.mult), k_px[c], k_step.get(c - 1))
                        k_step0[c] = a
                        mine[0] = V(lambda: v.tensor_tensor(Sv[:, 0, 0:HW], Sv[:, 0, 0:HW], tmp2.rearrange("p h d -> p (h d)"),
                                                            ALU.add), a, k_pa[(c, 0)])
                    return f

                def f():
                    mine[0] = V(lambda: v.scalar_tensor_tensor(
                        out=Sv[:, j, 0:HW], in0=Sv[:, j - 1, 0:HW], scalar=gf[:, c * CH + j:c * CH + j + 1],
                        in1=Sv[:, j, 0:HW], op0=ALU.mult, op1=ALU.add), mine[0] or k_px[c], k_pa[(c, j)], k_pa[(c, 0)])
                    k_step[c] = mine[0]
                return f
            return [one(j) for j in range(CH)]

        for c in range(XBN):
            xb(c, XB2, freeXB, sc_done)
        for c in range(3):
            g2(c)
            merged(fills2(c))
        xb(3, XB2, freeXB, sc_done)
        merged(pe_ops(0))
        merged(pe_ops(1))
        merged(soft2(0))
        px2(0)
        merged(pe_ops(2), px2_act(0))
        for c in range(NCH):
            if c + 3 < NCH:
                g2(c + 3)
            B_ = []
            if c + 3 < NCH:
                B_ += fills2(c + 3)
            if c + 1 < NCH:
                B_ += soft2(c + 1)
            merged(steps2(c), B_)
            if c + 4 < NCH:
                xb(c + 4, XB2, freeXB, sc_done)
            stored[c] = ld(chunk_view(s2, c, RW), S2[:, c % 2, :], k_step[c], sem=f"s{c % 2}")
            if c + 1 < NCH:
                px2(c + 1)
                merged(pe_ops(c + 3) if c + 3 < NCH else [], px2_act(c + 1))
            if c == NCH - 3:
                pe_last()
        st_t = [stored[c] for c in range(NCH - 2, NCH)]
        T2 = S2[:, (NCH - 1) % 2, :].rearrange("p (j d) -> p j d", j=CH)[:, CH - 1, :]
        m2_ = mend_soft(s2, T2, H, k_step[NCH - 1], st_t, 0)
        fence(("pe", Q.value["pe"]), ("act", Q.value["act"]))
        k_m2 = ("dve", Q.value["dve"])

        N2 = arena(13312, 2, GN * RW)
        U = arena(20200, 2, GN * H * D)
        UT = arena(25600, 3 * GN * P)
        TU = arena(28400, GN, H * D)
        wv = arena(31100, 6, GN * H)
        O2 = arena(31400, 2, GN * D)
        O3 = arena(32300, GN, D)
        LAM, ALP = 1.0507009873554805, 1.6732632423543772
        used, uf, k_u, k_o, k_n = {}, {}, {}, {}, {}

        def gathered(q):
            nb = N2[:, q % 2, :].rearrange("p (l d) -> p l d", l=GN)
            for i in range(GN):
                used[("g", q)] = gather(nb[:, i, :], s2[:], endi[:, q * GN + i:q * GN + i + 1], m2_, k_m2,
                                        used.get(q - 2), sem=f"n{q % 2}")

        def weighted(q):
            nb = N2[:, q % 2, :].rearrange("p (l d) -> p l d", l=GN)
            sl = slice(q * GN, (q + 1) * GN)
            mm, w1, w3_, dd = (wv[:, i, :].rearrange("p (l h) -> p l h", h=H) for i in range(4))
            nv = nb[:, :, 0:HW].rearrange("p l (h d) -> p l h d", h=H)
            Uv = U[:, q % 2, :].rearrange("p (l h d) -> p l h d", l=GN, h=H)
            Tv = TU.rearrange("p l (h d) -> p l h d", h=H)
            sh = [P, GN, H, D]
            V(lambda: v.tensor_tensor(mm, nb[:, :, HW:], es[:, sl, :], ALU.max), used[("g", q)], main.last("dve"))
            VL(lambda: v.tensor_tensor(w1, nb[:, :, HW:], mm, ALU.subtract))
            a = V(lambda: v.tensor_tensor(w3_, es[:, sl, :], mm, ALU.subtract))
            A(lambda: s.activation(w1, w1, ACT.Exp), a)
            a = A(lambda: s.activation(w3_, w3_, ACT.Exp))
            V(lambda: v.tensor_tensor(dd, nv[:, :, :, D], w1, ALU.mult), a)
            VL(lambda: v.tensor_tensor(dd, dd, w3_, ALU.add))
            VL(lambda: v.tensor_scalar(dd, dd, 1e-16, float(H), op0=ALU.add, op1=ALU.mult))
            VL(lambda: v.reciprocal(dd, dd))
            VL(lambda: v.tensor_tensor(w1, w1, dd, ALU.mult))
            V(lambda: v.tensor_tensor(w3_, w3_, dd, ALU.mult))
            used[q] = VL(lambda: v.tensor_tensor(Uv, nv[:, :, :, 0:D], bc(w1.unsqueeze(3), sh), ALU.mult), uf.get(("U", q - 2)))
            V(lambda: v.tensor_tensor(Tv, bc(X[:, sl, :].unsqueeze(2), sh), bc(w3_.unsqueeze(3), sh), ALU.mult))
            k_u[q] = VL(lambda: v.tensor_tensor(U[:, q % 2, :], U[:, q % 2, :], TU.rearrange("p l d -> p (l d)"), ALU.add))

        def projected(q):
            blocks = 3 * GN
            ev = {}
            for n_, b0 in enumerate(range(0, blocks, 4)):
                bn = min(4, blocks - b0)
                for i in range(bn):
                    a = T(lambda i=i, b0=b0, n_=n_: t.transpose(PS[n_ % 2][:, i * P:(i + 1) * P],
                                                                U[:, q % 2, (b0 + i) * P:(b0 + i + 1) * P], ident[:]),
                          k_u[q], uf.get(("b", n_ % 2)))
                e_ = A(lambda b0=b0, bn=bn, n_=n_: s.copy(UT[:, b0 * P:(b0 + bn) * P], PS[n_ % 2][:, 0:bn * P]), a,
                       uf.get(("UT", q - 1)))
                uf[("b", n_ % 2)] = e_
                for i in range(bn):
                    ev[b0 + i] = e_
            uf[("U", q)] = a
            for l in range(GN):
                for ch in range(3):
                    k_ = 3 * l + ch
                    b = T(lambda l=l, ch=ch, k_=k_: t.matmul(PS[2][:, l * D:(l + 1) * D], UT[:, k_ * P:(k_ + 1) * P],
                                                             W2[:, ch, :], start=(ch == 0), stop=(ch == 2)),
                          ev[k_], uf.get("o"))
            uf[("UT", q)] = k_o[q] = b

        def finished(q):
            sl = slice(q * GN, (q + 1) * GN)
            o2 = O2[:, q % 2, :].rearrange("p (l d) -> p l d", l=GN)
            ps2 = PS[2][:, 0:GN * D].rearrange("p (l d) -> p l d", d=D)
            uf["o"] = V(lambda: v.tensor_tensor(o2, ps2, bc(b2[:].unsqueeze(1), [P, GN, D]), ALU.add), k_o[q])
            a = VL(lambda: v.tensor_scalar(O3, o2, 0.0, None, op0=ALU.min))
            a = A(lambda: s.activation(O3, O3, ACT.Exp), a)
            V(lambda: v.tensor_scalar(o2, o2, 0.0, LAM, op0=ALU.max, op1=ALU.mult))
            VL(lambda: v.tensor_tensor(o2, o2, X[:, sl, :], ALU.add))
            V(lambda: v.tensor_scalar(O3, O3, -1.0, LAM * ALP, op0=ALU.add, op1=ALU.mult), a)
            VL(lambda: v.tensor_tensor(o2, o2, O3, ALU.add))
            k_n[q] = norm(o2, X[:, sl, :], sq, mu, rs, main.last("dve"))

        def tabled(q):
            sl = slice(q * GN, (q + 1) * GN)
            parts = [(q * GN, 4), (q * GN + 4, GN - 4)]
            at = [turn(l0, n, (3, 4), (k_n[q],)) for l0, n in parts]
            for (l0, n), (u, ev) in zip(parts, at):
                for i in range(n):
                    l = l0 + i - q * GN
                    p = T(lambda i=i, l=l, u=u: t.matmul(PS[7][:, l * D:(l + 1) * D], xtt[0:D, u % 2, i * P:(i + 1) * P],
                                                         W3[:, R3 * D:], start=True, stop=True), ev, uf.get("l"))
                products(u, ev, l0, n, W3, R3, y3, (5, 6), "a")
            ps7 = PS[7][:, 0:GN * D].rearrange("p (l d) -> p l d", d=D)
            uf["l"] = V(lambda: v.tensor_tensor(R[:, sl, :], X[:, sl, :], ps7, ALU.add), p)
            return VL(lambda: v.tensor_tensor(R[:, sl, :], R[:, sl, :], bc(b3[:].unsqueeze(1), [P, GN, D]), ALU.add))

        gathered(0)
        weighted(0)
        projected(0)
        for q in range(NG):
            if q + 1 < NG:
                gathered(q + 1)
                weighted(q + 1)
            finished(q)
            if q + 1 < NG:
                projected(q + 1)
            k_end = tabled(q)
        t_y3 = [("ysb%d" % i, Q.value["ysb%d" % i]) for i in range(4)]

        T3, k_t, st_t = linear_chunks(y3, I3, s3, [*t_y3, k_end])
        m3 = mend_linear(s3, T3, k_t, st_t)
        used = {}
        ov = out.rearrange("(p l) d -> p l d", l=NL)
        NG3 = arena(23400, 2, GN * D)
        for q in range(NG):
            nb = NG3[:, q % 2, :].rearrange("p (l d) -> p l d", l=GN)
            sl = slice(q * GN, (q + 1) * GN)
            for i in range(GN):
                tk = gather(nb[:, i, :], s3[:], endi[:, q * GN + i:q * GN + i + 1], m3, used.get(q - 2), sem=f"n{q % 2}")
            VL(lambda nb=nb, sl=sl: v.tensor_tensor(nb, nb, R[:, sl, :], ALU.add), tk)
            used[q] = k = norm(nb, X[:, sl, :], sq, mu, rs, ("dve", Q.value["dve"]))
            fin = ld(ov[:, sl, :].rearrange("p l d -> p (l d)"), X[:, sl, :].rearrange("p l d -> p (l d)"), k, sem="out")
        Q.wait("sync", fin, ("z", Q.value["z"]), ("zr", Q.value["zr"]))
        for n_ in names:
            if n_ in Q.value and n_ not in ("dve", "act", "pe", "pool") and n_[0:2] not in ("f0", "f1", "f2"):
                Q.wait("sync", (n_, Q.value[n_]))

        block = ctx.enter_context(nc.Block())

        @block.sync
        def _(e):
            Q.play("sync", e)

        @block.gpsimd
        def _(e):
            Q.play("gpsimd", e)

        @block.scalar
        def _(e):
            Q.play("scalar", e)

        @block.vector
        def _(e):
            Q.play("vector", e)

        @block.tensor
        def _(e):
            Q.play("tensor", e)


_INS = ["x", "src", "dst", "edge_type_16", "edge_type_8", "L0_gnn_weight", "L1_gnn_beta", "L2_gnn_W_l", "L2_gnn_W_r",
        "L2_gnn_att", "L2_gnn_bias", "L3_gnn_W", "L3_gnn_coeff", "L3_gnn_h_bias", "L3_gnn_loop_weight"]


def kernel(**inputs):
    import numpy as np
    import concourse.bacc as bacc
    from concourse.bass_utils import run_bass_kernel_spmd

    nc = bacc.Bacc("TRN2", target_bir_lowering=False, num_devices=1)
    arrays, args = {}, []
    for name in _INS:
        a = np.ascontiguousarray(inputs[name])
        if name == "x":
            a = np.concatenate([a, np.zeros((NN - N, D), a.dtype)])
        elif name == "dst":
            a = np.concatenate([a, np.full((EP + NC - E,), N, a.dtype)])
        elif name == "src":
            a = np.concatenate([a, np.full((EP - E,), N, a.dtype)])
        elif name in ("edge_type_16", "edge_type_8"):
            a = np.concatenate([a, np.zeros((EP - E,), a.dtype)])
        arrays["in_" + name] = a
        args.append(nc.dram_tensor("in_" + name, a.shape, mybir.dt.from_np(a.dtype), kind="ExternalInput").ap())
    args.append(nc.dram_tensor("out_0", (NN, D), mybir.dt.float32, kind="ExternalOutput").ap())
    build(nc, *args)
    r = run_bass_kernel_spmd(nc, [arrays], core_ids=[0])
    return np.asarray(r.results[0]["out_0"])[:N]
```

```python
from contextlib import ExitStack

import concourse.bass as bass
from concourse import mybir

P = 128
D = 64
N = 6250
NL = 49
NN = P * NL
E = 106250
NC = 832
EP = P * NC
CH = 16
NCH = NC // CH
R0 = 16
R3 = 8
H = 6
HW = H * 65
RW = HW + H
BIG = 1e30
SKIP = 200000.0
GN = 7
NG = NL // GN


class Queues:

    ENGINES = ("sync", "gpsimd", "scalar", "vector", "tensor")

    def __init__(self, sems):
        self.items = {e: [] for e in self.ENGINES}
        self.seen = {e: {} for e in self.ENGINES}
        self.value = {}
        self.sems = sems
        self.saved = {}

    def wait(self, eng, *tokens):
        for t in tokens:
            if t is None:
                continue
            name, v = t
            if v > self.seen[eng].get(name, 0):
                self.seen[eng][name] = v
                self.items[eng].append(("wait", self.sems[name], v))

    def emit(self, eng, fn, waits, sem, inc):
        self.wait(eng, *waits)
        self.value[sem] = self.value.get(sem, 0) + inc
        self.items[eng].append(("do", fn, self.sems[sem], inc))
        return (sem, self.value[sem])

    def begin_if(self, eng, flag):
        self.items[eng].append(("if", flag))
        self.saved[eng] = dict(self.seen[eng])

    def end_if(self, eng):
        self.items[eng].append(("end",))
        self.seen[eng] = self.saved.pop(eng)

    def play(self, eng, e):
        stack = []
        for it in self.items[eng]:
            if it[0] == "wait":
                e.wait_ge(it[1], it[2])
            elif it[0] == "do":
                it[1](e).then_inc(it[2], it[3])
            elif it[0] == "if":
                reg = e.value_load(it[1])
                c = e.If(reg != 0)
                c.__enter__()
                stack.append(c)
            else:
                stack.pop().__exit__(None, None, None)


def build(nc, x, src, dst, et16, et8, w0, beta, wl, wr, att, bias2, w3, coeff, hbias, loopw, out):
    F32 = mybir.dt.float32
    I32 = mybir.dt.int32
    BF16 = mybir.dt.bfloat16
    ALU = mybir.AluOpType
    ACT = mybir.ActivationFunctionType
    AX = mybir.AxisListType.X

    def dram(name, shape, dt=F32):
        return nc.dram_tensor(name, shape, dt).ap()

    y0 = dram("y0", (NN * R0, D))
    y3 = dram("y3", (NN * R3, D))
    s0 = dram("s0", (EP + 1, D))
    s1 = dram("s1", (EP + 1, 66))
    s2 = dram("s2", (EP + 1, RW))
    s3 = dram("s3", (EP + 1, D))
    xd = dram("xd", (EP, D))
    xt1 = dram("xt1", (NN, 65))
    xt2 = dram("xt2", (NN, D))
    cntd = dram("cntd", (NN,))
    srt = dram("srt", (EP, 4), I32)

    with ExitStack() as ctx:
        names = ["dve", "act", "pe", "pool", "ld", "ldn", "ldw", "ldy", "z", "cnt", "row", "xdi", "xt", "sc", "zr", "out"]
        names += [f"ysb{i}" for i in range(4)] + [f"g{i}" for i in range(5)] + [f"x{i}" for i in range(3)]
        names += [f"s{i}" for i in range(4)] + [f"n{i}" for i in range(2)]
        names += [f"f{k}{n}" for k in range(3) for n in ("dve", "pe", "pool", "sc", "ld", "cnt", "xs")]
        sems = {n: ctx.enter_context(nc.semaphore("k_" + n)) for n in names}
        Q = Queues(sems)

        def sb(name, shape, dt=F32):
            return ctx.enter_context(nc.sbuf_tensor(name, shape, dt))

        class Em:

            def __init__(self, pre):
                self.pre = pre

            def V(self, fn, *w):
                return Q.emit("vector", lambda e: fn(), w, self.pre + "dve", 1)

            def VL(self, fn, *w):
                return self.V(fn, self.last("dve"), *w)

            def T(self, fn, *w):
                return Q.emit("tensor", lambda e: fn(), w, self.pre + "pe", 1)

            def G(self, fn, *w):
                return Q.emit("gpsimd", lambda e: fn(), w, self.pre + "pool", 1)

            def last(self, n):
                return (self.pre + n, Q.value.get(self.pre + n, 0))

        main = Em("")
        V, VL, T, G = main.V, main.VL, main.T, main.G

        def A(fn, *w):
            return Q.emit("scalar", lambda e: fn(), w, "act", 1)

        def ld(o, i, *w, sem, eng="sync"):
            return Q.emit(eng, lambda e: e.dma_start(o, i, allow_slow_non_contiguous=True), w, sem, 16)

        def gather(o, table, idx, *w, sem):
            return Q.emit("gpsimd", lambda e: e.indirect_dma_start(
                out=o, out_offset=None, in_=table,
                in_offset=bass.IndirectOffsetOnAxis(ap=idx, axis=0)), w, sem, 16)

        def scatter(table, i, idx, bound, *w, sem):
            return Q.emit("gpsimd", lambda e: e.indirect_dma_start(
                out=table, out_offset=bass.IndirectOffsetOnAxis(ap=idx, axis=0), in_=i,
                in_offset=None, bounds_check=bound, oob_is_err=False), w, sem, 16)

        v, s, g, t = nc.vector, nc.scalar, nc.gpsimd, nc.tensor

        Dd = sb("Dd", [P, NC], I32)
        Si = sb("Si", [P, NC], I32)
        I3 = sb("I3", [P, NC], I32)
        gf = sb("gf", [P, NC])
        Bn = sb("Bn", [P, NC + 1])
        X = sb("X", [P, NL, D])
        R = sb("R", [P, NL, D])
        I0 = R[:].rearrange("p l d -> p (l d)")[:, 0:NC].bitcast(I32)
        W0 = R[:].rearrange("p l d -> p (l d)")[:, NC:NC + 2 * R0 * D]
        ident = sb("ident", [P, P])
        ones = sb("ones", [P, P])
        lower = sb("lower", [P, P])
        sm = sb("sm", [P, 32])
        dn = sb("dn", [P, 1], I32)
        flag = sb("flag", [P, 2], I32)
        Cq = sb("Cq", [P, P])
        CTn = sb("CTn", [P, P])
        En = sb("En", [P, P])
        cntn = sb("cntn", [P, NL])
        incl = sb("incl", [P, NL])
        nfl = sb("nfl", [P, NL])
        endi = sb("endi", [P, NL], I32)
        stai = sb("stai", [P, NL], I32)
        fixg = sb("fixg", [P, 1], I32)
        fixs = sb("fixs", [P, 1], I32)
        W3 = sb("W3", [P, R3 * D + D])
        WLR = sb("WLR", [P, H * D])
        WS = sb("WS", [D, H * D])
        W2 = sb("W2", [P, 3, D])
        A8 = sb("A8", [P, 3, 32])
        Vm = sb("Vm", [P, 32])
        Vs = sb("Vs", [D, 32])
        att3 = sb("att3", [P, 3])
        co = sb("co", [P, R3 * 2])
        wb = sb("wb", [P, 2, D])
        b2 = sb("b2", [P, D])
        b3 = sb("b3", [P, D])
        bet = sb("bet", [P, 1])
        es = sb("es", [P, NL, H])
        hi98 = sb("hi98", [P, 98], I32)[:]
        lo64 = sb("lo64", [P, 64], I32)[:]
        zrow = sb("zrow", [1, RW])
        zr1 = sb("zr1", [1, 66])
        ARENA = 38400
        AR = sb("AR", [P, ARENA])

        def arena(off, *shape):
            n = 1
            for k in shape:
                n *= k
            assert off + n <= ARENA, (off, shape)
            a = AR[:, off:off + n]
            if len(shape) == 2:
                a = a.rearrange("p (a b) -> p a b", a=shape[0])
            if len(shape) == 3:
                a = a.rearrange("p (a b c) -> p a b c", a=shape[0], b=shape[1])
            return a

        PS = [ctx.enter_context(nc.psum_tensor(f"ps{i}", [P, 512], F32)) for i in range(8)]

        def bc(a, shape):
            return a.broadcast_to(shape)

        AF = AR[:, 0:NC * 2].bitcast(I32)
        Df = arena(2100, NC)
        e16t, e8t = AF[:, 0:NC], AF[:, NC:2 * NC]
        ld(Dd[:], dst[0:EP].rearrange("(p j) -> p j", j=NC), sem="ld")
        ld(dn[:], dst[NC:NC + EP].rearrange("(p j) -> p j", j=NC)[:, 0:1], sem="ld")
        ld(Si[:], src.rearrange("(p j) -> p j", j=NC), sem="ld")
        ld(e16t, et16.rearrange("(p j) -> p j", j=NC), sem="ld")
        l_edges = ld(e8t, et8.rearrange("(p j) -> p j", j=NC), sem="ld")
        l_x = ld(X[:], x.rearrange("(p l) d -> p l d", l=NL), sem="ldn")
        for lo in (0, D):
            at = (lo > 0) * R0 * D
            l_y = ld(W0[lo:lo + D, at:at + R0 * D].rearrange("p (r o) -> p r o", r=R0), w0.rearrange("r i o -> i r o"), sem="ldy")
        k_wz = V(lambda: v.memset(W0[0:D, R0 * D:], 0.0))
        k_wz = V(lambda: v.memset(W0[D:P, 0:R0 * D], 0.0))
        ld(WLR[0:D, :], wl, sem="ldw")
        ld(WLR[D:P, :], wr, sem="ldw")
        ld(WS[:], wr, sem="ldw")
        wlv = wl.rearrange("f (c h o) -> f c h o", c=3, h=2)
        ld(W2[0:D, :, :], wlv[:, :, 0, :], sem="ldw")
        ld(W2[D:P, :, :], wlv[:, :, 1, :], sem="ldw")
        attf = att.rearrange("h o -> (h o)")
        ld(att3[:], attf.rearrange("(c q) -> q c", c=3), sem="ldw")
        ld(co[:], coeff.rearrange("r b -> (r b)").partition_broadcast(P), sem="ldw")
        for lo in (0, D):
            ld(wb[lo:lo + D], w3.rearrange("b i o -> i b o"), sem="ldw")
            ld(W3[lo:lo + D, R3 * D:], loopw, sem="ldw")
        ld(b2[:], bias2.partition_broadcast(P), sem="ldw")
        ld(b3[:], hbias.partition_broadcast(P), sem="ldw")
        ld(bet[:], beta.partition_broadcast(P), sem="ldw")
        attb = arena(2 * NC, H, D)
        l_w = ld(attb.rearrange("p h o -> p (h o)"), attf.partition_broadcast(P), sem="ldw")

        k_ones = V(lambda: v.memset(ones[:], 1.0))
        c1 = G(lambda: g.affine_select(out=ident[:], in_=ones[:], compare_op=ALU.is_equal, fill=0.0, base=0,
                                       pattern=[[-1, P]], channel_multiplier=1), k_ones)
        c2 = G(lambda: g.affine_select(out=lower[:], in_=ones[:], compare_op=ALU.is_gt, fill=0.0, base=0,
                                       pattern=[[1, P]], channel_multiplier=-1))
        pidx = sm[:, 30:31].bitcast(I32)
        G(lambda: g.iota(hi98, [[1, 98]], base=0, channel_multiplier=0))
        G(lambda: g.iota(pidx, [[0, 1]], base=0, channel_multiplier=1))
        c3 = G(lambda: g.iota(lo64, [[1, 64]], base=0, channel_multiplier=0))

        zt = arena(31500, CH * D)
        k_z = V(lambda: v.memset(zt, 0.0))
        V(lambda: v.memset(zrow[:], 0.0))
        VL(lambda: v.memset(zrow[0:1, HW:], -BIG))
        V(lambda: v.memset(zr1[:], 0.0))
        k_zr = VL(lambda: v.memset(zr1[0:1, 65:66], -BIG))
        ld(s0[EP:EP + 1, :], zr1[0:1, 0:D], k_zr, sem="zr")
        ld(s3[EP:EP + 1, :], zr1[0:1, 0:D], k_zr, sem="zr")
        ld(s1[EP:EP + 1, :], zr1[:], k_zr, sem="zr")
        l_zr = ld(s2[EP:EP + 1, :], zrow[:], k_zr, sem="zr")

        dnf, bad, badc = sm[:, 0:1], sm[:, 1:2], sm[:, 2:3]
        scr = arena(5000, NC)
        V(lambda: v.tensor_copy(Df, Dd[:]), l_edges)
        VL(lambda: v.tensor_copy(dnf, dn[:]))
        VL(lambda: v.tensor_tensor(scr[:, 0:NC - 1], Df[:, 0:NC - 1], Df[:, 1:NC], ALU.is_gt))
        VL(lambda: v.tensor_tensor(scr[:, NC - 1:NC], Df[:, NC - 1:NC], dnf, ALU.is_gt))
        a = VL(lambda: v.tensor_reduce(bad, scr, AX, ALU.max))
        b = T(lambda: t.matmul(PS[0][:, 0:1], ones[:], bad, start=True, stop=True), a)
        k_flag = V(lambda: v.tensor_copy(flag[:, 0:1], PS[0][:, 0:1]), b)

        def resort(em, swap):
            FV, pre = em.VL, em.pre
            NB = (NN + 511) // 512
            IO = arena(5000, NN).bitcast(I32)
            CN = arena(5000 + NN, NN)
            JJ = arena(5000 + 2 * NN, NN)
            RR = arena(5000 + 3 * NN, NC, 4).bitcast(I32)
            rank = arena(5000 + 3 * NN + 4 * NC, NC)
            posi = gf[:].bitcast(I32)
            tmp = Bn[:, 0:NC]
            io = em.G(lambda: g.iota(IO, [[1, NN]], base=0, channel_multiplier=0))
            cols = (Dd[:], Si[:], e16t, e8t) if swap else (Si[:], Dd[:], e16t, e8t)
            for k, c in enumerate(cols):
                FV(lambda k=k, c=c: v.tensor_copy(RR[:, :, k], c))
            FV(lambda: v.tensor_copy(Df, RR[:, :, 1]))
            FV(lambda: v.memset(CN, 0.0), io)
            FV(lambda: v.memset(tmp, 0.0))
            FV(lambda: v.memset(rank, 0.0))
            for j in range(NC):
                FV(lambda j=j: v.scalar_tensor_tensor(out=JJ, in0=IO, scalar=Df[:, j:j + 1], in1=CN, op0=ALU.is_equal,
                                                      op1=ALU.mult, accum_out=rank[:, j:j + 1]))
                FV(lambda j=j: v.scalar_tensor_tensor(out=CN, in0=IO, scalar=Df[:, j:j + 1], in1=CN, op0=ALU.is_equal,
                                                      op1=ALU.add))
            done = em.last("dve")
            for bk in range(NB):
                lo, hi = bk * 512, min(NN, bk * 512 + 512)
                em.T(lambda lo=lo, hi=hi: t.matmul(PS[0][:, 0:hi - lo], ones[:], CN[:, lo:hi], start=True, stop=True), done)
                p = em.T(lambda lo=lo, hi=hi: t.matmul(PS[1][:, 0:hi - lo], lower[:], CN[:, lo:hi], start=True, stop=True), c2)
                FV(lambda lo=lo, hi=hi: v.tensor_copy(JJ[:, lo:hi], PS[0][:, 0:hi - lo]), p)
                done = FV(lambda lo=lo, hi=hi: v.tensor_copy(CN[:, lo:hi], PS[1][:, 0:hi - lo]))
            FV(lambda: v.tensor_tensor_scan(JJ, JJ, JJ, 0.0, ALU.add, ALU.bypass))
            FV(lambda: v.tensor_tensor(CN[:, 1:NN], CN[:, 1:NN], JJ[:, 0:NN - 1], ALU.add))
            for j in range(NC):
                FV(lambda j=j: v.scalar_tensor_tensor(out=JJ, in0=IO, scalar=Df[:, j:j + 1], in1=CN, op0=ALU.is_equal,
                                                      op1=ALU.mult, accum_out=tmp[:, j:j + 1]))
            FV(lambda: v.tensor_tensor(rank, rank, tmp, ALU.add))
            fin = FV(lambda: v.tensor_copy(posi, rank))
            for j in range(NC):
                sc = scatter(srt, RR[:, j, :], posi[:, j:j + 1], EP - 1, fin, sem=pre + "sc")
            sv = srt.rearrange("(p j) k -> p j k", j=NC)
            ld(RR, sv, sc, sem=pre + "ld")
            l = ld(dn[0:P - 1, :], sv[1:P, 0, 1:2], sc, sem=pre + "ld")
            FV(lambda: v.tensor_copy(Si[:], RR[:, :, 0]), l)
            FV(lambda: v.tensor_copy(Dd[:], RR[:, :, 1]))
            FV(lambda: v.tensor_copy(e16t, RR[:, :, 2]))
            FV(lambda: v.tensor_copy(e8t, RR[:, :, 3]))
            FV(lambda: v.tensor_copy(Df, Dd[:]))
            FV(lambda: v.tensor_copy(dnf, dn[:]))

        dhi = arena(3000, NC).bitcast(I32)
        dlo = arena(4000, NC).bitcast(I32)

        def flags(em):
            em.V(lambda: v.scalar_tensor_tensor(out=I3[:], in0=Si[:], scalar=8.0, in1=e8t, op0=ALU.mult, op1=ALU.add),
                 em.last("dve"))
            em.V(lambda: v.memset(gf[:, 0:1], 0.0))
            em.V(lambda: v.memset(Bn[:, NC:NC + 1], -BIG))
            em.V(lambda: v.tensor_tensor(gf[:, 1:NC], Df[:, 1:NC], Df[:, 0:NC - 1], ALU.is_equal))
            em.VL(lambda: v.tensor_scalar(Bn[:, 0:NC], gf[:], -1.0, BIG, op0=ALU.add, op1=ALU.mult))
            em.V(lambda: v.tensor_scalar(dhi, Dd[:], 6, None, op0=ALU.logical_shift_right))
            return em.V(lambda: v.tensor_scalar(dlo, Dd[:], 63, None, op0=ALU.bitwise_and))

        pf, cont, key, df_, eqn, inv, pos, eqc = (sm[:, k:k + 1] for k in range(3, 11))

        def masks(em):
            scr2 = arena(5000, NC)
            dg = arena(6000, 2, P)
            V, VL = em.V, em.VL
            V(lambda: v.tensor_copy(pf, pidx), c3)
            V(lambda: v.tensor_copy(df_, Df[:, 0:1]))
            V(lambda: v.tensor_tensor(eqn, Df[:, NC - 1:NC], dnf, ALU.is_equal), em.last("dve"))
            VL(lambda: v.tensor_scalar(inv, pf, 126.5, None, op0=ALU.is_lt))
            VL(lambda: v.tensor_tensor(cont, eqn, inv, ALU.mult))
            VL(lambda: v.tensor_scalar(key, Df[:, NC - 1:NC], 1.0, None, op0=ALU.add))
            VL(lambda: v.tensor_scalar(key, key, cont, -1.0, op0=ALU.mult, op1=ALU.add))
            VL(lambda: v.tensor_scalar(dg[:, 0, :], ident[:], key, None, op0=ALU.mult), c1)
            a = VL(lambda: v.tensor_scalar(dg[:, 1, :], ident[:], df_, None, op0=ALU.mult))
            b = em.T(lambda: t.matmul(PS[1][:, 0:2 * P], ones[:], dg.rearrange("p a b -> p (a b)"), start=True, stop=True), a)
            V(lambda: v.tensor_scalar(Cq[:], PS[1][:, P:2 * P], key, None, op0=ALU.is_equal), b)
            V(lambda: v.tensor_scalar(CTn[:], PS[1][:, 0:P], df_, None, op0=ALU.is_equal))
            V(lambda: v.tensor_scalar(En[:], PS[1][:, 0:P], key, None, op0=ALU.is_equal))
            VL(lambda: v.tensor_reduce(inv, CTn[:], AX, ALU.max))
            VL(lambda: v.tensor_scalar(CTn[:], CTn[:], -1.0, BIG, op0=ALU.add, op1=ALU.mult))
            VL(lambda: v.tensor_scalar(En[:], En[:], -1.0, BIG, op0=ALU.add, op1=ALU.mult))
            VL(lambda: v.tensor_scalar(scr2, Df, df_, None, op0=ALU.is_equal))
            VL(lambda: v.reduce_sum(eqc, scr2, AX))
            VL(lambda: v.tensor_scalar(pos, pf, float(NC), -1.0, op0=ALU.mult, op1=ALU.add))
            VL(lambda: v.tensor_tensor(pos, pos, eqc, ALU.add))
            VL(lambda: v.tensor_copy(fixg[:], pos))
            VL(lambda: v.tensor_scalar(eqc, eqc, float(NC) - 0.5, None, op0=ALU.is_gt))
            VL(lambda: v.tensor_tensor(eqc, eqc, cont, ALU.mult))
            VL(lambda: v.tensor_tensor(inv, inv, eqc, ALU.is_gt))
            VL(lambda: v.tensor_scalar(inv, inv, -SKIP, SKIP, op0=ALU.mult, op1=ALU.add))
            VL(lambda: v.tensor_tensor(pos, pos, inv, ALU.add))
            return VL(lambda: v.tensor_copy(fixs[:], pos))

        ohh = arena(17400, CH * 98 // 2).bitcast(BF16).rearrange("p (j a) -> p j a", j=CH)
        ohl = arena(18300, CH * 64 // 2).bitcast(BF16).rearrange("p (j a) -> p j a", j=CH)

        def hist(em, c, before):
            em.V(lambda: v.tensor_tensor(ohh, bc(dhi[:, c * CH:(c + 1) * CH].unsqueeze(2), [P, CH, 98]),
                                         bc(hi98.unsqueeze(1), [P, CH, 98]), ALU.is_equal), before, c3,
                 k_dl if em is main else em.last("dve"))
            a = em.V(lambda: v.tensor_tensor(ohl, bc(dlo[:, c * CH:(c + 1) * CH].unsqueeze(2), [P, CH, 64]),
                                             bc(lo64.unsqueeze(1), [P, CH, 64]), ALU.is_equal))
            for j in range(CH):
                b = em.T(lambda j=j: t.matmul(PS[0][0:98, 0:64], ohh[:, j, :], ohl[:, j, :],
                                              start=(c == 0 and j == 0), stop=(c == NCH - 1 and j == CH - 1)), a)
            return b

        def node_rows(em, before):
            VL, pre = em.VL, em.pre
            hsb = arena(19000, 64)
            a = em.V(lambda: v.tensor_copy(hsb[0:98, :], PS[0][0:98, 0:64]), before)
            b = ld(cntd.rearrange("(a b) -> a b", b=64), hsb[0:98, :], a, sem=pre + "cnt")
            b = ld(cntn[:], cntd.rearrange("(p l) -> p l", l=NL), b, sem=pre + "cnt")
            em.V(lambda: v.tensor_tensor_scan(incl[:], cntn[:], cntn[:], 0.0, ALU.add, ALU.bypass), b)
            a = VL(lambda: v.tensor_copy(sm[:, 11:12], incl[:, NL - 1:NL]))
            b = em.T(lambda: t.matmul(PS[1][:, 0:1], lower[:], sm[:, 11:12], start=True, stop=True), a, c2)
            VL(lambda: v.tensor_copy(sm[:, 12:13], PS[1][:, 0:1]), b)
            VL(lambda: v.tensor_scalar(incl[:], incl[:], sm[:, 12:13], None, op0=ALU.add))
            VL(lambda: v.tensor_scalar(nfl[:], cntn[:], 0.5, None, op0=ALU.is_gt))
            VL(lambda: v.tensor_tensor(cntn[:], incl[:], cntn[:], ALU.subtract))
            VL(lambda: v.tensor_scalar(incl[:], incl[:], -1.0 - EP, None, op0=ALU.add))
            VL(lambda: v.tensor_tensor(incl[:], incl[:], nfl[:], ALU.mult))
            VL(lambda: v.tensor_scalar(endi[:], incl[:], float(EP), None, op0=ALU.add))
            VL(lambda: v.tensor_scalar(nfl[:], nfl[:], -SKIP, SKIP, op0=ALU.mult, op1=ALU.add))
            return VL(lambda: v.tensor_tensor(stai[:], cntn[:], nfl[:], ALU.add))

        BRANCHING = ("vector", "tensor", "gpsimd", "sync")
        xdv = xd.rearrange("(p j) d -> p j d", j=NC)

        def exchange(em, which, rows, *before):
            for e_ in BRANCHING:
                Q.wait(e_, *before)
                Q.begin_if(e_, which)
            em.V(lambda: v.memset(e16t, 0.0))
            em.V(lambda: v.tensor_scalar(e8t, I3[:], 7, None, op0=ALU.bitwise_and))
            resort(em, True)
            flags(em)
            masks(em)
            b = None
            for c in range(NCH):
                b = hist(em, c, b)
            a = node_rows(em, b)
            k = em.V(lambda: v.memset(zt, 0.0), a)
            for c in range(NCH):
                z = ld(xdv[:, c * CH:(c + 1) * CH, :].rearrange("p j d -> p (j d)"), zt, k, sem=em.pre + "ld")
            for l in range(NL):
                z = scatter(xd, rows[:, l, :], stai[:, l:l + 1], EP - 1, k, z, sem=em.pre + "xs")
            for e_ in BRANCHING:
                Q.wait(e_, z)
            for e_ in BRANCHING:
                Q.end_if(e_)

        for e_ in BRANCHING:
            Q.wait(e_, k_flag)
            Q.begin_if(e_, flag[0:1, 0:1])
        resort(Em("f0"), False)
        for e_ in BRANCHING:
            Q.end_if(e_)
        k_i0 = V(lambda: v.scalar_tensor_tensor(out=I0, in0=Si[:], scalar=16.0, in1=e16t, op0=ALU.mult, op1=ALU.add))
        k_dl = k_bn = flags(main)

        xtt = arena(8000, 2, 512)
        ydone, tfree = {}, {}
        tcount = {"b": 0, "y": 0, "k": 0}

        def pairs_of(l0, n):
            return [(l0 + i, min(2, n - i), i // 2) for i in range(0, n, 2)]

        def turn(l0, n, banks, ready, eng="v"):
            u = tcount["b"]
            tcount["b"] += 1
            bnk = banks[u % len(banks)]
            xv = X[:].rearrange("p l d -> p (l d)")
            prs = pairs_of(l0, n)
            for l, w, i in prs:
                a = T(lambda l=l, w=w, i=i: t.transpose(PS[bnk][0:w * D, i * P:(i + 1) * P], xv[:, l * D:(l + w) * D], ident[:]),
                      *ready, tfree.get(("t", bnk)))
            full = n // 2 * P
            parts = ([(P, 0, full)] if full else []) + ([(D, full, full + P)] if n % 2 else [])
            for rows, lo, hi in parts:
                f = lambda rows=rows, lo=lo, hi=hi: (v.tensor_copy if eng == "v" else s.copy)(
                    xtt[0:rows, u % 2, lo:hi], PS[bnk][0:rows, lo:hi])
                a = (V if eng == "v" else A)(f, a, tfree.get(("x", u - 2)))
            tfree[("t", bnk)] = a
            return u, a

        def products(u, ev, l0, n, W, nrel, ytab, ysb, banks, engines, over_zeros, extra=None, between=()):
            yv = ytab.rearrange("(p l r) d -> p (l r d)", l=NL, r=nrel)
            wt = nrel * D
            for l, w, i in pairs_of(l0, n):
                k = tcount["k"]
                tcount["k"] += 1
                toks = []
                if extra is not None:
                    extra(l, w, xtt[:, u % 2, i * P:(i + 1) * P], ev)
                for o in range(0, wt, 512):
                    for hf in range(w):
                        y = tcount["y"]
                        tcount["y"] += 1
                        bnk = banks[y % len(banks)]
                        rows, at = slice(0, w * D), hf * over_zeros
                        p = T(lambda i=i, o=o + at, bnk=bnk, rows=rows: t.matmul(
                            PS[bnk][:], xtt[rows, u % 2, i * P:(i + 1) * P], W[rows, o:o + 512], start=True, stop=True),
                            ev, tfree.get(("y", bnk)))
                        to = ysb[:, k % 4, hf * wt + o:hf * wt + o + 512]
                        if engines[y % len(engines)] == "a":
                            q = A(lambda bnk=bnk, to=to: s.copy(to, PS[bnk][:]), p, ydone.get(k - 4))
                        else:
                            q = V(lambda bnk=bnk, to=to: v.tensor_copy(to, PS[bnk][:]), p, ydone.get(k - 4))
                        tfree[("y", bnk)] = q
                        toks.append(q)
                ydone[k] = ld(yv[:, l * wt:(l + w) * wt], ysb[:, k % 4, 0:w * wt], *toks, sem=f"ysb{k % 4}")
                if i < len(between):
                    between[i]()
            tfree[("x", u)] = p

        ysb0 = arena(9024, 4, 2 * R0 * D)
        batches = [(l0, min(8, NL - l0)) for l0 in range(0, NL, 8)]
        nxt = turn(*batches[0], (2, 3), (l_x, l_y, c1, k_wz))
        for n_, (l0, n) in enumerate(batches):
            cur = nxt
            if n_ + 1 < len(batches):
                nxt = turn(*batches[n_ + 1], (2, 3), ())
            products(*cur, l0, n, W0, R0, y0, ysb0, (4, 5, 6, 7), "av", over_zeros=R0 * D)
        zfill = {}

        def zero_rows(c):
            zfill["k"] = ld(xdv[:, c * CH:(c + 1) * CH, :].rearrange("p j d -> p (j d)"), zt, k_z, sem="z")

        t_y0 = [("ysb%d" % i, Q.value["ysb%d" % i]) for i in range(4)]
        k_fix = masks(main)

        tA = arena(7000, H, D)
        V(lambda: v.tensor_tensor(tA, WLR[:].rearrange("p (h o) -> p h o", h=H), attb, ALU.mult), l_w)
        VL(lambda: v.memset(Vm[:], 0.0))
        VL(lambda: v.reduce_sum(Vm[:, 0:H], tA, AX))
        VL(lambda: v.tensor_scalar(Vm[:], Vm[:], 0.2, None, op0=ALU.mult))
        V(lambda: v.tensor_tensor(WS[:], WS[:], WLR[0:D, :], ALU.add))
        VL(lambda: v.tensor_tensor(tA[0:D], WS[:].rearrange("p (h o) -> p h o", h=H), attb[0:D], ALU.mult))
        VL(lambda: v.memset(Vs[:], 0.0))
        VL(lambda: v.reduce_sum(Vs[:, 0:H], tA[0:D], AX))
        VL(lambda: v.tensor_scalar(Vs[:], Vs[:], 0.2, None, op0=ALU.mult))
        VL(lambda: v.memset(A8[:], 0.0))
        for c in range(3):
            VL(lambda c=c: v.tensor_scalar(A8[0:D, c, 2 * c:2 * c + 1], att3[0:D, c:c + 1], 0.8, None, op0=ALU.mult))
            VL(lambda c=c: v.tensor_scalar(A8[D:P, c, 2 * c + 1:2 * c + 2], att3[D:P, c:c + 1], 0.8, None, op0=ALU.mult))
        for r in range(R3):
            V(lambda r=r: v.tensor_scalar(W3[:, r * D:(r + 1) * D], wb[:, 0, :], co[:, 2 * r:2 * r + 1], None, op0=ALU.mult))
            k_w = VL(lambda r=r: v.scalar_tensor_tensor(out=W3[:, r * D:(r + 1) * D], in0=wb[:, 1, :],
                                                        scalar=co[:, 2 * r + 1:2 * r + 2],
                                                        in1=W3[:, r * D:(r + 1) * D], op0=ALU.mult, op1=ALU.add))

        def chunk_view(st, c, w):
            return st[0:EP, :].rearrange("(p j) d -> p j d", j=NC)[:, c * CH:(c + 1) * CH, :].rearrange("p j d -> p (j d)")

        def linear_chunks(tab, idx, st, ready, side=None):
            NBUF = 4
            GB = arena(13200, NBUF, CH * D)
            stored, first = {}, {}
            last = None
            for c in range(NCH):
                b_ = c % NBUF
                buf = GB[:, b_, :].rearrange("p (j d) -> p j d", j=CH)
                prev = GB[:, (c - 1) % NBUF, :].rearrange("p (j d) -> p j d", j=CH)
                for j in range(CH):
                    tk = gather(buf[:, j, :], tab, idx[:, c * CH + j:c * CH + j + 1], *ready, stored.get(c - NBUF),
                                first.get(c - NBUF + 1), sem=f"g{b_}")
                if side is not None:
                    side(c)
                for j in range(CH):
                    if c == 0 and j == 0:
                        continue
                    pr = buf[:, j - 1, :] if j else prev[:, CH - 1, :]
                    last = VL(lambda c=c, j=j, pr=pr, buf=buf: v.scalar_tensor_tensor(
                        out=buf[:, j, :], in0=pr, scalar=gf[:, c * CH + j:c * CH + j + 1], in1=buf[:, j, :],
                        op0=ALU.mult, op1=ALU.add), tk, k_bn)
                    if j == 0:
                        first[c] = last
                stored[c] = ld(chunk_view(st, c, D), GB[:, b_, :], last, sem=f"s{b_}")
            return GB[:, (NCH - 1) % NBUF, (CH - 1) * D:CH * D], last, [stored[c] for c in range(NCH - NBUF, NCH)]

        HF = ((1999, 8), (1361, 9), (1733, 7), (1117, 10), (1871, 6), (1553, 9))
        HS = arena(20000, len(HF), NC).bitcast(I32)
        HD = arena(20000 + len(HF) * NC, len(HF), NC).bitcast(I32)
        hj = arena(30000, NC)
        acc = arena(30900, 32)
        pairs = [(a_, b_) for a_ in range(len(HF)) for b_ in range(a_)]
        twin = []
        for tile_, of in ((HS, Si), (HD, Dd)):
            for i, (m_, k_) in enumerate(HF):
                twin.append(lambda tile_=tile_, of=of, i=i, m_=m_: V(
                    lambda: v.tensor_scalar(tile_[:, i, :], of[:], float(m_), None, op0=ALU.mult)))
                twin.append(lambda tile_=tile_, i=i, k_=k_: VL(
                    lambda: v.tensor_scalar(tile_[:, i, :], tile_[:, i, :], k_, 7, op0=ALU.logical_shift_right,
                                            op1=ALU.bitwise_and)))
        for i, (a_, b_) in enumerate(pairs):
            for o_, (p_, q_) in ((i, (a_, b_)), (16 + i, (b_, a_))):
                twin.append(lambda o_=o_, p_=p_, q_=q_: VL(
                    lambda: v.scalar_tensor_tensor(out=hj, in0=HS[:, p_, :], scalar=1.0, in1=HD[:, q_, :], op0=ALU.mult,
                                                   op1=ALU.mult, accum_out=acc[:, o_:o_ + 1])))

        hist_pe = {}

        def side(c):
            zero_rows(c)
            hist_pe[c] = hist(main, c, hist_pe.get(c - 1))
            for _ in range(2):
                if twin:
                    twin.pop(0)()

        T0, k_t, st_t = linear_chunks(y0, I0, s0, [*t_y0, k_i0], side)
        npr = len(pairs)
        a = VL(lambda: v.tensor_tensor(acc[:, 0:npr], acc[:, 0:npr], acc[:, 16:16 + npr], ALU.subtract))
        b = T(lambda: t.matmul(PS[1][:, 0:npr], ones[:], acc[:, 0:npr], start=True, stop=True), a)
        V(lambda: v.tensor_copy(acc[:, 0:npr], PS[1][:, 0:npr]), b)
        VL(lambda: v.tensor_tensor(acc[:, 0:npr], acc[:, 0:npr], acc[:, 0:npr], ALU.mult))
        VL(lambda: v.tensor_reduce(sm[:, 13:14], acc[:, 0:npr], AX, ALU.max))
        VL(lambda: v.tensor_scalar(sm[:, 13:14], sm[:, 13:14], 0.5, None, op0=ALU.is_gt))
        k_twin = VL(lambda: v.tensor_copy(flag[:, 1:2], sm[:, 13:14]))
        k_node = node_rows(main, hist_pe[NCH - 1])

        def mend_linear(st, Tl, k_last, stored):
            fr = arena(19100, D)
            gt = gather(fr, st[:], fixg[:], *stored, k_fix, l_zr, sem="row")
            a = T(lambda: t.matmul(PS[2][:, 0:D], Cq[:], Tl, start=True, stop=True), k_last)
            b = VL(lambda: v.tensor_tensor(fr, fr, PS[2][:, 0:D], ALU.add), a, gt)
            return scatter(st[:], fr, fixs[:], EP - 1, b, sem="row")

        def norm(y, o, sq, mu, rs, *w):
            n = y.shape[1]
            sh = [P, n, D]
            V(lambda: v.reduce_sum(mu, y, AX), *w)
            VL(lambda: v.tensor_scalar(mu, mu, 1.0 / D, None, op0=ALU.mult))
            VL(lambda: v.tensor_tensor(y, y, bc(mu.unsqueeze(2), sh), ALU.subtract))
            VL(lambda: v.tensor_tensor(sq, y, y, ALU.mult))
            VL(lambda: v.reduce_sum(rs, sq, AX))
            a = VL(lambda: v.tensor_scalar(rs, rs, 1.0 / D, 1e-5, op0=ALU.mult, op1=ALU.add))
            a = A(lambda: s.sqrt(rs, rs), a)
            VL(lambda: v.reciprocal(rs, rs), a)
            return VL(lambda: v.tensor_tensor(o, y, bc(rs.unsqueeze(2), sh), ALU.mult))

        sq = arena(19300, GN, D)
        mu = arena(19800, GN)
        rs = arena(19820, GN)

        m0 = mend_linear(s0, T0, k_t, st_t)
        xts = arena(20000, NL, 65)
        zz = R
        NG0 = arena(23400, 2, GN * D)
        used = {}
        sc_done = None

        def node_gathers(q, NB, st, *w):
            nb = NB[:, q % 2, :].rearrange("p (l d) -> p l d", l=GN)
            for i in range(GN):
                used[("g", q)] = gather(nb[:, i, :], st[:], endi[:, q * GN + i:q * GN + i + 1], *w, used.get(q - 2),
                                        sem=f"n{q % 2}")

        k_row = {}

        def to_edges(q, rows, *w):
            for l in range(q * GN, (q + 1) * GN):
                a = scatter(xd, rows[:, l, :], stai[:, l:l + 1], EP - 1, k_row[q], *w, sem="sc")
            return a

        node_gathers(0, NG0, s0, m0, k_node)
        for q in range(NG):
            nb = NG0[:, q % 2, :].rearrange("p (l d) -> p l d", l=GN)
            sl = slice(q * GN, (q + 1) * GN)
            if q + 1 < NG:
                node_gathers(q + 1, NG0, s0, m0, k_node)
            tk = used[("g", q)]
            VL(lambda nb=nb, sl=sl: v.tensor_tensor(nb, nb, X[:, sl, :], ALU.add), tk)
            k = norm(nb, X[:, sl, :], sq, mu, rs, ("dve", Q.value["dve"]))
            used[q] = k
            VL(lambda sl=sl: v.tensor_tensor(sq, X[:, sl, :], X[:, sl, :], ALU.mult))
            VL(lambda: v.reduce_sum(rs, sq, AX))
            a = VL(lambda: v.tensor_scalar(rs, rs, 1e-8, None, op0=ALU.add))
            a = A(lambda: s.sqrt(rs, rs), a)
            VL(lambda: v.reciprocal(rs, rs), a)
            VL(lambda sl=sl: v.tensor_copy(xts[:, sl, 0:D], X[:, sl, :]))
            a = VL(lambda sl=sl: v.tensor_copy(xts[:, sl, D], rs))
            VL(lambda: v.tensor_scalar(mu, rs, bet[:], None, op0=ALU.mult))
            b = VL(lambda sl=sl: v.tensor_tensor(zz[:, sl, :], X[:, sl, :], bc(mu.unsqueeze(2), [P, GN, D]), ALU.mult))
            xw = ld(xt1.rearrange("(p l) d -> p l d", l=NL)[:, sl, :].rearrange("p l d -> p (l d)"),
                    xts[:, sl, :].rearrange("p l d -> p (l d)"), a, sem="xt")
            k_row[q] = b
            if q:
                sc_done = to_edges(q - 1, zz, zfill["k"])
        sc_done = to_edges(NG - 1, zz, zfill["k"])
        k_end = ("dve", Q.value["dve"])

        def now():
            return [(n_, Q.value[n_]) for n_ in ("dve", "act", "pe")]

        exchange(Em("f1"), flag[0:1, 1:2], zz, *now(), xw, sc_done)

        def fence(*toks):
            for e_ in Queues.ENGINES:
                Q.wait(e_, *toks)

        fence(k_end)

        def merged(*lists):
            total = max(len(x_) for x_ in lists)
            at = [0] * len(lists)
            for i in range(total):
                for k_, x_ in enumerate(lists):
                    while at[k_] * total < (i + 1) * len(x_):
                        x_[at[k_]]()
                        at[k_] += 1

        G1 = arena(0, 4, CH * 65)
        XB1 = arena(4200, 3, CH * D)
        XF1 = arena(7300, 2, CH * D)
        TM1 = arena(9400, CH, D)
        S1 = arena(10500, 3, CH * 66)
        e1, m1 = arena(13700, CH), arena(13720, CH)
        mf1 = arena(13740, CH)
        pf1 = arena(13760, 2, CH + 1)
        xi1 = arena(13800, 65)
        gi = gather(xi1, xt1, Dd[:, 0:1], xw, k_end, sem="xdi")
        k_g, k_xb, freeG, freeXB, freeXF, stored, pxd = {}, {}, {}, {}, {}, {}, {}
        k_fill = {}

        def g1(c):
            for j in range(CH):
                k_g[c] = gather(G1[:, c % 4, j * 65:(j + 1) * 65], xt1, Si[:, c * CH + j:c * CH + j + 1],
                                xw, freeG.get(c - 4), sem=f"g{c % 4}")

        def xb(c, XB, free, ready):
            k_xb[c] = ld(XB[:, c % XBN, :], xdv[:, c * CH:(c + 1) * CH, :].rearrange("p j d -> p (j d)"),
                         ready, free.get(c - XBN), sem=f"x{c % XBN}")

        XBN = 3

        def fills1(c):
            ops = []
            XBv = XB1[:, c % 3, :].rearrange("p (j d) -> p j d", j=CH)
            XFv = XF1[:, c % 2, :].rearrange("p (j d) -> p j d", j=CH)
            XFp = XF1[:, (c - 1) % 2, :].rearrange("p (j d) -> p j d", j=CH)
            mine = [None]

            def one(j):
                if c == 0 and j == 0:
                    def f():
                        V(lambda: v.tensor_scalar(mu[:, 0:1], xi1[:, 64:65], bet[:], None, op0=ALU.mult), gi)
                        mine[0] = VL(lambda: v.tensor_scalar(XFv[:, 0, :], xi1[:, 0:D], mu[:, 0:1], None, op0=ALU.mult))
                    return f
                pr = XFv[:, j - 1, :] if j else XFp[:, CH - 1, :]

                def f():
                    mine[0] = V(lambda: v.scalar_tensor_tensor(
                        out=XFv[:, j, :], in0=pr, scalar=gf[:, c * CH + j:c * CH + j + 1], in1=XBv[:, j, :],
                        op0=ALU.mult, op1=ALU.add), k_xb[c], mine[0] or k_fill.get(c - 1), freeXF.get(c - 2))
                    k_fill[c] = mine[0]
                    freeXB[c] = mine[0]
                return f
            return [one(j) for j in range(CH)]

        def soft1(c):
            Gv = G1[:, c % 4, :].rearrange("p (j d) -> p j d", j=CH)
            XFv = XF1[:, c % 2, :].rearrange("p (j d) -> p j d", j=CH)
            Sv = S1[:, c % 3, :].rearrange("p (j d) -> p j d", j=CH)
            Sp = S1[:, (c - 1) % 3, :].rearrange("p (j d) -> p j d", j=CH)
            pe_ = pf1[:, c % 2, :]
            mine = [None]

            def L(fn, *w):
                def f():
                    mine[0] = V(fn, mine[0] or k_fill[c], *w)
                return f

            def at_dot():
                freeXF[c] = V(lambda: v.tensor_tensor(TM1, Gv[:, :, 0:D], XFv, ALU.mult), k_fill[c], k_g[c])
                mine[0] = freeXF[c]
            ops = [at_dot,
                   L(lambda: v.reduce_sum(e1, TM1, AX)),
                   L(lambda: v.tensor_tensor(e1, e1, Gv[:, :, D], ALU.mult)),
                   L(lambda: v.tensor_tensor_scan(mf1, Bn[:, c * CH:(c + 1) * CH], e1,
                                                  Sp[:, CH - 1, 65:66] if c else -BIG, ALU.add, ALU.max)),
                   L(lambda: v.tensor_tensor_scan(m1[:, ::-1], Bn[:, c * CH + 1:(c + 1) * CH + 1][:, ::-1], mf1[:, ::-1],
                                                  -BIG, ALU.add, ALU.max)),
                   L(lambda: v.tensor_tensor(pe_[:, 0:CH], e1, m1, ALU.subtract))]
            if c:
                ops.append(L(lambda: v.scalar_tensor_tensor(out=pe_[:, CH:CH + 1], in0=Sp[:, CH - 1, 65:66],
                                                            scalar=Bn[:, c * CH:c * CH + 1], in1=m1[:, 0:1],
                                                            op0=ALU.add, op1=ALU.subtract)))
            n_ = CH + 1 if c else CH

            def ex():
                pxd[c] = A(lambda: s.activation(pe_[:, 0:n_], pe_[:, 0:n_], ACT.Exp), mine[0])
            ops.append(ex)
            ops.append(L(lambda: v.tensor_copy(Sv[:, :, 65], m1), stored.get(c - 3)))
            return ops

        def px1(c):
            Gv = G1[:, c % 4, :].rearrange("p (j d) -> p j d", j=CH)
            Sv = S1[:, c % 3, :].rearrange("p (j d) -> p j d", j=CH)
            pe_ = pf1[:, c % 2, 0:CH]
            V(lambda: v.tensor_tensor(Sv[:, :, 0:D], Gv[:, :, 0:D], bc(pe_.unsqueeze(2), [P, CH, D]), ALU.mult),
              pxd[c], stored.get(c - 3))
            freeG[c] = V(lambda: v.tensor_copy(Sv[:, :, D], pe_))

        k_step = {}

        def steps1(c):
            Sv = S1[:, c % 3, :].rearrange("p (j d) -> p j d", j=CH)
            Sp = S1[:, (c - 1) % 3, :].rearrange("p (j d) -> p j d", j=CH)
            mine = [None]

            def one(j):
                if c == 0 and j == 0:
                    return lambda: None
                pr = Sv[:, j - 1, 0:65] if j else Sp[:, CH - 1, 0:65]
                sc_ = gf[:, c * CH + j:c * CH + j + 1] if j else pf1[:, c % 2, CH:CH + 1]

                def f():
                    mine[0] = V(lambda: v.scalar_tensor_tensor(out=Sv[:, j, 0:65], in0=pr, scalar=sc_, in1=Sv[:, j, 0:65],
                                                               op0=ALU.mult, op1=ALU.add),
                                mine[0] or freeG[c], k_step.get(c - 1))
                    k_step[c] = mine[0]
                return f
            return [one(j) for j in range(CH)]

        for c in range(3):
            xb(c, XB1, freeXB, sc_done)
        g1(0)
        g1(1)
        merged(fills1(0))
        merged(soft1(0))
        px1(0)
        merged(fills1(1))
        for c in range(NCH):
            if c + 2 < NCH:
                g1(c + 2)
            if c + 3 < NCH:
                xb(c + 3, XB1, freeXB, sc_done)
            B_ = []
            if c + 1 < NCH:
                B_ += soft1(c + 1)
            if c + 2 < NCH:
                B_ += fills1(c + 2)
            merged(steps1(c), B_)
            stored[c] = ld(chunk_view(s1, c, 66), S1[:, c % 3, :], k_step[c], sem=f"s{c % 3}")
            if c + 1 < NCH:
                px1(c + 1)
        st_t = [stored[c] for c in range(NCH - 3, NCH)]
        T1 = S1[:, (NCH - 1) % 3, :].rearrange("p (j d) -> p j d", j=CH)[:, CH - 1, :]

        def mend_soft(st, Tl, heads, k_last, stored_, base):
            aw = heads * 65
            o = base

            def take(*shape):
                nonlocal o
                n = 1
                for k_ in shape:
                    n *= k_
                a_ = arena(o, *shape)
                o += n
                return a_
            fr = take(aw + heads)
            dgm, mk = take(heads, P), take(heads, P)
            Ts, mseg, mc = take(aw), take(heads), take(heads)
            Mx, w1, w2 = take(heads), take(heads), take(heads)
            gt = gather(fr, st[:], fixg[:], *stored_, k_fix, l_zr, sem="row")
            ml = Tl[:, aw:aw + heads]
            a = None
            for h in range(heads):
                a = V(lambda h=h: v.tensor_scalar(dgm[:, h, :], ident[:], ml[:, h:h + 1], None, op0=ALU.mult), k_last)
            nb = (heads + 2) // 3
            for i in range(nb):
                k_ = min(3, heads - 3 * i)
                b = T(lambda i=i, k_=k_: t.matmul(PS[i][:, 0:k_ * P], ones[:],
                                                  dgm[:, 3 * i:3 * i + k_, :].rearrange("p a b -> p (a b)"),
                                                  start=True, stop=True), a)
            for msk, res in ((En, mseg), (CTn, mc)):
                for i in range(nb):
                    k_ = min(3, heads - 3 * i)
                    V(lambda i=i, k_=k_, msk=msk: v.tensor_tensor(
                        mk[:, 3 * i:3 * i + k_, :], PS[i][:, 0:k_ * P].rearrange("p (a b) -> p a b", b=P),
                        bc(msk[:].unsqueeze(1), [P, k_, P]), ALU.add), b, ("dve", Q.value["dve"]))
                VL(lambda res=res: v.tensor_reduce(res, mk, AX, ALU.max))
            a = VL(lambda: v.tensor_tensor(mseg, ml, mseg, ALU.subtract))
            a = A(lambda: s.activation(mseg, mseg, ACT.Exp), a)
            Tv = Tl[:, 0:aw].rearrange("p (h d) -> p h d", h=heads)
            a = V(lambda: v.tensor_tensor(Ts.rearrange("p (h d) -> p h d", h=heads), Tv,
                                          bc(mseg.unsqueeze(2), [P, heads, 65]), ALU.mult), a)
            b = T(lambda: t.matmul(PS[2][:, 0:aw], Cq[:], Ts, start=True, stop=True), a)
            mr = fr[:, aw:aw + heads]
            V(lambda: v.tensor_tensor(Mx, mr, mc, ALU.max), gt, a)
            VL(lambda: v.tensor_tensor(w1, mr, Mx, ALU.subtract))
            a = V(lambda: v.tensor_tensor(w2, mc, Mx, ALU.subtract))
            A(lambda: s.activation(w1, w1, ACT.Exp), a)
            a = A(lambda: s.activation(w2, w2, ACT.Exp))
            frv = fr[:, 0:aw].rearrange("p (h d) -> p h d", h=heads)
            tv = Ts.rearrange("p (h d) -> p h d", h=heads)
            V(lambda: v.tensor_tensor(frv, frv, bc(w1.unsqueeze(2), [P, heads, 65]), ALU.mult), a)
            V(lambda: v.tensor_tensor(tv, PS[2][:, 0:aw].rearrange("p (h d) -> p h d", h=heads),
                                      bc(w2.unsqueeze(2), [P, heads, 65]), ALU.mult), b)
            VL(lambda: v.tensor_tensor(frv, frv, tv, ALU.add))
            a = VL(lambda: v.tensor_copy(mr, Mx))
            return scatter(st[:], fr, fixs[:], EP - 1, a, sem="row")

        m1_ = mend_soft(s1, T1, 1, k_step[NCH - 1], st_t, 14000)

        NG1 = arena(23400, 2, GN * 66)
        den = arena(24400, GN)
        xq = arena(24420, 2, 512)
        rl = arena(25500, 2, 3 * 512)
        eto = arena(28600, 2, 512)
        used.clear()
        evx, rlx, k_et, k_fo, k_eo = {}, {}, {}, {}, {}
        WP = arena(30000, 2, 3 * P)
        VP = arena(30800, 2, 32)
        k_wp = main.last("dve")
        for hf in range(2):
            V(lambda hf=hf: v.memset(WP[(1 - hf) * D:(2 - hf) * D, hf, :], 0.0))
            V(lambda hf=hf: v.memset(VP[(1 - hf) * D:(2 - hf) * D, hf, :], 0.0))
            k_wp = V(lambda hf=hf: v.memset(xq[D:P, hf, 3 * P:4 * P], 0.0))
            ld(WP[hf * D:hf * D + D, hf, :], WS[:], k_wp, sem="ldw")
            l_wp = ld(VP[hf * D:hf * D + D, hf, :], Vs[:], k_wp, sem="ldw")
        units = [(q, hf) for q in range(NG) for hf in range(2)]

        def own_t(q, ready):
            xv = X[:].rearrange("p l d -> p (l d)")
            for l, w, i in pairs_of(q * GN, GN):
                a = T(lambda l=l, w=w, i=i: t.transpose(PS[q % 2][0:w * D, i * P:(i + 1) * P], xv[:, l * D:(l + w) * D], ident[:]),
                      ready, evx.get(q - 2))
            for rows, lo, hi in ((P, 0, 3 * P), (D, 3 * P, 4 * P)):
                evx[q] = A(lambda rows=rows, lo=lo, hi=hi: s.copy(xq[0:rows, q % 2, lo:hi], PS[q % 2][0:rows, lo:hi]), a,
                           k_et.get(2 * q - 3), k_wp)

        def own_z(u):
            q, hf = units[u]
            w_ = (4 - hf) * P
            for ch in range(3):
                bnk = 2 + (3 * u + ch) % 4
                b = T(lambda ch=ch, bnk=bnk: t.matmul(PS[bnk][:, 0:w_], WP[:, hf, ch * P:(ch + 1) * P], xq[:, q % 2, 0:w_],
                                                      start=True, stop=True), evx[q], l_wp, rlx.get(3 * u + ch - 4))
                rlx[3 * u + ch] = A(lambda ch=ch, bnk=bnk: s.activation(rl[:, u % 2, ch * 512:ch * 512 + w_], PS[bnk][:, 0:w_],
                                                                      ACT.Relu), b, k_et.get(u - 2))

        def own_e(u):
            q, hf = units[u]
            n = 4 - hf
            w_ = n * P
            for ch in range(3):
                T(lambda ch=ch: t.matmul(PS[6][32 * ch:32 * ch + 32, 0:w_], A8[:, ch, :], rl[:, u % 2, ch * 512:ch * 512 + w_],
                                         start=True, stop=True), rlx[3 * u + 2], k_fo.get(u - 1))
            k_et[u] = T(lambda: t.matmul(PS[6][96:128, 0:w_], VP[:, hf, :], xq[:, q % 2, 0:w_], start=True, stop=True))
            k_fo[u] = A(lambda: s.copy(eto[:, u % 2, 0:w_], PS[6][:, 0:w_]), k_et[u], k_eo.get(("f", u - 2)))
            for i in range(n):
                a = T(lambda i=i: t.transpose(PS[7][:, i * P:(i + 1) * P], eto[:, u % 2, i * P:(i + 1) * P], ident[:]),
                      k_fo[u], k_eo.get(u - 1))
            k_eo[("f", u)] = a

        def own_r(u):
            q, hf = units[u]
            n = 4 - hf
            view = PS[7][:, 0:n * P].rearrange("p (i t x) -> p i x t", i=n, t=4)[:, :, 0:H, :]
            cols = slice(q * GN + hf, q * GN + hf + 2 * n - 1, 2)
            k_eo[u] = V(lambda: v.reduce_sum(es[:, cols, :], view, AX), k_eo[("f", u)])

        xb_read = [k_xb[c] for c in range(NCH - 3, NCH)]
        node_gathers(0, NG1, s1, m1_)
        k_x2 = {}
        for q in range(NG):
            nb = NG1[:, q % 2, :].rearrange("p (l d) -> p l d", l=GN)
            sl = slice(q * GN, (q + 1) * GN)
            if q + 1 < NG:
                node_gathers(q + 1, NG1, s1, m1_)
            V(lambda nb=nb: v.tensor_scalar(den, nb[:, :, D], 1e-16, None, op0=ALU.max), used[("g", q)], main.last("dve"))
            VL(lambda: v.reciprocal(den, den))
            VL(lambda nb=nb: v.tensor_tensor(nb[:, :, 0:D], nb[:, :, 0:D], bc(den.unsqueeze(2), [P, GN, D]), ALU.mult))
            VL(lambda nb=nb, sl=sl: v.tensor_tensor(nb[:, :, 0:D], nb[:, :, 0:D], X[:, sl, :], ALU.add))
            used[q] = k = norm(nb[:, :, 0:D], X[:, sl, :], sq, mu, rs, main.last("dve"))
            xw = ld(xt2.rearrange("(p l) d -> p l d", l=NL)[:, sl, :].rearrange("p l d -> p (l d)"),
                    X[:, sl, :].rearrange("p l d -> p (l d)"), k, sem="xt")
            k_row[q] = k
            if q:
                sc_done = to_edges(q - 1, X, *xb_read)
            for u in (2 * q, 2 * q + 1):
                if u >= 2:
                    own_e(u - 2)
                if u == 2 * q:
                    own_t(q, k)
                if u >= 1:
                    own_z(u - 1)
                if u >= 2:
                    own_r(u - 2)
        sc_done = to_edges(NG - 1, X, *xb_read)
        own_z(2 * NG - 1)
        for u in (2 * NG - 2, 2 * NG - 1):
            own_e(u)
            own_r(u)
        k_end = ("dve", Q.value["dve"])
        fence(k_end, ("act", Q.value["act"]), ("pe", Q.value["pe"]))
        exchange(Em("f2"), flag[0:1, 1:2], X, *now(), xw, sc_done)

        NX = 5
        XBN = 3
        XS = arena(0, NX, CH * P)
        XB2 = arena(10240, XBN, CH * D)
        S2 = arena(13312, 2, CH * RW)
        XT2 = arena(25984, 6, 512)
        RL2 = arena(29056, 5, 3 * 512)
        eb = arena(36736, H, CH)
        mf2 = arena(36832, H, CH)
        mb2 = arena(36928, H, CH)
        Bb = arena(37024, H * CH + 1)
        Bf = Bb[:, 0:H * CH].rearrange("p (h j) -> p h j", h=H)
        pf2 = arena(37216, 2, H * (CH + 1))
        tmp2 = arena(37420, H, 65)
        ETs = arena(37810, 512)
        stored, k_step, k_xb, freeXB, k_fill, k_g, pxd = {}, {}, {}, {}, {}, {}, {}
        freeXS, k_E, k_px, k_pa, k_step0 = {}, {}, {}, {}, {}
        V(lambda: v.memset(Bb, -BIG))

        HV = 4
        freeXA = {}

        def xsv(c):
            return XS[:, c % NX, :].rearrange("p (j d) -> p j d", j=CH)

        gi = gather(xsv(0)[:, 0, D:P], xt2, Dd[:, 0:1], xw, sem="xdi")

        def g2(c):
            for j in range(CH):
                k_g[c] = gather(xsv(c)[:, j, 0:D], xt2, Si[:, c * CH + j:c * CH + j + 1], xw,
                                freeXS.get(c - NX), freeXA.get(c - NX), sem=f"g{c % NX}")

        def fills2(c):
            XBv = XB2[:, c % XBN, :].rearrange("p (j d) -> p j d", j=CH)
            cur, prv = xsv(c), xsv(c - 1)
            mine = [None]

            def one(j):
                if c == 0 and j == 0:
                    return lambda: None
                pr = cur[:, j - 1, D:P] if j else prv[:, CH - 1, D:P]

                def f():
                    mine[0] = V(lambda: v.scalar_tensor_tensor(
                        out=cur[:, j, D:P], in0=pr, scalar=gf[:, c * CH + j:c * CH + j + 1], in1=XBv[:, j, :],
                        op0=ALU.mult, op1=ALU.add), k_xb[c], mine[0] or k_fill.get(c - 1), gi, freeXS.get(c - NX), freeXA.get(c - NX))
                    k_fill[c] = freeXB[c] = mine[0]
                return f
            return [one(j) for j in range(CH)]

        evT, relu, etok, et_ev, e_read, k_eb, k_mx = {}, {}, {}, {}, {}, {}, {}
        logits = PS[7][:].rearrange("p (i q x) -> p x q i", i=4, q=4)[:, 0:H]
        NGR = CH // 4

        def pe_t(u):
            c, q = divmod(u, NGR)
            for i in range(4):
                a = T(lambda i=i: t.transpose(PS[u % 2][:, i * P:(i + 1) * P], xsv(c)[:, 4 * q + i, :], ident[:]),
                      k_g[c], k_fill[c], evT.get(u - 2))
            evT[u] = A(lambda: s.copy(XT2[:, u % 6, :], PS[u % 2][:]), a, etok.get((u - 6) // NGR))

        def pe_m(u, ch):
            bnk = 2 + (3 * u + ch) % 4
            a = T(lambda: t.matmul(PS[bnk][:], WLR[:, ch * P:(ch + 1) * P], XT2[:, u % 6, :], start=True, stop=True),
                  evT[u], relu.get(3 * u + ch - 4))
            relu[3 * u + ch] = A(lambda: s.activation(RL2[:, u % 5, ch * 512:(ch + 1) * 512], PS[bnk][:], ACT.Relu),
                                 a, etok.get((u - 5) // NGR))

        def pe_e(c, ch):
            for q in range(NGR):
                u = c * NGR + q
                if ch < 3:
                    w_, m_ = A8[:, ch, :], RL2[:, u % 5, ch * 512:(ch + 1) * 512]
                else:
                    w_, m_ = Vm[:], XT2[:, u % 6, :]
                a = T(lambda ch=ch, q=q, w_=w_, m_=m_: t.matmul(PS[6][32 * q:32 * q + 32, :], w_, m_, start=(ch == 0),
                                                                stop=(ch == 3)), relu[3 * u + 2], et_ev.get(c - 1))
            if ch == 3:
                etok[c] = a
                et_ev[c] = A(lambda: s.copy(ETs, PS[6][:]), a, k_E.get(c - 1))

        def pe_f(c):
            for i in range(4):
                a = T(lambda i=i: t.transpose(PS[7][:, i * P:(i + 1) * P], ETs[:, i * P:(i + 1) * P], ident[:]),
                      et_ev[c], e_read.get(c - 1))
            k_E[c] = a
            k_eb[c] = A(lambda: s.copy(eb.rearrange("p h (q i) -> p h q i", q=4), logits), a)

        def pe_ops(c):
            ops = []
            for q in range(NGR):
                u = c * NGR + q
                ops.append(lambda u=u: pe_t(u))
                if u == 0:
                    continue
                if c and q == 2:
                    ops.append(lambda: pe_f(c - 1))
                for ch in range(3):
                    ops.append(lambda u=u, ch=ch: pe_m(u - 1, ch))
                    if c and q == 1:
                        ops.append(lambda ch=ch: pe_e(c - 1, ch))
                if c and q == 1:
                    ops.append(lambda: pe_e(c - 1, 3))
            return ops

        def pe_last():
            for ch in range(3):
                pe_m(NCH * NGR - 1, ch)
            for ch in range(4):
                pe_e(NCH - 1, ch)
            pe_f(NCH - 1)

        def soft2(c):
            Sv = S2[:, c % 2, :].rearrange("p (j d) -> p j d", j=CH)
            Sp = S2[:, (c - 1) % 2, :].rearrange("p (j d) -> p j d", j=CH)
            pe_ = pf2[:, c % 2, 0:H * CH].rearrange("p (h j) -> p h j", h=H)
            pq = pf2[:, c % 2, H * CH:H * CH + H]
            mine = [None]
            fl = lambda a_: a_.rearrange("p h j -> p (h j)")

            def L(fn, *w):
                def f():
                    mine[0] = V(fn, mine[0], *w)
                return f

            ops = [L(lambda: v.tensor_copy(Bf[:, :, 1:CH], bc(Bn[:, c * CH + 1:(c + 1) * CH].unsqueeze(1), [P, H, CH - 1])),
                     k_eb[c], k_mx.get(c - 1))]
            if c:
                ops.append(L(lambda: v.scalar_tensor_tensor(out=eb[:, :, 0], in0=Sp[:, CH - 1, HW:], scalar=Bn[:, c * CH:c * CH + 1],
                                                            in1=eb[:, :, 0], op0=ALU.add, op1=ALU.max)))
            ops += [L(lambda: v.tensor_tensor_scan(fl(mf2), fl(Bf), fl(eb), -BIG, ALU.add, ALU.max)),
                    L(lambda: v.tensor_tensor_scan(fl(mb2)[:, ::-1], Bb[:, 1:][:, ::-1], fl(mf2)[:, ::-1], -BIG, ALU.add, ALU.max)),
                    L(lambda: v.tensor_tensor(pe_.rearrange("p h (q i) -> p h q i", q=4), logits,
                                              mb2.rearrange("p h (q i) -> p h q i", q=4), ALU.subtract))]

            def note():
                e_read[c] = mine[0]
            ops.append(note)
            if c:
                ops.append(L(lambda: v.scalar_tensor_tensor(out=pq, in0=Sp[:, CH - 1, HW:], scalar=Bn[:, c * CH:c * CH + 1],
                                                            in1=mb2[:, :, 0], op0=ALU.add, op1=ALU.subtract)))
            n_ = H * (CH + 1) if c else H * CH

            def ex():
                pxd[c] = A(lambda: s.activation(pf2[:, c % 2, 0:n_], pf2[:, c % 2, 0:n_], ACT.Exp), mine[0])
                k_mx[c] = A(lambda: s.copy(Sv[:, :, HW:].rearrange("p j h -> p h j"), mb2), stored.get(c - 2), k_step0.get(c - 1))
            ops.append(ex)
            return ops

        def px2(c):
            Sv = S2[:, c % 2, :].rearrange("p (j d) -> p j d", j=CH)
            pe_ = pf2[:, c % 2, 0:H * CH].rearrange("p (h j) -> p h j", h=H)
            if c:
                Sp = S2[:, (c - 1) % 2, :].rearrange("p (j d) -> p j d", j=CH)
                pq = pf2[:, c % 2, H * CH:H * CH + H]
                k_step0[c] = V(lambda: v.tensor_tensor(tmp2, Sp[:, CH - 1, 0:HW].rearrange("p (h d) -> p h d", h=H),
                                                       bc(pq.unsqueeze(2), [P, H, 65]), ALU.mult), pxd[c], k_step[c - 1])
            for h in range(HV):
                V(lambda h=h: v.tensor_tensor(Sv[:, :, h * 65:h * 65 + D], xsv(c)[:, :, 0:D],
                                              bc(pe_[:, h, :].unsqueeze(2), [P, CH, D]), ALU.mult), pxd[c], stored.get(c - 2),
                  k_step.get(c - 1))
                k_px[c] = freeXS[c] = main.last("dve")

        def px2_act(c):
            Sv = S2[:, c % 2, :].rearrange("p (j d) -> p j d", j=CH)
            pe_ = pf2[:, c % 2, 0:H * CH].rearrange("p (h j) -> p h j", h=H)

            def one(j, h):
                def f():
                    k_pa[(c, j)] = freeXA[c] = A(
                        lambda: s.activation(Sv[:, j, h * 65:h * 65 + D], xsv(c)[:, j, 0:D], ACT.Copy,
                                             scale=pe_[:, h, j:j + 1]), pxd[c], stored.get(c - 2), k_step0.get(c - 1))
                return f

            def sums():
                A(lambda: s.copy(Sv[:, :, 0:HW].rearrange("p j (h d) -> p j h d", h=H)[:, :, :, D].rearrange("p j h -> p h j"), pe_),
                  pxd[c], stored.get(c - 2), k_step0.get(c - 1))
            return [sums] + [one(j, h) for j in range(CH) for h in range(HV, H)]

        def steps2(c):
            Sv = S2[:, c % 2, :].rearrange("p (j d) -> p j d", j=CH)
            mine = [None]

            def one(j):
                if c == 0 and j == 0:
                    return lambda: None
                if j == 0:
                    def f():
                        mine[0] = V(lambda: v.tensor_tensor(Sv[:, 0, 0:HW], Sv[:, 0, 0:HW], tmp2.rearrange("p h d -> p (h d)"),
                                                            ALU.add), k_step0[c], k_px[c], k_pa[(c, 0)])
                    return f

                def f():
                    mine[0] = V(lambda: v.scalar_tensor_tensor(
                        out=Sv[:, j, 0:HW], in0=Sv[:, j - 1, 0:HW], scalar=gf[:, c * CH + j:c * CH + j + 1],
                        in1=Sv[:, j, 0:HW], op0=ALU.mult, op1=ALU.add), mine[0] or k_px[c], k_pa[(c, j)], k_pa[(c, 0)])
                    k_step[c] = mine[0]
                return f
            return [one(j) for j in range(CH)]

        def spread(ops):
            return [lambda: None] * (CH - 1 - len(ops)) + ops

        for c in range(XBN):
            xb(c, XB2, freeXB, sc_done)
        for c in range(4):
            g2(c)
            merged(fills2(c))
            if c < 2:
                xb(c + 3, XB2, freeXB, sc_done)
        merged(pe_ops(0))
        merged(pe_ops(1))
        merged(soft2(0))
        px2(0)
        merged(pe_ops(2), px2_act(0))
        for c in range(NCH):
            if c + 4 < NCH:
                g2(c + 4)
            merged(fills2(c + 4) if c + 4 < NCH else [], steps2(c), spread(soft2(c + 1)) if c + 1 < NCH else [])
            if c + 5 < NCH:
                xb(c + 5, XB2, freeXB, sc_done)
            stored[c] = ld(chunk_view(s2, c, RW), S2[:, c % 2, :], k_step[c], k_mx[c], sem=f"s{c % 2}")
            if c + 1 < NCH:
                px2(c + 1)
                merged(pe_ops(c + 3) if c + 3 < NCH else [], px2_act(c + 1))
            if c == NCH - 3:
                pe_last()
        st_t = [stored[c] for c in range(NCH - 2, NCH)]
        T2 = S2[:, (NCH - 1) % 2, :].rearrange("p (j d) -> p j d", j=CH)[:, CH - 1, :]
        m2_ = mend_soft(s2, T2, H, k_step[NCH - 1], st_t, 0)
        fence(("pe", Q.value["pe"]), ("act", Q.value["act"]))
        k_m2 = ("dve", Q.value["dve"])

        N2 = arena(13312, 2, GN * RW)
        U = arena(20200, 2, GN * H * D)
        UT = arena(25600, 3 * GN * P)
        TU = arena(28400, GN, H * D)
        wv = arena(31100, 6, GN * H)
        O2 = arena(31400, 2, GN * D)
        O3 = arena(32300, GN, D)
        LAM, ALP = 1.0507009873554805, 1.6732632423543772
        used.clear()
        uf, k_u, k_o, k_n = {}, {}, {}, {}
        ysb3 = arena(9024, 4, 2 * R3 * D)

        def weighted(q):
            nb = N2[:, q % 2, :].rearrange("p (l d) -> p l d", l=GN)
            sl = slice(q * GN, (q + 1) * GN)
            mm, w1, w3_, dd = (wv[:, i, :].rearrange("p (l h) -> p l h", h=H) for i in range(4))
            nv = nb[:, :, 0:HW].rearrange("p l (h d) -> p l h d", h=H)
            Uv = U[:, q % 2, :].rearrange("p (l h d) -> p l h d", l=GN, h=H)
            Tv = TU.rearrange("p l (h d) -> p l h d", h=H)
            sh = [P, GN, H, D]
            V(lambda: v.tensor_tensor(mm, nb[:, :, HW:], es[:, sl, :], ALU.max), used[("g", q)], main.last("dve"))
            VL(lambda: v.tensor_tensor(w1, nb[:, :, HW:], mm, ALU.subtract))
            a = V(lambda: v.tensor_tensor(w3_, es[:, sl, :], mm, ALU.subtract))
            A(lambda: s.activation(w1, w1, ACT.Exp), a)
            a = A(lambda: s.activation(w3_, w3_, ACT.Exp))
            V(lambda: v.tensor_tensor(dd, nv[:, :, :, D], w1, ALU.mult), a)
            VL(lambda: v.tensor_tensor(dd, dd, w3_, ALU.add))
            VL(lambda: v.tensor_scalar(dd, dd, 1e-16, float(H), op0=ALU.add, op1=ALU.mult))
            VL(lambda: v.reciprocal(dd, dd))
            VL(lambda: v.tensor_tensor(w1, w1, dd, ALU.mult))
            V(lambda: v.tensor_tensor(w3_, w3_, dd, ALU.mult))
            used[q] = VL(lambda: v.tensor_tensor(Uv, nv[:, :, :, 0:D], bc(w1.unsqueeze(3), sh), ALU.mult), uf.get(("U", q - 2)))
            V(lambda: v.tensor_tensor(Tv, bc(X[:, sl, :].unsqueeze(2), sh), bc(w3_.unsqueeze(3), sh), ALU.mult))
            k_u[q] = VL(lambda: v.tensor_tensor(U[:, q % 2, :], U[:, q % 2, :], TU.rearrange("p l d -> p (l d)"), ALU.add))

        def projected(q):
            blocks = 3 * GN
            ev = {}
            for n_, b0 in enumerate(range(0, blocks, 4)):
                bn = min(4, blocks - b0)
                for i in range(bn):
                    a = T(lambda i=i, b0=b0, n_=n_: t.transpose(PS[n_ % 2][:, i * P:(i + 1) * P],
                                                                U[:, q % 2, (b0 + i) * P:(b0 + i + 1) * P], ident[:]),
                          k_u[q], uf.get(("b", n_ % 2)))
                e_ = A(lambda b0=b0, bn=bn, n_=n_: s.copy(UT[:, b0 * P:(b0 + bn) * P], PS[n_ % 2][:, 0:bn * P]), a,
                       uf.get(("UT", q - 1)))
                uf[("b", n_ % 2)] = e_
                for i in range(bn):
                    ev[b0 + i] = e_
            uf[("U", q)] = a
            for l in range(GN):
                for ch in range(3):
                    k_ = 3 * l + ch
                    b = T(lambda l=l, ch=ch, k_=k_: t.matmul(PS[2][:, l * D:(l + 1) * D], UT[:, k_ * P:(k_ + 1) * P],
                                                             W2[:, ch, :], start=(ch == 0), stop=(ch == 2)),
                          ev[k_], uf.get("o"))
            uf[("UT", q)] = k_o[q] = b

        def finished(q):
            sl = slice(q * GN, (q + 1) * GN)
            o2 = O2[:, q % 2, :].rearrange("p (l d) -> p l d", l=GN)
            ps2 = PS[2][:, 0:GN * D].rearrange("p (l d) -> p l d", d=D)
            tok = {}

            def bias_exp():
                uf["o"] = V(lambda: v.tensor_tensor(o2, ps2, bc(b2[:].unsqueeze(1), [P, GN, D]), ALU.add), k_o[q])
                a = VL(lambda: v.tensor_scalar(O3, o2, 0.0, None, op0=ALU.min))
                tok["e"] = A(lambda: s.activation(O3, O3, ACT.Exp), a)
                V(lambda: v.tensor_scalar(o2, o2, 0.0, LAM, op0=ALU.max, op1=ALU.mult))
                VL(lambda: v.tensor_tensor(o2, o2, X[:, sl, :], ALU.add))

            def selu_norm():
                V(lambda: v.tensor_scalar(O3, O3, -1.0, LAM * ALP, op0=ALU.add, op1=ALU.mult), tok["e"])
                VL(lambda: v.tensor_tensor(o2, o2, O3, ALU.add))
                k_n[q] = norm(o2, X[:, sl, :], sq, mu, rs, main.last("dve"))
            return bias_exp, selu_norm

        turned = {}
        W3z = arena(33000, 2, (R3 + 1) * D)
        for hf in range(2):
            V(lambda hf=hf: v.memset(W3z[(1 - hf) * D:(2 - hf) * D, hf, :], 0.0), k_m2)
            k_w3 = V(lambda hf=hf: v.tensor_copy(W3z[hf * D:hf * D + D, hf, :], W3[hf * D:hf * D + D, :]))

        def tabled_1(q):
            turned[q] = turn(q * GN, GN, (3,), (k_n[q],), "a")

        def tabled_2(q, between):
            def loops(l, w, xt_, ev):
                i = (l - q * GN) // 2
                for hf in range(w):
                    bnk = (4, 7)[hf]
                    uf[("lp", q)] = T(lambda hf=hf, bnk=bnk: t.matmul(
                        PS[bnk][:, i * D:(i + 1) * D], xt_[0:w * D], W3z[0:w * D, hf, R3 * D:], start=True, stop=True),
                        ev, uf.get("l"), k_w3)
            products(*turned[q], q * GN, GN, W3z.rearrange("p a o -> p (a o)"), R3, y3, ysb3, (5, 6), "a", extra=loops,
                     over_zeros=(R3 + 1) * D, between=between)

        def tabled_3(q):
            sl = slice(q * GN, (q + 1) * GN)
            for hf, n in ((0, 4), (1, 3)):
                ps = PS[(4, 7)[hf]][:, 0:n * D].rearrange("p (l d) -> p l d", d=D)
                cols = slice(q * GN + hf, q * GN + hf + 2 * n - 1, 2)
                uf["l"] = V(lambda ps=ps, cols=cols: v.tensor_tensor(R[:, cols, :], X[:, cols, :], ps, ALU.add), uf[("lp", q)])
            return VL(lambda: v.tensor_tensor(R[:, sl, :], R[:, sl, :], bc(b3[:].unsqueeze(1), [P, GN, D]), ALU.add))

        node_gathers(0, N2, s2, m2_, k_m2)
        node_gathers(1, N2, s2, m2_, k_m2)
        weighted(0)
        projected(0)
        weighted(1)
        for q in range(NG + 1):
            now_ = []
            if q + 2 < NG:
                node_gathers(q + 2, N2, s2, m2_, k_m2)
            if q < NG:
                first_, second_ = finished(q)
                first_()
                now_.append(second_)
            if q + 2 < NG:
                now_.append(lambda q=q: weighted(q + 2))
            if q:
                tabled_2(q - 1, now_)
            else:
                for f in now_:
                    f()
            if q + 1 < NG:
                projected(q + 1)
            if q < NG:
                tabled_1(q)
            if q:
                k_end = tabled_3(q - 1)
        t_y3 = [("ysb%d" % i, Q.value["ysb%d" % i]) for i in range(4)]

        T3, k_t, st_t = linear_chunks(y3, I3, s3, [*t_y3, k_end])
        m3 = mend_linear(s3, T3, k_t, st_t)
        used.clear()
        ov = out.rearrange("(p l) d -> p l d", l=NL)
        NG3 = arena(23400, 2, GN * D)
        for q in range(NG):
            nb = NG3[:, q % 2, :].rearrange("p (l d) -> p l d", l=GN)
            sl = slice(q * GN, (q + 1) * GN)
            node_gathers(q, NG3, s3, m3)
            VL(lambda nb=nb, sl=sl: v.tensor_tensor(nb, nb, R[:, sl, :], ALU.add), used[("g", q)])
            used[q] = k = norm(nb, X[:, sl, :], sq, mu, rs, ("dve", Q.value["dve"]))
            fin = ld(ov[:, sl, :].rearrange("p l d -> p (l d)"), X[:, sl, :].rearrange("p l d -> p (l d)"), k, sem="out")
        Q.wait("sync", fin, ("z", Q.value["z"]), ("zr", Q.value["zr"]))
        for n_ in names:
            if n_ in Q.value and n_ not in ("dve", "act", "pe", "pool") and n_[0:2] not in ("f0", "f1", "f2"):
                Q.wait("sync", (n_, Q.value[n_]))

        block = ctx.enter_context(nc.Block())

        @block.sync
        def _(e):
            Q.play("sync", e)

        @block.gpsimd
        def _(e):
            Q.play("gpsimd", e)

        @block.scalar
        def _(e):
            Q.play("scalar", e)

        @block.vector
        def _(e):
            Q.play("vector", e)

        @block.tensor
        def _(e):
            Q.play("tensor", e)


_INS = ["x", "src", "dst", "edge_type_16", "edge_type_8", "L0_gnn_weight", "L1_gnn_beta", "L2_gnn_W_l", "L2_gnn_W_r",
        "L2_gnn_att", "L2_gnn_bias", "L3_gnn_W", "L3_gnn_coeff", "L3_gnn_h_bias", "L3_gnn_loop_weight"]


def kernel(**inputs):
    import numpy as np
    import concourse.bacc as bacc
    from concourse.bass_utils import run_bass_kernel_spmd

    nc = bacc.Bacc("TRN2", target_bir_lowering=False, num_devices=1)
    arrays, args = {}, []
    for name in _INS:
        a = np.ascontiguousarray(inputs[name])
        if name == "x":
            a = np.concatenate([a, np.zeros((NN - N, D), a.dtype)])
        elif name == "dst":
            a = np.concatenate([a, np.full((EP + NC - E,), N, a.dtype)])
        elif name == "src":
            a = np.concatenate([a, np.full((EP - E,), N, a.dtype)])
        elif name in ("edge_type_16", "edge_type_8"):
            a = np.concatenate([a, np.zeros((EP - E,), a.dtype)])
        arrays["in_" + name] = a
        args.append(nc.dram_tensor("in_" + name, a.shape, mybir.dt.from_np(a.dtype), kind="ExternalInput").ap())
    args.append(nc.dram_tensor("out_0", (NN, D), mybir.dt.float32, kind="ExternalOutput").ap())
    build(nc, *args)
    r = run_bass_kernel_spmd(nc, [arrays], core_ids=[0])
    return np.asarray(r.results[0]["out_0"])[:N]
```
